# Optimizing a Trainium2 kernel written in Bass

```python
import numpy as np
import jax
import jax.numpy as jnp

def _softmax(x, axis=-1):
    return jax.nn.softmax(x, axis=axis)

def _gelu(x):
    return jax.nn.gelu(x, approximate=True)

def _silu(x):
    return jax.nn.silu(x)

def _sigmoid(x):
    return jax.nn.sigmoid(x)

def _layernorm(x, axis=-1, eps=1e-05):
    m = jnp.mean(x, axis=axis, keepdims=True)
    v = jnp.var(x, axis=axis, keepdims=True)
    return (x - m) / jnp.sqrt(v + eps)

def _scatter_add(tgt, idx, src, axis=0):
    return tgt.at[idx].add(src)

def _segment_sum(src, seg, n):
    return jax.ops.segment_sum(src, seg, n)
kernel_name = 'mk_sandwich_d2_jaxref_r8_067250'

def setup_inputs(seed: int=0):
    np.random.seed(seed)
    _w = jnp.asarray

    def _L0_attn_setup():
        import jax, jax.numpy as jnp
        import numpy as np
        from jax import lax
        B, T, D, H = (4, 512, 128, 16)
        d = D // H
        key = jax.random.key(seed)
        k0, k1, k2, k3, k4 = jax.random.split(key, 5)
        s = 1.0 / np.sqrt(D)
        x = jax.random.normal(k0, (B, T, D), dtype=jnp.float32)
        Wv = jax.random.normal(k1, (D, D), dtype=jnp.float32) * s
        Wo = jax.random.normal(k2, (D, D), dtype=jnp.float32) * s
        Wg = jax.random.normal(k3, (H, D), dtype=jnp.float32) * s
        Wb = jax.random.normal(k4, (H, D), dtype=jnp.float32) * s
        return {'x': x, 'Wv': Wv, 'Wo': Wo, 'Wg': Wg, 'Wb': Wb}
    _L0_attn_in = _L0_attn_setup()

    def _L0_ffn_setup():
        import jax, jax.numpy as jnp
        import numpy as np
        DIM = 128
        DEPTH = 6
        HEADS = 16
        DIM_HEAD = 64
        WINDOW = 32
        INNER = HEADS * DIM_HEAD
        DIM_INNER = int(DIM * 4 * 2 / 3)
        QK_SCALE = 8.0

        def shift_tokens(t):
            a, s = jnp.split(t, 2, -1)
            s = jnp.pad(s, ((0, 0), (1, 0), (0, 0)))[:, :-1]
            return jnp.concatenate([a, s], -1)

        def l2norm(t):
            return t / jnp.maximum(jnp.linalg.norm(t, axis=-1, keepdims=True), 1e-12)

        def rotate_half(x):
            x1, x2 = jnp.split(x, 2, -1)
            return jnp.concatenate([-x2, x1], -1)

        def rotary_tables(n):
            half = jnp.arange(0, DIM_HEAD, 2, dtype=jnp.float32)
            inv_freq = 1.0 / 10000.0 ** (half / DIM_HEAD)
            t = jnp.arange(n, dtype=jnp.float32)
            freqs = t[:, None] * inv_freq[None, :]
            freqs = jnp.concatenate([freqs, freqs], -1)
            base_scale = (half + 0.4 * DIM_HEAD) / (1.4 * DIM_HEAD)
            power = (t - n // 2) / (WINDOW // 2)
            scale = base_scale[None, :] ** power[:, None]
            scale = jnp.concatenate([scale, scale], -1)
            return (freqs, scale)

        def local_attention(q, k, v):
            b, h, n, d = q.shape
            w = WINDOW
            nw = n // w
            bq = q.reshape(b, h, nw, w, d)
            bk = k.reshape(b, h, nw, w, d)
            bv = v.reshape(b, h, nw, w, d)

            def look(t):
                p = jnp.pad(t, ((0, 0), (0, 0), (1, 0), (0, 0), (0, 0)))
                return jnp.concatenate([p[:, :, :nw], p[:, :, 1:]], axis=3)
            bk2, bv2 = (look(bk), look(bv))
            seq = jnp.arange(n).reshape(nw, w)
            seq_p = jnp.pad(seq, ((1, 0), (0, 0)), constant_values=-1)
            jt = jnp.concatenate([seq_p[:nw], seq_p[1:]], axis=1)
            it = seq[:, :, None]
            jb = jt[:, None, :]
            mask = (it < jb) | (it > jb + w) | (jb == -1)
            sim = jnp.einsum('bhwie,bhwje->bhwij', bq, bk2) * QK_SCALE
            sim = jnp.where(mask, -jnp.finfo(sim.dtype).max, sim)
            attn = jax.nn.softmax(sim, -1)
            out = jnp.einsum('bhwij,bhwje->bhwie', attn, bv2)
            return out.reshape(b, h, n, d)

        def attn_layer(x, Wqkv, qs, ksc, Wo):
            b, n, _ = x.shape
            qkv = x @ Wqkv
            q, k, v = jnp.split(qkv, 3, -1)
            sh = lambda t: t.reshape(b, n, HEADS, DIM_HEAD).transpose(0, 2, 1, 3)
            q, k, v = (sh(q), sh(k), sh(v))
            q = l2norm(q) * qs
            k = l2norm(k) * ksc
            freqs, scale = rotary_tables(n)
            cos, sin = (jnp.cos(freqs), jnp.sin(freqs))
            q = q * cos * scale + rotate_half(q) * sin * scale
            inv = 1.0 / scale
            k = k * cos * inv + rotate_half(k) * sin * inv
            out = local_attention(q, k, v)
            out = out.transpose(0, 2, 1, 3).reshape(b, n, INNER)
            return out @ Wo

        def ffn_layer(x, g, bln, W1, b1, W2, b2):
            mu = x.mean(-1, keepdims=True)
            var = ((x - mu) ** 2).mean(-1, keepdims=True)
            xn = (x - mu) / jnp.sqrt(var + 1e-05) * g + bln
            hg = xn @ W1 + b1
            a, gate = jnp.split(hg, 2, -1)
            return a * jax.nn.gelu(gate, approximate=False) @ W2 + b2
        key = jax.random.key(seed)
        ks = jax.random.split(key, 8)
        B, N = (2, 256)
        init = lambda k, shape: jax.random.normal(k, shape, jnp.float32) * 0.02
        return {'x': jax.random.normal(ks[0], (B, N, DIM), jnp.float32), 'Wqkv': init(ks[1], (DEPTH, DIM, 3 * INNER)), 'q_scale': jnp.ones((DEPTH, DIM_HEAD), jnp.float32), 'k_scale': jnp.ones((DEPTH, DIM_HEAD), jnp.float32), 'Wo': init(ks[2], (DEPTH, INNER, DIM)), 'ln_g': jnp.ones((DEPTH, DIM), jnp.float32), 'ln_b': jnp.zeros((DEPTH, DIM), jnp.float32), 'W1': init(ks[3], (DEPTH, DIM, 2 * DIM_INNER)), 'b1': jnp.zeros((DEPTH, 2 * DIM_INNER), jnp.float32), 'W2': init(ks[4], (DEPTH, DIM_INNER, DIM)), 'b2': jnp.zeros((DEPTH, DIM), jnp.float32)}
    _L0_ffn_in = _L0_ffn_setup()

    def _L1_attn_setup():
        import jax, jax.numpy as jnp
        import numpy as np
        D_MODEL = 128
        key = jax.random.key(seed)
        kx, kq, kk, kv = jax.random.split(key, 4)
        B, T, D = (4, 256, D_MODEL)
        bound = np.sqrt(6.0 / D) / np.sqrt(3.0)
        x = jax.random.normal(kx, (B, T, D), dtype=jnp.float32)
        w_q = jax.random.uniform(kq, (D, D), jnp.float32, -bound, bound)
        w_k = jax.random.uniform(kk, (D, D), jnp.float32, -bound, bound)
        w_v = jax.random.uniform(kv, (D, D), jnp.float32, -bound, bound)
        return {'x': x, 'w_q': w_q, 'w_k': w_k, 'w_v': w_v}
    _L1_attn_in = _L1_attn_setup()

    def _L1_ffn_setup():
        import jax, jax.numpy as jnp
        import numpy as np
        N_EXPERTS = 16
        TOP_K = int(N_EXPERTS * 0.2)
        EPS = 1e-12
        key = jax.random.key(seed)
        ks = jax.random.split(key, 6)
        B, T, D, H, E = (4, 128, 128, 256, N_EXPERTS)
        x = jax.random.normal(ks[0], (B, T, D), dtype=jnp.float32)
        gate = jax.random.normal(ks[1], (D, E), dtype=jnp.float32)
        W1 = jax.random.normal(ks[2], (E, D, H), dtype=jnp.float32) * (1.0 / np.sqrt(D))
        b1 = jax.random.normal(ks[3], (E, H), dtype=jnp.float32) * 0.02
        W2 = jax.random.normal(ks[4], (E, H, D), dtype=jnp.float32) * (1.0 / np.sqrt(H))
        b2 = jax.random.normal(ks[5], (E, D), dtype=jnp.float32) * 0.02
        return {'x': x, 'gate': gate, 'W1': W1, 'b1': b1, 'W2': W2, 'b2': b2}
    _L1_ffn_in = _L1_ffn_setup()
    _d = {'L0_attn_x': _L0_attn_in['x'], 'L0_attn_Wv': _L0_attn_in['Wv'], 'L0_attn_Wo': _L0_attn_in['Wo'], 'L0_attn_Wg': _L0_attn_in['Wg'], 'L0_attn_Wb': _L0_attn_in['Wb'], 'L0_ffn_Wqkv': _L0_ffn_in['Wqkv'], 'L0_ffn_q_scale': _L0_ffn_in['q_scale'], 'L0_ffn_k_scale': _L0_ffn_in['k_scale'], 'L0_ffn_Wo': _L0_ffn_in['Wo'], 'L0_ffn_ln_g': _L0_ffn_in['ln_g'], 'L0_ffn_ln_b': _L0_ffn_in['ln_b'], 'L0_ffn_W1': _L0_ffn_in['W1'], 'L0_ffn_b1': _L0_ffn_in['b1'], 'L0_ffn_W2': _L0_ffn_in['W2'], 'L0_ffn_b2': _L0_ffn_in['b2'], 'L1_attn_w_q': _L1_attn_in['w_q'], 'L1_attn_w_k': _L1_attn_in['w_k'], 'L1_attn_w_v': _L1_attn_in['w_v'], 'L1_ffn_gate': _L1_ffn_in['gate'], 'L1_ffn_W1': _L1_ffn_in['W1'], 'L1_ffn_b1': _L1_ffn_in['b1'], 'L1_ffn_W2': _L1_ffn_in['W2'], 'L1_ffn_b2': _L1_ffn_in['b2']}
    _x0 = _d['L0_attn_x']
    _d['L0_attn_x'] = jax.random.normal(jax.random.fold_in(jax.random.key(seed), 1), (4, 1024, 128), dtype=_x0.dtype)
    del _x0
    return _d

def reference(L0_attn_x, L0_attn_Wv, L0_attn_Wo, L0_attn_Wg, L0_attn_Wb, L0_ffn_Wqkv, L0_ffn_q_scale, L0_ffn_k_scale, L0_ffn_Wo, L0_ffn_ln_g, L0_ffn_ln_b, L0_ffn_W1, L0_ffn_b1, L0_ffn_W2, L0_ffn_b2, L1_attn_w_q, L1_attn_w_k, L1_attn_w_v, L1_ffn_gate, L1_ffn_W1, L1_ffn_b1, L1_ffn_W2, L1_ffn_b2):

    def _L0_attn_ref(x, Wv, Wo, Wg, Wb):
        import jax, jax.numpy as jnp
        import numpy as np
        from jax import lax
        B, T, D, H = (4, 512, 128, 16)
        d = D // H
        Bb, Tt, Dd = x.shape
        dd = Dd // H
        rk = x.reshape(Bb, Tt, H, dd)
        rk = rk / jnp.maximum(jnp.linalg.norm(rk, axis=-1, keepdims=True), 1e-12)
        wk = jnp.pad(rk[:, :-1], ((0, 0), (1, 0), (0, 0), (0, 0)))
        v = (x @ Wv.T).reshape(Bb, Tt, H, dd)
        gate = jax.nn.sigmoid(x @ Wg.T)
        beta = jax.nn.sigmoid(x @ Wb.T)

        def step(S, inp):
            rk_t, wk_t, v_t, g_t, b_t = inp
            pred = jnp.einsum('bhk,bhkd->bhd', wk_t, S)
            err = (v_t - pred) * b_t[..., None]
            S = S + wk_t[..., None] * err[..., None, :]
            o = jnp.einsum('bhk,bhkd->bhd', rk_t, S) * g_t[..., None]
            return (S, o)
        to_time = lambda a: jnp.moveaxis(a, 1, 0)
        xs = (to_time(rk), to_time(wk), to_time(v), to_time(gate), to_time(beta))
        S0 = jnp.zeros((Bb, H, dd, dd), x.dtype)
        _, out = lax.scan(step, S0, xs)
        out = jnp.moveaxis(out, 0, 1).reshape(Bb, Tt, Dd)
        return out @ Wo.T

    def _L0_ffn_ref(x, Wqkv, q_scale, k_scale, Wo, ln_g, ln_b, W1, b1, W2, b2):
        import jax, jax.numpy as jnp
        import numpy as np
        DIM = 128
        DEPTH = 6
        HEADS = 16
        DIM_HEAD = 64
        WINDOW = 32
        INNER = HEADS * DIM_HEAD
        DIM_INNER = int(DIM * 4 * 2 / 3)
        QK_SCALE = 8.0

        def shift_tokens(t):
            a, s = jnp.split(t, 2, -1)
            s = jnp.pad(s, ((0, 0), (1, 0), (0, 0)))[:, :-1]
            return jnp.concatenate([a, s], -1)

        def l2norm(t):
            return t / jnp.maximum(jnp.linalg.norm(t, axis=-1, keepdims=True), 1e-12)

        def rotate_half(x):
            x1, x2 = jnp.split(x, 2, -1)
            return jnp.concatenate([-x2, x1], -1)

        def rotary_tables(n):
            half = jnp.arange(0, DIM_HEAD, 2, dtype=jnp.float32)
            inv_freq = 1.0 / 10000.0 ** (half / DIM_HEAD)
            t = jnp.arange(n, dtype=jnp.float32)
            freqs = t[:, None] * inv_freq[None, :]
            freqs = jnp.concatenate([freqs, freqs], -1)
            base_scale = (half + 0.4 * DIM_HEAD) / (1.4 * DIM_HEAD)
            power = (t - n // 2) / (WINDOW // 2)
            scale = base_scale[None, :] ** power[:, None]
            scale = jnp.concatenate([scale, scale], -1)
            return (freqs, scale)

        def local_attention(q, k, v):
            b, h, n, d = q.shape
            w = WINDOW
            nw = n // w
            bq = q.reshape(b, h, nw, w, d)
            bk = k.reshape(b, h, nw, w, d)
            bv = v.reshape(b, h, nw, w, d)

            def look(t):
                p = jnp.pad(t, ((0, 0), (0, 0), (1, 0), (0, 0), (0, 0)))
                return jnp.concatenate([p[:, :, :nw], p[:, :, 1:]], axis=3)
            bk2, bv2 = (look(bk), look(bv))
            seq = jnp.arange(n).reshape(nw, w)
            seq_p = jnp.pad(seq, ((1, 0), (0, 0)), constant_values=-1)
            jt = jnp.concatenate([seq_p[:nw], seq_p[1:]], axis=1)
            it = seq[:, :, None]
            jb = jt[:, None, :]
            mask = (it < jb) | (it > jb + w) | (jb == -1)
            sim = jnp.einsum('bhwie,bhwje->bhwij', bq, bk2) * QK_SCALE
            sim = jnp.where(mask, -jnp.finfo(sim.dtype).max, sim)
            attn = jax.nn.softmax(sim, -1)
            out = jnp.einsum('bhwij,bhwje->bhwie', attn, bv2)
            return out.reshape(b, h, n, d)

        def attn_layer(x, Wqkv, qs, ksc, Wo):
            b, n, _ = x.shape
            qkv = x @ Wqkv
            q, k, v = jnp.split(qkv, 3, -1)
            sh = lambda t: t.reshape(b, n, HEADS, DIM_HEAD).transpose(0, 2, 1, 3)
            q, k, v = (sh(q), sh(k), sh(v))
            q = l2norm(q) * qs
            k = l2norm(k) * ksc
            freqs, scale = rotary_tables(n)
            cos, sin = (jnp.cos(freqs), jnp.sin(freqs))
            q = q * cos * scale + rotate_half(q) * sin * scale
            inv = 1.0 / scale
            k = k * cos * inv + rotate_half(k) * sin * inv
            out = local_attention(q, k, v)
            out = out.transpose(0, 2, 1, 3).reshape(b, n, INNER)
            return out @ Wo

        def ffn_layer(x, g, bln, W1, b1, W2, b2):
            mu = x.mean(-1, keepdims=True)
            var = ((x - mu) ** 2).mean(-1, keepdims=True)
            xn = (x - mu) / jnp.sqrt(var + 1e-05) * g + bln
            hg = xn @ W1 + b1
            a, gate = jnp.split(hg, 2, -1)
            return a * jax.nn.gelu(gate, approximate=False) @ W2 + b2
        for i in range(DEPTH):
            x = attn_layer(shift_tokens(x), Wqkv[i], q_scale[i], k_scale[i], Wo[i]) + x
            x = ffn_layer(shift_tokens(x), ln_g[i], ln_b[i], W1[i], b1[i], W2[i], b2[i]) + x
        return x

    def _L1_attn_ref(x, w_q, w_k, w_v):
        import jax, jax.numpy as jnp
        import numpy as np
        D_MODEL = 128
        B, T, D = x.shape
        q = jnp.einsum('btk,kd->btd', x, w_q)
        k = jnp.einsum('btk,kd->btd', x, w_k)
        v = jnp.einsum('btk,kd->btd', x, w_v)
        gamma = 1.0 / jnp.sqrt(jnp.float32(D))
        causal = jnp.tril(jnp.ones((T, T), dtype=bool))
        scores = jnp.einsum('bqd,bkd->bqk', q, k) * gamma
        scores = jnp.where(causal[None, :, :], scores, -jnp.inf)
        a = jax.nn.softmax(scores, axis=-1)
        y = jnp.einsum('bqt,btd->bqd', a, v)
        return y

    def _L1_ffn_ref(x, gate, W1, b1, W2, b2):
        import jax, jax.numpy as jnp
        import numpy as np
        N_EXPERTS = 16
        TOP_K = int(N_EXPERTS * 0.2)
        EPS = 1e-12
        raw_gate = jax.nn.softmax(jnp.einsum('btd,de->bte', x, gate), axis=-1)
        _, topk_idx = jax.lax.top_k(raw_gate, TOP_K)
        mask = jax.nn.one_hot(topk_idx, raw_gate.shape[-1], dtype=raw_gate.dtype).sum(axis=2)
        gate_topk = mask * raw_gate
        gate_topk = gate_topk / jnp.maximum(jnp.sum(jnp.abs(gate_topk), axis=-1, keepdims=True), EPS)
        hidden = jax.nn.relu(jnp.einsum('btd,edh->bteh', x, W1) + b1)
        expert_out = jnp.einsum('bteh,ehd->bted', hidden, W2) + b2
        return jnp.einsum('bte,bted->btd', gate_topk, expert_out)
    x = L0_attn_x
    x = x + _layernorm(_L0_attn_ref(_layernorm(x, axis=-1), L0_attn_Wv, L0_attn_Wo, L0_attn_Wg, L0_attn_Wb), axis=-1)
    x = x + _layernorm(_L0_ffn_ref(_layernorm(x, axis=-1), L0_ffn_Wqkv, L0_ffn_q_scale, L0_ffn_k_scale, L0_ffn_Wo, L0_ffn_ln_g, L0_ffn_ln_b, L0_ffn_W1, L0_ffn_b1, L0_ffn_W2, L0_ffn_b2), axis=-1)
    x = x + _layernorm(_L1_attn_ref(_layernorm(x, axis=-1), L1_attn_w_q, L1_attn_w_k, L1_attn_w_v), axis=-1)
    x = x + _layernorm(_L1_ffn_ref(_layernorm(x, axis=-1), L1_ffn_gate, L1_ffn_W1, L1_ffn_b1, L1_ffn_W2, L1_ffn_b2), axis=-1)
    return x

_drawn_inputs = setup_inputs


def setup_inputs(seed=0):
    import zlib

    import numpy as np

    out = dict(_drawn_inputs(seed))
    spreads = {'L0_ffn_q_scale': (1.0, 0.6),
     'L0_ffn_k_scale': (1.0, 0.6),
     'L0_ffn_ln_g': (1.0, 0.6),
     'L0_ffn_ln_b': (0.0, 0.8),
     'L0_ffn_b1': (0.0, 0.589),
     'L0_ffn_b2': (0.0, 0.1)}
    factors = {'L0_ffn_W1': 2.787, 'L1_ffn_b1': 7.671, 'L1_ffn_b2': 5.351}
    for name, (base, spread) in spreads.items():
        noise = np.random.default_rng([zlib.crc32(name.encode()), seed]).standard_normal(out[name].shape)
        drawn = base * np.exp(spread * noise) if base else spread * noise
        out[name] = jnp.asarray(drawn.astype(out[name].dtype))
    for name, factor in factors.items():
        out[name] = (out[name] * factor).astype(out[name].dtype)
    return out
```

```python
import concourse.bass as bass
from concourse import mybir
from contextlib import ExitStack
F32 = mybir.dt.float32
I32 = mybir.dt.int32
ALU = mybir.AluOpType
ACT = mybir.ActivationFunctionType
AX = mybir.AxisListType
P = 128
RSQRT_MAGIC = float(0x5F3759DF)
NEWTON = 3
LN_EPS = 1e-5


def rsqrt_on_dve(v, link, x, y, bits, half, guard=None, bias=None):
    if guard is not None:
        link(v.tensor_scalar(x, x, guard, None, ALU.max))
    else:
        link(v.tensor_scalar(x, x, bias, None, ALU.add))
    link(v.tensor_scalar(bits, x.bitcast(I32), 1, None, ALU.arith_shift_right))
    link(v.tensor_scalar(y.bitcast(I32), bits, -1.0, RSQRT_MAGIC, ALU.mult, ALU.add))
    for _ in range(NEWTON):
        link(v.scalar_tensor_tensor(half, y, -0.5, x, ALU.mult, ALU.mult))
        link(v.tensor_tensor(half, half, y, ALU.mult))
        link(v.scalar_tensor_tensor(y, half, 1.5, y, ALU.add, ALU.mult))


class Steps:

    def __init__(self, eng, own, base=0):
        self.eng, self.own, self.base, self.n = eng, own, base, 0

    def __call__(self, ins):
        ins.then_inc(self.own, 1)
        self.n += 1
        self.eng.wait_ge(self.own, self.base + self.n)


class NormBuffers:

    def __init__(self, sb, n):
        self.n = n
        self.st = sb("ln_st", [P, n, 6])
        self.mv = sb("ln_mv", [P, n, 2])
        self.var = sb("ln_var", [P, n])
        self.rstd = sb("ln_rstd", [P, n])
        self.bits = sb("ln_bits", [P, n], I32)
        self.half = sb("ln_half", [P, n])


def norm_stats(dve, step, nb, src, rows):
    for q in rows:
        step(dve.bn_stats(nb.st[:, q, :], src(q)))


def norm_apply(dve, step, nb, src, dst, lo=0, n=None):
    n = nb.n if n is None else n
    for q in range(lo, lo + n):
        ins = dve.bn_aggr(nb.mv[:, q, :], nb.st[:, q, :])
    step(ins)
    r = slice(lo, lo + n)
    step(dve.tensor_copy(nb.var[:, r], nb.mv[:, r, 1]))
    rsqrt_on_dve(dve, step, nb.var[:, r], nb.rstd[:, r], nb.bits[:, r], nb.half[:, r], bias=LN_EPS)
    for q in range(lo, lo + n):
        ins = dve.tensor_scalar(dst(q), src(q), nb.mv[:, q, 0:1], nb.rstd[:, q:q + 1], ALU.subtract, ALU.mult)
    step(ins)


def stage_a(nc, sem, XA, identf, x_dram, Wv, Wg, Wb, Wo, x1_dram, z_dram, s_dram):
    B, T, D = x_dram.shape
    H = Wg.shape[0]
    DK = D // H
    NC = P // B
    L = T // NC
    HZ = 2 * DK
    NW = D + 2 * H
    HALF = 64
    DVE_HEADS, POOL_HEADS = (0, 11), (11, 16)
    UN = 4
    assert H == 16 and L % UN == 0

    with ExitStack() as ctx:
        sb = lambda n, s, d=F32: ctx.enter_context(nc.sbuf_tensor("a_" + n, s, d))
        pb = lambda n: ctx.enter_context(nc.psum_tensor("a_" + n, [P, 512], F32))
        X = sb("X", [P, L, D])
        xn = sb("xn", [P, L, D])
        R = sb("R", [P, L + 1, D])
        V = sb("V", [P, L, D])
        O = sb("O", [P, L, D])
        GB = sb("GB", [P, L, 2 * H])
        nbeta = sb("nbeta", [P, L, H])
        PH = sb("PH", [P, L + 1, H, HZ])
        Z = sb("Z", [P, H, DK, HZ])
        tmp = sb("tmp", [P, H, DK, HZ])
        tree = sb("tree", [P, H, DK // 2, HZ])
        E = sb("E", [P, H, HZ])
        ss = sb("ss", [P, L * H])
        rn = sb("rn", [P, L * H])
        bits = sb("bits", [P, L * H], I32)
        half = sb("half", [P, L * H])
        ZS = sb("ZS", [B * H, NC, DK, HZ])
        SI = sb("SI", [B * H, NC, DK, DK])
        stmp = sb("stmp", [B * H, DK, DK, DK])
        S0 = sb("S0", [P, H, DK, DK])
        xT = sb("xT", [P, 2, 4, P])
        wv = sb("wv", [P, D])
        wgb = sb("wgb", [2 * H, D])
        wo = sb("wo", [P, D])
        wT = sb("wT", [P, NW + D])
        nb = NormBuffers(sb, L)
        PT = [pb("PT0"), pb("PT1")]
        PV = [pb("PV%d" % k) for k in range(4)]

        x_in, w_in, prev_in, z_out, zs_in, s_out, s0_in, x1_out = (
            sem("a_x_in"), sem("a_w_in"), sem("a_prev_in"), sem("a_z_out"), sem("a_zs_in"), sem("a_s_out"),
            sem("a_s0_in"), sem("a_x1_out"))
        dve_own, pool_own, dve_run, pool_run = sem("a_dve_own"), sem("a_pool_own"), sem("a_dve_run"), sem("a_pool_run")
        pool_apart = sem("a_pool_apart")
        normed, r_ready, w_turned, wT_ready, turned, xT_ready, projected, v_ready, gb_ready = (
            sem("a_normed"), sem("a_r_ready"), sem("a_w_turned"), sem("a_wT_ready"), sem("a_turned"),
            sem("a_xT_ready"), sem("a_projected"), sem("a_v_ready"), sem("a_gb_ready"))
        bv_ready, z_ready, scanned, o_dve, o_pool, x1_ready, xn1_ready, xa_ready = (
            sem("a_bv_ready"), sem("a_z_ready"), sem("a_scanned"), sem("a_o_dve"), sem("a_o_pool"), sem("a_x1_ready"),
            sem("a_xn1_ready"), sem("a_xa_ready"))
        block = ctx.enter_context(nc.Block())
        NG = L // 4

        Rf = R[:, :, :].rearrange("p l d -> p (l d)")
        PHf = PH[:, :, :, :].rearrange("p l h c -> p (l h c)")
        Vf = V[:, :, :].rearrange("p l d -> p (l d)")
        nbf = nbeta[:, :, :].rearrange("p l h -> p (l h)")

        def apart(eng, on_pool):
            if on_pool:
                eng.sem_inc(pool_apart, 1)

        def state_read(eng, step, heads, i, on_pool):
            a, b = heads
            n = b - a
            w = Rf[:, bass.ds(i * D + a * DK, n * DK)].rearrange("p (h k) -> p h k", k=DK)
            apart(eng, on_pool)
            step(eng.tensor_tensor(tmp[:, a:b], Z[:, a:b], w.unsqueeze(3).broadcast_to([P, n, DK, HZ]), ALU.mult))
            out = PHf[:, bass.ds(i * (H * HZ) + a * HZ, n * HZ)].rearrange("p (h c) -> p h c", c=HZ)
            if on_pool:
                step(eng.tensor_tensor(tree[:, a:b], tmp[:, a:b, 0:4], tmp[:, a:b, 4:8], ALU.add))
                step(eng.tensor_tensor(tree[:, a:b, 0:2], tree[:, a:b, 0:2], tree[:, a:b, 2:4], ALU.add))
                apart(eng, on_pool)
                step(eng.tensor_tensor(out, tree[:, a:b, 0], tree[:, a:b, 1], ALU.add))
            else:
                step(eng.tensor_reduce(out, tmp[:, a:b].rearrange("p h k c -> p h c k"), AX.X, ALU.add))

        def state_step(eng, step, heads, i, on_pool):
            a, b = heads
            n = b - a
            state_read(eng, step, heads, i, on_pool)
            w = Rf[:, bass.ds(i * D + a * DK, n * DK)].rearrange("p (h k) -> p h k", k=DK)
            rd = PHf[:, bass.ds(i * (H * HZ) + a * HZ, n * HZ)].rearrange("p (h c) -> p h c", c=HZ)
            nbi = nbf[:, bass.ds(i * H + a, n)]
            bv = Vf[:, bass.ds(i * D + a * DK, n * DK)].rearrange("p (h k) -> p h k", k=DK)
            apart(eng, on_pool)
            step(eng.tensor_tensor(E[:, a:b], rd, nbi.unsqueeze(2).broadcast_to([P, n, HZ]), ALU.mult))
            apart(eng, on_pool)
            step(eng.tensor_tensor(E[:, a:b, DK:HZ], E[:, a:b, DK:HZ], bv, ALU.add))
            apart(eng, on_pool)
            step(eng.tensor_tensor(tmp[:, a:b], w.unsqueeze(3).broadcast_to([P, n, DK, HZ]),
                                   E[:, a:b].unsqueeze(2).broadcast_to([P, n, DK, HZ]), ALU.mult))
            step(eng.tensor_tensor(Z[:, a:b], Z[:, a:b], tmp[:, a:b], ALU.add))

        def recurrence(eng, own, heads, on_pool):
            per = 8 if on_pool else 6
            with eng.Fori(0, L // UN) as t:
                base = eng.snap(t * (UN * per))
                i0 = eng.snap(t * UN)
                step = Steps(eng, own, base)
                for u in range(UN):
                    state_step(eng, step, heads, i0 + u, on_pool)
                assert step.n == UN * per
            step = Steps(eng, own, L * per)
            state_read(eng, step, heads, L, on_pool)
            eng.sem_inc(z_ready, 1)
            return step

        def outputs(eng, step, heads, on_pool):
            a, b = heads
            n = b - a
            flat = tmp[:, :, :, :].rearrange("p h k c -> p (h k c)")
            for u in range(L):
                m = 64 * n
                x = flat[:, a * P + (u % 2) * m:a * P + (u % 2 + 1) * m].rearrange("p (h j k) -> p h j k", j=DK, k=DK)
                step(eng.tensor_tensor(x, PH[:, u + 1, a:b, 0:DK].unsqueeze(2).broadcast_to([P, n, DK, DK]),
                                       S0[:, a:b].rearrange("p h k j -> p h j k"), ALU.mult))
                out = O[:, u, a * DK:b * DK].rearrange("p (h j) -> p h j", j=DK)
                if on_pool:
                    step(eng.tensor_tensor(x[:, :, :, 0:4], x[:, :, :, 0:4], x[:, :, :, 4:8], ALU.add))
                    step(eng.tensor_tensor(x[:, :, :, 0:2], x[:, :, :, 0:2], x[:, :, :, 2:4], ALU.add))
                    step(eng.tensor_tensor(out, x[:, :, :, 0], x[:, :, :, 1], ALU.add))
                else:
                    step(eng.tensor_reduce(out, x, AX.X, ALU.add))
                if u % 4 == 3:
                    o = O[:, u - 3:u + 1, a * DK:b * DK].rearrange("p l (h j) -> p l h j", j=DK)
                    step(eng.tensor_tensor(o, o, PH[:, u - 2:u + 2, a:b, DK:HZ], ALU.add))
                    step(eng.tensor_tensor(o, o, GB[:, u - 3:u + 1, a:b].unsqueeze(3).broadcast_to([P, 4, n, DK]), ALU.mult))
                    eng.sem_inc(o_pool if on_pool else o_dve, 1)

        @block.sync
        def _(sp):
            sp.dma_start(X[:, :, :], x_dram.rearrange("b (c i) d -> (b c) i d", i=L)).then_inc(x_in, 16)
            sp.dma_start(wv[:, :], Wv).then_inc(w_in, 16)
            sp.dma_start(wgb[0:H, :], Wg).then_inc(w_in, 16)
            sp.dma_start(wgb[H:2 * H, :], Wb).then_inc(w_in, 16)
            sp.dma_start(wo[:, :], Wo).then_inc(w_in, 16)
            sp.wait_ge(r_ready, 2)
            for b in range(B):
                sp.dma_start(R[b * NC + 1:(b + 1) * NC, 0, :], R[b * NC:(b + 1) * NC - 1, L, :]).then_inc(prev_in, 16)
            sp.wait_ge(z_ready, 2)
            sp.dma_start(z_dram.rearrange("b c h x -> (b c) (h x)"), Z[:, :, :, :].rearrange("p h k c -> p (h k c)"))\
              .then_inc(z_out, 16)
            sp.wait_ge(z_out, 16)
            for b in range(B):
                sp.dma_start(ZS[b * H:(b + 1) * H].rearrange("p c k z -> p c (k z)"),
                             z_dram[b].rearrange("c h x -> h c x")).then_inc(zs_in, 16)
            sp.wait_ge(scanned, 1)
            for b in range(B):
                sp.dma_start(s_dram[b].rearrange("c h x -> h c x"),
                             SI[b * H:(b + 1) * H].rearrange("p c k j -> p c (k j)")).then_inc(s_out, 16)
            sp.wait_ge(s_out, 16 * B)
            sp.dma_start(S0[:, :, :, :].rearrange("p h k j -> p (h k j)"), s_dram.rearrange("b c h x -> (b c) (h x)"))\
              .then_inc(s0_in, 16)
            sp.wait_ge(x1_ready, 1)
            sp.dma_start(x1_dram.rearrange("b (c i) d -> (b c) i d", i=L), X[:, :, :]).then_inc(x1_out, 16)
            sp.wait_ge(x1_out, 16)

        @block.gpsimd
        def _(pool):
            pool.memset(R[:, 0, :], 0.0).then_inc(r_ready, 1)
            step = Steps(pool, pool_own)
            pool.memset(XA[:, :, 0:1], 0.0)
            step(pool.memset(Z[:, :, :, :], 0.0))
            Zf = Z[:, :, :, :].rearrange("p h k c -> p h (k c)")
            pool.memset(Zf[:, :, 0:(DK - 1) * (HZ + 1) + 1:HZ + 1], 1.0).then_inc(bv_ready, 1)
            for g in range(NG):
                pool.wait_ge(gb_ready, 2 * g + 2)
                r = slice(4 * g, 4 * g + 4)
                v = V[:, r, :].rearrange("p l (h k) -> p l h k", k=DK)
                pool.tensor_tensor(v, v, GB[:, r, H:2 * H].unsqueeze(3).broadcast_to([P, 4, H, DK]), ALU.mult).then_inc(bv_ready, 1)
            pool.wait_ge(prev_in, 16 * B)
            pool.wait_ge(bv_ready, NG + 2)
            step = recurrence(pool, pool_run, POOL_HEADS, True)
            pool.wait_ge(s0_in, 16)
            outputs(pool, step, POOL_HEADS, True)

        @block.tensor
        def _(pe):
            pe.wait_ge(w_in, 64)
            pe.transpose(PT[0][:, 0:D], wv[:, :], identf[:, :])
            pe.transpose(PT[0][:, D:NW], wgb[:, :], identf[0:2 * H, 0:2 * H])
            pe.transpose(PT[0][:, NW:NW + D], wo[:, :], identf[:, :]).then_inc(w_turned, 1)
            pe.wait_ge(wT_ready, 1)

            def turn(src, g, k):
                for u in range(4):
                    ins = pe.transpose(PT[k % 2][:, u * P:(u + 1) * P], src[:, 4 * g + u, :], identf[:, :])
                ins.then_inc(turned, 1)

            def project(g):
                pe.wait_ge(xT_ready, g + 1)
                for u in range(4):
                    if g >= 2 and u % 2 == 0:
                        pe.wait_ge(gb_ready, 2 * (g - 2) + u // 2 + 1)
                    bank = PV[2 * (g % 2) + u // 2]
                    ins = pe.matmul(bank[:, (u % 2) * NW:(u % 2 + 1) * NW], xT[:, g % 2, u, :], wT[:, 0:NW], start=True, stop=True)
                    if u % 2 == 1:
                        ins.then_inc(projected, 1)

            pe.wait_ge(normed, 1)
            for g in range(NG):
                if g >= 2:
                    pe.wait_ge(xT_ready, g - 1)
                turn(xn, g, g)
                if g >= 1:
                    project(g - 1)
            project(NG - 1)
            for g in range(NG):
                pe.wait_ge(o_dve, g + 1)
                pe.wait_ge(o_pool, g + 1)
                if g >= 2:
                    pe.wait_ge(xT_ready, NG + g - 1)
                turn(O, g, g)
                pe.wait_ge(xT_ready, NG + g + 1)
                if g >= 2:
                    pe.wait_ge(v_ready, NG * 2 + g - 1)
                for u in range(4):
                    ins = pe.matmul(PV[g % 2][:, u * P:(u + 1) * P], xT[:, g % 2, u, :], wT[:, NW:NW + D], start=True, stop=True)
                ins.then_inc(projected, 1)
            pe.wait_ge(xn1_ready, 1)
            for g in range(NG):
                if g >= 2:
                    pe.wait_ge(xa_ready, g - 1)
                turn(xn, g, g)

        @block.scalar
        def _(act):
            act.wait_ge(w_turned, 1)
            act.copy(wT[:, :], PT[0][:, 0:NW + D]).then_inc(wT_ready, 1)

            def copy_turned(k, g):
                act.wait_ge(turned, k * NG + g + 1)
                if k * NG + g >= 2:
                    act.wait_ge(projected, 2 * min(g - 1, NG) if k == 0 else 2 * NG + max(0, g - 1))
                act.copy(xT[:, g % 2, :, :].rearrange("p u t -> p (u t)"), PT[g % 2][:, :]).then_inc(xT_ready, 1)

            def copy_projected(g):
                for a in range(2):
                    act.wait_ge(projected, 2 * g + a + 1)
                    x = PV[2 * (g % 2) + a][:, 0:2 * NW].rearrange("p (u n) -> p u n", n=NW)
                    r = slice(4 * g + 2 * a, 4 * g + 2 * a + 2)
                    act.copy(V[:, r, :], x[:, :, 0:D]).then_inc(v_ready, 1)
                    act.activation(GB[:, r, :], x[:, :, D:NW], ACT.Sigmoid).then_inc(gb_ready, 1)

            for g in range(NG):
                copy_turned(0, g)
                if g >= 1:
                    copy_projected(g - 1)
            copy_projected(NG - 1)
            for g in range(NG):
                copy_turned(1, g)
                act.wait_ge(projected, 2 * NG + g + 1)
                act.copy(V[:, 4 * g:4 * g + 4, :].rearrange("p l d -> p (l d)"), PV[g % 2][:, :]).then_inc(v_ready, 1)
            for g in range(NG):
                act.wait_ge(turned, 2 * NG + g + 1)
                x = PT[g % 2][:, :].rearrange("p (u b c) -> p u b c", u=4, b=B)
                for a in range(2):
                    r = slice(HALF * a, HALF * a + HALF)
                    for u in range(4):
                        s = 4 * g + u + a
                        ins = act.copy(XA[r, :, s:s + (NC - 1) * L + 1:L], x[r, u])
                ins.then_inc(xa_ready, 1)

        @block.vector
        def _(dve):
            step = Steps(dve, dve_own)
            dve.wait_ge(x_in, 16)
            xs, xns = (lambda q: X[:, q, :]), (lambda q: xn[:, q, :])
            norm_stats(dve, step, nb, xs, range(L))
            norm_apply(dve, step, nb, xs, xns)
            dve.sem_inc(normed, 1)
            flat = lambda t: t[:, :, :].rearrange("p l d -> p (l d)")
            step(dve.tensor_tensor(flat(O), flat(xn), flat(xn), ALU.mult))
            step(dve.tensor_reduce(ss[:, :], flat(O).rearrange("p (n k) -> p n k", k=DK), AX.X, ALU.add))
            rsqrt_on_dve(dve, step, ss[:, :], rn[:, :], bits[:, :], half[:, :], guard=1e-24)
            dve.tensor_tensor(Rf[:, D:(L + 1) * D].rearrange("p (n k) -> p n k", k=DK), flat(xn).rearrange("p (n k) -> p n k", k=DK),
                              rn[:, :].unsqueeze(2).broadcast_to([P, L * H, DK]), ALU.mult).then_inc(r_ready, 1)
            dve.wait_ge(gb_ready, 2 * NG)
            dve.tensor_scalar(nbeta[:, :, :], GB[:, :, H:2 * H], -1.0, None, ALU.mult).then_inc(bv_ready, 1)
            dve.wait_ge(prev_in, 16 * B)
            dve.wait_ge(bv_ready, NG + 2)
            recurrence(dve, dve_run, DVE_HEADS, False)
            dve.wait_ge(zs_in, 16 * B)
            step(dve.memset(SI[:, 0], 0.0))
            step(dve.tensor_copy(SI[:, 1], ZS[:, 0, :, DK:HZ]))
            BH = B * H
            for c in range(1, NC - 1):
                step(dve.tensor_tensor(stmp[:, :, :, :], ZS[:, c, :, 0:DK].unsqueeze(2).broadcast_to([BH, DK, DK, DK]),
                                       SI[:, c].rearrange("p m j -> p j m").unsqueeze(1).broadcast_to([BH, DK, DK, DK]), ALU.mult))
                step(dve.tensor_reduce(SI[:, c + 1], stmp[:, :, :, :], AX.X, ALU.add))
                step(dve.tensor_tensor(SI[:, c + 1], SI[:, c + 1], ZS[:, c, :, DK:HZ], ALU.add))
            dve.sem_inc(scanned, 1)
            dve.wait_ge(s0_in, 16)
            outputs(dve, step, DVE_HEADS, False)
            vs = lambda q: V[:, q, :]
            for g in range(NG):
                dve.wait_ge(v_ready, 2 * NG + g + 1)
                norm_stats(dve, step, nb, vs, range(4 * g, 4 * g + 4))
            norm_apply(dve, step, nb, vs, vs)
            step(dve.tensor_tensor(flat(X), flat(X), flat(V), ALU.add))
            dve.sem_inc(x1_ready, 1)
            norm_stats(dve, step, nb, xs, range(L))
            norm_apply(dve, step, nb, xs, xns)
            dve.sem_inc(xn1_ready, 1)


def stage_b(nc, sem_of, XA, identf, Wqkv, q_scale, k_scale, Wo, ln_g, ln_b, W1, b1, W2, b2, rot_dram, mask_dram, quad_dram):
    DEPTH, D, QKV = Wqkv.shape
    INNER = QKV // 3
    DH = q_scale.shape[1]
    H = INNER // DH
    FI = W2.shape[1]
    NB, T1 = XA.shape[1], XA.shape[2]
    T = T1 - 1
    NJ = T // P
    NBLK = NB * NJ
    WIN = 32
    KW = P + WIN
    NP = H // 2
    FG = 512
    NG = NB * T // FG
    FK = [min(P, FI - c * P) for c in range(-(-FI // P))]
    HALF = 64
    head = lambda slot: 2 * (slot % NP) + slot // NP
    SB = [(hh * NP + p, min(3, NP - p)) for hh in range(2) for p in range(0, NP, 3)]
    PG = [0, NP, NP // 2, NP + NP // 2]
    NS = len(SB)
    assert NS == 6 and len(FK) == 3 and H == 16 and NJ % 2 == 0

    with ExitStack() as ctx:
        sb = lambda n, s, d=F32: ctx.enter_context(nc.sbuf_tensor("b_" + n, s, d))
        pb = lambda n: ctx.enter_context(nc.psum_tensor("b_" + n, [P, 512], F32))
        sem = lambda n: sem_of("b_" + n)

        XB = sb("XB", [P, NB, T1])
        wqkv = sb("wqkv", [P, QKV])
        wo = sb("wo", [P, NP, D])
        w1 = sb("w1", [P, 2 * FI])
        w2 = sb("w2", [P, len(FK), D])
        b1c = sb("b1c", [P, 2 * len(FK)])
        gcol = sb("gcol", [P, 1])
        bcol = sb("bcol", [P, 1])
        b2c = sb("b2c", [P, 1])
        tab = sb("tab", [P, NJ, 4, DH])
        svec = sb("svec", [P, 4, DH])
        mask = sb("mask", [P, 2, KW])
        xst = sb("xst", [P, 2, P])
        qk = sb("qk", [P, 2 * INNER])
        m2 = sb("m2", [P, 2, 512])
        sq = sb("sq", [P, 2, 512])
        ss = sb("ss", [P, 2 * H])
        rn = sb("rn", [P, 2, 2 * H])
        bits = sb("bits", [P, 2 * H], I32)
        half = sb("half", [P, 2 * H])
        qT = sb("qT", [P, NP, P])
        kT = sb("kT", [P, 2, NP, KW])
        V = sb("V", [P, 4, H, DH])
        VP = sb("VP", [P, 2, H // 4, DH])
        Sm = sb("Sm", [P, 2, H, KW])
        nmx = sb("nmx", [P, H])
        rs = sb("rs", [P, 2, H])
        rinv = sb("rinv", [P, H])
        PTs = sb("PTs", [P, H, P])
        PPs = sb("PPs", [P, H // 4, 4, WIN])
        quad = sb("quad", [P, 4])
        PC = sb("PC", [WIN, H, WIN])
        OT = sb("OT", [P, NP, P])
        st = sb("st", [P, 4, 6])
        mv = sb("mv", [P, 4, 2])
        var4 = sb("var4", [P, 4])
        rstd = sb("rstd", [P, 4])
        bits4 = sb("bits4", [P, 4], I32)
        half4 = sb("half4", [P, 4])
        xn = sb("xn", [P, 4, P])
        xnT = sb("xnT", [P, 2, FG])
        gg = sb("gg", [P, len(FK), FG])
        hg = sb("hg", [P, len(FK), FG])

        PQ = [pb("PQ0"), pb("PQ1")]
        PT = [pb("PT0"), pb("PT1")]
        PS = [pb("PS0"), pb("PS1")]
        PO = [pb("PO0"), pb("PO1")]

        wqkv_in, wo_in, ff_in, tab_in = sem("wqkv_in"), sem("wo_in"), sem("ff_in"), sem("tab_in")
        mask_in, zeroed = sem("mask_in"), sem("zeroed")
        vprev_in = [sem("vprev_in0"), sem("vprev_in1")]
        tab_ready, xst_ready, qkv_mm = sem("tab_ready"), sem("xst_ready"), sem("qkv_mm")
        v_copied, squared, chunk_read, rn_ready = sem("v_copied"), sem("squared"), sem("chunk_read"), sem("rn_ready")
        summed, k_normed, qk_turned, pt_copied, kprev_ready = (
            sem("summed"), sem("k_normed"), sem("qk_turned"), sem("pt_copied"), sem("kprev_ready"))
        scored, masked, max_ready, exped, rinv_ready, p_normed = (
            sem("scored"), sem("masked"), sem("max_ready"), sem("exped"), sem("rinv_ready"), sem("p_normed"))
        p_turned, pp_turned, pp_copied, pv_mm, ot_copied, wo_mm, attn_added = (
            sem("p_turned"), sem("pp_turned"), sem("pp_copied"), sem("pv_mm"), sem("ot_copied"), sem("wo_mm"),
            sem("attn_added"))
        max_found = sem("max_found")
        sq_summed = sem("sq_summed")
        dve_own, f_own = sem("dve_own"), sem("f_own")
        f_turned, f_normed, f_back, xnT_ready, w1_mm, gelued, gated, w2_mm, ff_added = (
            sem("f_turned"), sem("f_normed"), sem("f_back"), sem("xnT_ready"), sem("w1_mm"), sem("gelued"),
            sem("gated"), sem("w2_mm"), sem("ff_added"))
        block = ctx.enter_context(nc.Block())

        aparts = {nc.gpsimd: sem("pool_apart"), nc.tensor: sem("pe_apart"), nc.vector: sem("dve_apart"), nc.sync: sem("sp_apart")}

        def apart(eng):
            eng.sem_inc(aparts[eng], 1)

        def counts(eng, n, *multiples):
            return {m: (eng.snap(n * m) if not isinstance(n, int) else n * m) for m in multiples}

        def turn_use(j):
            return 4 * j + 4 * max(0, j - 1)

        def p_turn_use(j):
            return 4 * min(NJ, j + 2) + 4 * j

        def rows(eng, l, body, last):
            if NB > 1:
                with eng.Fori(0, NB - 1) as b:
                    body(b, False)
            last(NB - 1)

        @block.sync
        def _(sp):
            def load_layer(l):
                at = lambda w: w[bass.ds(l, 1)]
                sp.dma_start(wqkv[:, :], at(Wqkv).rearrange("l p n -> p (l n)"))\
                  .then_inc(wqkv_in, 16)
                sp.dma_start(tab[:, :, :, :], rot_dram).then_inc(tab_in, 16)
                for t, (src, lo) in enumerate([(q_scale, 0), (q_scale, 1), (k_scale, 0), (k_scale, 1)]):
                    for a in range(2):
                        f = (a + lo) % 2
                        sp.dma_start(svec[:, t, a * DH // 2:(a + 1) * DH // 2],
                                     at(src)[0, f * DH // 2:(f + 1) * DH // 2].partition_broadcast(P)).then_inc(tab_in, 16)

            def load_wo(l):
                sp.dma_start(wo[:, :, :], Wo[bass.ds(l, 1)].rearrange("l (c p) n -> p (l c) n", p=P)).then_inc(wo_in, 16)

            def load_ff(l):
                at = lambda w: w[bass.ds(l, 1)]
                sp.dma_start(w1[:, :], at(W1).rearrange("l p n -> p (l n)")).then_inc(ff_in, 16)
                for c, k in enumerate(FK):
                    sp.dma_start(w2[0:k, c, :], at(W2)[:, c * P:c * P + k, :].rearrange("l p n -> p (l n)")).then_inc(ff_in, 16)
                    for a in range(2):
                        sp.dma_start(b1c[0:k, 2 * c + a:2 * c + a + 1],
                                     at(b1)[:, a * FI + c * P:a * FI + c * P + k].rearrange("l p -> p l")).then_inc(ff_in, 16)
                for dst, src in ((gcol, ln_g), (bcol, ln_b), (b2c, b2)):
                    sp.dma_start(dst[:, :], at(src).rearrange("l p -> p l")).then_inc(ff_in, 16)

            sp.dma_start(mask[:, :, :], mask_dram).then_inc(mask_in, 16)
            sp.dma_start(quad[:, :], quad_dram).then_inc(mask_in, 16)
            load_layer(0)
            load_wo(0)
            load_ff(0)

            def vprev(n8, j):
                sp.wait_ge(v_copied, n8[2] + 2 * j)
                apart(sp)
                sp.wait_ge(qk_turned, n8[4] + 4 * j + 1)
                src = V[P - WIN:P, (j - 1) % 4, :, :].rearrange("p (s g) d -> p g s d", g=4)
                for g in range(4):
                    sp.dma_start(VP[WIN * g:WIN * (g + 1), j % 2, :, :], src[:, g]).then_inc(vprev_in[j % 2], 16)

            def row(l):
                def body(b, _):
                    n8 = counts(sp, l * NBLK + b * NJ, 2, 4)
                    for j in range(NJ):
                        vprev(n8, j)
                return body

            def layer(l, more):
                rows(sp, l, row(l), lambda b: row(l)(b, True))
                if more:
                    end = counts(sp, l + 1, 6 * NBLK, 4 * NBLK, NBLK, NG)
                    end_ff = sp.snap(end[NG] + NG)
                    sp.wait_ge(qkv_mm, end[6 * NBLK])
                    apart(sp)
                    sp.wait_ge(chunk_read, end[4 * NBLK])
                    apart(sp)
                    load_layer(l + 1)
                    sp.wait_ge(wo_mm, end[NBLK])
                    apart(sp)
                    load_wo(l + 1)
                    sp.wait_ge(ff_added, end_ff)
                    apart(sp)
                    load_ff(l + 1)

            if DEPTH > 1:
                with sp.Fori(0, DEPTH - 1) as l:
                    layer(l, True)
            layer(DEPTH - 1, False)

        @block.gpsimd
        def _(pool):
            pool.memset(kT[:, 1, :, :], 0.0).then_inc(zeroed, 1)
            pool.memset(V[:, 3, :, :], 0.0).then_inc(zeroed, 1)
            pool.memset(XB[:, :, 0:1], 0.0).then_inc(zeroed, 1)

            def stage(colb, b8, j, done):
                if done:
                    pool.wait_ge(qkv_mm, b8[6] + 6 * (j - 1))
                apart(pool)
                pool.tensor_copy(xst[:, j % 2, :], XAf[:, bass.ds(colb + (j // NJ) * T1 + (j % NJ) * P, P)]).then_inc(xst_ready, 1)

            XAf = XA[:, :, :].rearrange("p b t -> p (b t)")

            def qk_work(n8, j):
                for c in range(4):
                    x = qk[:, c * 512:(c + 1) * 512]
                    pool.wait_ge(chunk_read, n8[4] + 4 * j + c + 1)
                    pool.tensor_tensor(x, x, m2[:, c % 2, :], ALU.add).then_inc(summed, 1)
                pool.wait_ge(rn_ready, n8[1] + j + 1)
                for c in (2, 3):
                    x = qk[:, c * 512:(c + 1) * 512].rearrange("p (h d) -> p h d", d=DH)
                    if c == 2:
                        pool.wait_ge(summed, n8[4] + 4 * j + 4)
                    pool.tensor_tensor(x, x, rn[:, j % 2, 8 * c:8 * c + 8].unsqueeze(2).broadcast_to([P, 8, DH]), ALU.mult)\
                        .then_inc(k_normed, 1)

            def kprev(n8, u8, j):
                if j > 0:
                    pool.wait_ge(pt_copied, u8 + 2 + turn_use(j - 1) + 4)
                apart(pool)
                if j % NJ == 0:
                    pool.memset(kT[:, j % 2, :, 0:WIN], 0.0).then_inc(kprev_ready, 1)
                else:
                    pool.tensor_copy(kT[:, j % 2, :, 0:WIN], kT[:, (j + 1) % 2, :, P:KW]).then_inc(kprev_ready, 1)

            def p_norm(n8, j):
                for a in range(2):
                    heads = slice(8 * a, 8 * a + 8)
                    pool.wait_ge(rinv_ready, n8[2] + 2 * j + a + 1)
                    pool.tensor_tensor(PC[:, heads, :], Sm[0:WIN, j % 2, heads, 0:WIN],
                                       rinv[0:WIN, heads].unsqueeze(2).broadcast_to([WIN, 8, WIN]), ALU.mult)
                    x = Sm[:, j % 2, heads, WIN:KW]
                    pool.tensor_tensor(x, x, rinv[:, heads].unsqueeze(2).broadcast_to([P, 8, P]), ALU.mult).then_inc(p_normed, 1)

            def row(l):
                def body(b, last):
                    n = l * NBLK + b * NJ
                    n8 = counts(pool, n, 1, 2, 4, 6)
                    u8 = pool.snap(l * (8 * NBLK) + b * (8 * NJ)) if NJ else 0
                    colb = pool.snap(b * T1) if not isinstance(b, int) else b * T1
                    for j in range(NJ):
                        if j + 1 < NJ or not last:
                            kprev(n8, u8, j + 1)
                        if j + 2 < NJ or not last:
                            stage(colb, n8, j + 2, True)
                        if j + 1 < NJ:
                            qk_work(n8, j + 1)
                        p_norm(n8, j)
                    if not last:
                        qk_work(n8, NJ)
                return body

            def layer(l):
                pool.wait_ge(tab_in, pool.snap((l + 1) * (16 * 9)))
                pool.tensor_tensor(tab[:, :, :, :], tab[:, :, :, :],
                                   svec[:, :, :].unsqueeze(1).broadcast_to([P, NJ, 4, DH]), ALU.mult).then_inc(tab_ready, 1)
                pool.wait_ge(ff_added, pool.snap((l + 1) * NG))
                n0 = counts(pool, l * NBLK, 1, 2, 4, 6)
                stage(0, n0, 0, False)
                stage(0, n0, 1, False)
                kprev(n0, 0, 0)
                qk_work(n0, 0)
                rows(pool, l, row(l), lambda b: row(l)(b, True))

            pool.wait_ge(zeroed, 3)
            with pool.Fori(0, DEPTH) as l:
                layer(l)

        @block.tensor
        def _(pe):
            def qkv(n8, j, chunks, first=False):
                x = xst[:, j % 2, :]
                if 0 in chunks:
                    pe.wait_ge(xst_ready, n8[1] + j + 1)
                for c in chunks:
                    if c < 2 and not first:
                        pe.wait_ge(v_copied, n8[2] + 2 * j - 1 + c)
                    if c > 1:
                        pe.wait_ge(chunk_read, n8[4] + 4 * j + c - 1)
                    pe.matmul(PQ[c % 2][:, :], x, wqkv[:, c * 512:(c + 1) * 512], start=True, stop=True).then_inc(qkv_mm, 1)

            def turn_qk(n8, u8, j, groups, first=False):
                for g in groups:
                    if g < 2:
                        pe.wait_ge(summed, n8[4] + 4 * j + g + 1)
                    else:
                        pe.wait_ge(k_normed, n8[2] + 2 * j + g - 1)
                    if not (first and g < 2):
                        pe.wait_ge(pt_copied, u8 + 2 + turn_use(j) + g - 1)
                    for p in range(4):
                        mm = pe.transpose(PT[g % 2][:, p * P:(p + 1) * P], qk[:, (4 * g + p) * P:(4 * g + p + 1) * P], identf[:, :])
                    mm.then_inc(qk_turned, 1)

            def scores(n8, u8, nP, j, first):
                for s, (h0, nh) in enumerate(SB):
                    if s == 0:
                        pe.wait_ge(pt_copied, u8 + 2 + turn_use(j) + 4)
                        pe.wait_ge(kprev_ready, n8[1] + j + 1)
                        if not first:
                            pe.wait_ge(pp_copied, n8[1] + nP + 1)
                    elif s == 1:
                        if not first:
                            pe.wait_ge(attn_added, n8[1] + nP + 1)
                    else:
                        pe.wait_ge(masked, n8[6] + 6 * j + s - 1)
                    for i in range(nh):
                        p, hh = (h0 + i) % NP, (h0 + i) // NP
                        mm = pe.matmul(PS[s % 2][:, i * KW:(i + 1) * KW], qT[HALF * hh:HALF * hh + HALF, p, :],
                                       kT[HALF * hh:HALF * hh + HALF, j % 2, p, :], start=True, stop=True)
                    mm.then_inc(scored, 1)

            def turn_p(n8, u8, j, g):
                pe.wait_ge(p_normed, n8[2] + 2 * j + g % 2 + 1)
                pe.wait_ge(pt_copied, u8 + 2 + p_turn_use(j) + g - 1)
                for i in range(4):
                    mm = pe.transpose(PT[g % 2][:, i * P:(i + 1) * P], Sm[:, j % 2, PG[g] + i, WIN:KW], identf[:, :])
                mm.then_inc(p_turned, 1)

            def turn_prev(n8, nS, j):
                pe.wait_ge(p_normed, n8[2] + 2 * j + 2)
                pe.wait_ge(masked, n8[6] + 6 * nS - 1)
                apart(pe)
                for g in range(4):
                    mm = pe.transpose(PS[0][:, g * WIN:(g + 1) * WIN], PC[:, 4 * g:4 * g + 4, :],
                                      identf[0:WIN, 0:WIN])
                mm.then_inc(pp_turned, 1)

            def pv(n8, u8, j, a, first, b2):
                pe.wait_ge(pt_copied, u8 + 2 + p_turn_use(j) + 2 * a + 2)
                if a == 0:
                    pe.wait_ge(pp_copied, n8[1] + j + 2)
                    pe.wait_ge(v_copied, n8[2] + 2 * j + 2)
                    pe.wait_ge(vprev_in[j % 2], b2 + (j // 2 + 1) * 64)
                if not first:
                    pe.wait_ge(ot_copied, n8[2] + 2 * j + 1 + a)
                for hh in range(2):
                    r = slice(HALF * hh, HALF * hh + HALF)
                    G = 2 * hh + a
                    for g in range(4):
                        pe.matmul(PO[a][r, g * P:(g + 1) * P], V[:, j % 4, 4 * G + g, :], PTs[:, 4 * G + g, :],
                                  start=(g == 0), stop=False, skip_group_check=True)
                    mm = pe.matmul(PO[a][r, :].rearrange("p (g t) -> p g t", g=4)[:, :, 0:WIN], VP[:, j % 2, G, :],
                                   PPs[:, G, :, :], start=False, stop=True, skip_group_check=True)
                mm.then_inc(pv_mm, 1)

            def out_proj(n8, nS, j):
                pe.wait_ge(masked, n8[6] + 6 * nS)
                for p in range(NP):
                    if p % 4 == 0:
                        pe.wait_ge(ot_copied, n8[2] + 2 * j + p // 4 + 3)
                    mm = pe.matmul(PS[1][:, 0:P], wo[:, p, :], OT[:, p, :], start=(p == 0), stop=(p == NP - 1))
                mm.then_inc(wo_mm, 1)

            def turn_first(n8, u8, j):
                turn_p(n8, u8, j, 0)
                turn_p(n8, u8, j, 1)
                turn_prev(n8, min(NJ, j + 2), j)

            def slot(n8, u8, b2, j, nxt):
                if j >= 1:
                    turn_first(n8, u8, j - 1)
                if nxt:
                    qkv(n8, j + 1, (0, 1))
                if j >= 1:
                    pv(n8, u8, j - 1, 0, False, b2)
                if nxt:
                    qkv(n8, j + 1, (2,))
                if j >= 1:
                    turn_p(n8, u8, j - 1, 2)
                    turn_p(n8, u8, j - 1, 3)
                if nxt:
                    qkv(n8, j + 1, (3,))
                if j >= 1:
                    pv(n8, u8, j - 1, 1, False, b2)
                if nxt:
                    qkv(n8, j + 1, (4,))
                    turn_qk(n8, u8, j + 1, (0, 1))
                    qkv(n8, j + 1, (5,))
                if j >= 1:
                    out_proj(n8, min(NJ, j + 1), j - 1)

            def row(l):
                def body(b, last):
                    n8 = counts(pe, l * NBLK + b * NJ, 1, 2, 4, 6)
                    u8 = pe.snap(l * (8 * NBLK) + b * (8 * NJ))
                    b2 = pe.snap((l * NBLK + b * NJ) * 32)
                    for j in range(NJ):
                        turn_qk(n8, u8, j, (2, 3))
                        scores(n8, u8, max(0, j - 1), j, False)
                        slot(n8, u8, b2, j, j + 1 < NJ)
                    slot_end(n8, u8, b2, not last)
                return body

            def slot_end(n8, u8, b2, nxt):
                turn_first(n8, u8, NJ - 1)
                if nxt:
                    qkv(n8, NJ, (0, 1))
                pv(n8, u8, NJ - 1, 0, False, b2)
                if nxt:
                    qkv(n8, NJ, (2,))
                turn_p(n8, u8, NJ - 1, 2)
                turn_p(n8, u8, NJ - 1, 3)
                if nxt:
                    qkv(n8, NJ, (3,))
                pv(n8, u8, NJ - 1, 1, False, b2)
                if nxt:
                    qkv(n8, NJ, (4,))
                    turn_qk(n8, u8 + 8 * NJ - turn_use(NJ), NJ, (0, 1))
                    qkv(n8, NJ, (5,))
                out_proj(n8, NJ, NJ - 1)

            def ff_turn(g8, n):
                b, t0 = n // (T // FG), (n % (T // FG)) * FG
                if n > 0:
                    pe.wait_ge(f_normed, g8[1] + n)
                for q in range(4):
                    mm = pe.transpose(PT[0][:, q * P:(q + 1) * P], XB[:, b, t0 + q * P:t0 + (q + 1) * P], identf[:, :])
                mm.then_inc(f_turned, 1)

            def ff_back(g8, n):
                pe.wait_ge(f_normed, g8[1] + n + 1)
                if n > 0:
                    pe.wait_ge(xnT_ready, g8[1] + n)
                for q in range(4):
                    mm = pe.transpose(PT[1][:, q * P:(q + 1) * P], xn[:, q, :], identf[:, :])
                mm.then_inc(f_back, 1)

            def ff_up(g8, n):
                pe.wait_ge(xnT_ready, g8[1] + n + 1)
                for c, k in enumerate(FK):
                    for a in range(2):
                        if c == 0 and n > 0:
                            pe.wait_ge(gated, g8[3] + 3 * n)
                        if c == 2:
                            pe.wait_ge((gelued, gated)[a], g8[3] + 3 * n + 1)
                        bank = (PQ, PS)[c % 2][a]
                        lo = (1 - a) * FI + c * P
                        pe.matmul(bank[0:k, :], w1[:, lo:lo + k], xnT[:, n % 2, :], start=True, stop=True).then_inc(w1_mm, 1)

            def ff_down(g8, n):
                if n > 1:
                    pe.wait_ge(ff_added, g8[1] + NG + n - 1)
                for c, k in enumerate(FK):
                    pe.wait_ge(gated, g8[3] + 3 * n + c + 1)
                    mm = pe.matmul(PO[n % 2][:, :], w2[0:k, c, :], hg[0:k, c, :], start=(c == 0), stop=(c == 2))
                mm.then_inc(w2_mm, 1)

            with pe.Fori(0, DEPTH) as l:
                pe.wait_ge(wqkv_in, pe.snap((l + 1) * 16))
                pe.wait_ge(wo_in, pe.snap((l + 1) * 16))
                n0 = counts(pe, l * NBLK, 1, 2, 4, 6)
                qkv(n0, 0, range(6), True)
                turn_qk(n0, pe.snap(l * (8 * NBLK)), 0, (0, 1), True)
                rows(pe, l, row(l), lambda b: row(l)(b, True))
                g8 = counts(pe, l * NG, 1, 3)
                pe.wait_ge(attn_added, pe.snap((l + 1) * NBLK + 1))
                ff_turn(g8, 0)
                ff_back(g8, 0)
                pe.wait_ge(ff_in, pe.snap((l + 1) * (16 * 13)))
                for n in range(NG):
                    if n + 1 < NG:
                        ff_turn(g8, n + 1)
                    ff_up(g8, n)
                    if n + 1 < NG:
                        ff_back(g8, n + 1)
                    ff_down(g8, n)

        @block.scalar
        def _(act):
            def copy_v(n8, j, c):
                act.wait_ge(qkv_mm, n8[6] + 6 * j + c + 5)
                act.copy(V[:, j % 4, :, :].rearrange("p (h a) d -> p h a d", h=2)[:, :, 4 * c:4 * c + 4, :],
                         PQ[c][:, :].rearrange("p (a h d) -> p h a d", h=2, d=DH)).then_inc(v_copied, 1)

            def square(n8, j, c):
                act.wait_ge(qkv_mm, n8[6] + 6 * j + c + 1)
                if c > 1:
                    act.wait_ge(sq_summed, n8[4] + 4 * j + c - 1)
                act.activation(sq[:, c % 2, :], PQ[c % 2][:, :], ACT.Square).then_inc(squared, 1)

            def copy_qk(n8, j, groups):
                for g in groups:
                    act.wait_ge(qk_turned, n8[4] + 4 * j + g + 1)
                    src = PT[g % 2][:, :].rearrange("p (c t) -> p c t", t=P)
                    dst = qT[:, 4 * g:4 * g + 4, :] if g < 2 else kT[:, j % 2, 4 * g - 8:4 * g - 4, WIN:KW]
                    act.copy(dst, src).then_inc(pt_copied, 1)

            def exps(n8, j, s0, s1):
                for s in range(s0, s1):
                    if s % 8 == 0:
                        act.wait_ge(max_ready, n8[2] + 2 * j + s // 8 + 1)
                    x = Sm[:, j % 2, s, :]
                    act.activation(x, x, ACT.Exp, bias=nmx[:, s:s + 1], scale=rn[:, j % 2, head(s):head(s) + 1],
                                   accum_out=rs[:, j % 2, s:s + 1]).then_inc(exped, 1)

            def copy_p(n8, j, g):
                act.wait_ge(p_turned, n8[4] + 4 * j + g + 1)
                act.copy(PTs[:, PG[g]:PG[g] + 4, :], PT[g % 2][:, :].rearrange("p (c t) -> p c t", t=P)).then_inc(pt_copied, 1)

            def copy_ot(n8, j, a):
                act.wait_ge(pv_mm, n8[2] + 2 * j + a + 1)
                act.copy(OT[:, 4 * a:4 * a + 4, :], PO[a][:, :].rearrange("p (c t) -> p c t", t=P)).then_inc(ot_copied, 1)

            def slot(n8, j, nxt, this=True):
                if this:
                    copy_qk(n8, j, (2, 3))
                if j >= 1:
                    copy_p(n8, j - 1, 0)
                    copy_p(n8, j - 1, 1)
                if this:
                    exps(n8, j, 0, 4)
                if nxt:
                    square(n8, j + 1 if this else j, 0)
                    square(n8, j + 1 if this else j, 1)
                if this:
                    exps(n8, j, 4, 8)
                if j >= 1:
                    copy_ot(n8, j - 1, 0)
                if nxt:
                    square(n8, j + 1 if this else j, 2)
                if j >= 1:
                    copy_p(n8, j - 1, 2)
                    copy_p(n8, j - 1, 3)
                if this:
                    exps(n8, j, 8, 12)
                if nxt:
                    square(n8, j + 1 if this else j, 3)
                if j >= 1:
                    copy_ot(n8, j - 1, 1)
                if this:
                    exps(n8, j, 12, 16)
                if nxt:
                    copy_v(n8, j + 1 if this else j, 0)
                    copy_qk(n8, j + 1 if this else j, (0, 1))
                    copy_v(n8, j + 1 if this else j, 1)

            def row(l):
                def body(b, last):
                    n8 = counts(act, l * NBLK + b * NJ, 1, 2, 4, 6)
                    for j in range(NJ):
                        slot(n8, j, j + 1 < NJ)
                    slot(n8, NJ, not last, False)
                return body

            act.sem_inc(pt_copied, 2)
            act.sem_inc(ot_copied, 2)
            act.wait_ge(zeroed, 3)
            with act.Fori(0, DEPTH) as l:
                n0 = counts(act, l * NBLK, 2, 4, 6)
                for c in range(4):
                    square(n0, 0, c)
                copy_v(n0, 0, 0)
                copy_v(n0, 0, 1)
                copy_qk(n0, 0, (0, 1))
                rows(act, l, row(l), lambda b: row(l)(b, True))
                g8 = counts(act, l * NG, 1, 3, 6)

                def norm_out(n):
                    act.wait_ge(f_back, g8[1] + n + 1)
                    if n > 1:
                        act.wait_ge(w1_mm, g8[6] + 6 * (n - 1))
                    act.activation(xnT[:, n % 2, :], PT[1][:, :], ACT.Identity, bias=bcol[:, 0:1], scale=gcol[:, 0:1])\
                       .then_inc(xnT_ready, 1)

                act.wait_ge(ff_in, act.snap((l + 1) * (16 * 13)))
                norm_out(0)
                for n in range(NG):
                    for c, k in enumerate(FK):
                        act.wait_ge(w1_mm, g8[6] + 6 * n + 2 * c + 1)
                        if n > 0 and c == 0:
                            act.wait_ge(gated, g8[3] + 3 * n)
                        act.activation(gg[0:k, c, :], (PQ, PS)[c % 2][0][0:k, :], ACT.Gelu, bias=b1c[0:k, 2 * c + 1:2 * c + 2])\
                           .then_inc(gelued, 1)
                    if n + 1 < NG:
                        norm_out(n + 1)

        @block.vector
        def _(dve):
            XAf = XA[:, :, :].rearrange("p b t -> p (b t)")
            XBf = XB[:, :, :].rearrange("p b t -> p (b t)")
            OWN = 12

            def linker(base):
                k = [0]

                def link(ins):
                    k[0] += 1
                    ins.then_inc(dve_own, 1)
                    dve.wait_ge(dve_own, base + k[0])
                return link

            def chunk(n8, j, c):
                src = PQ[c % 2][:, :].rearrange("p (h d) -> p h d", d=DH)
                swapped = PQ[c % 2][:, :].rearrange("p (h a d) -> p h a d", a=2, d=DH // 2)[:, :, ::-1, :]
                t = 2 * (c // 2)
                ctab = tab[:, j % NJ, t, :].unsqueeze(1).broadcast_to([P, 8, DH])
                stab = tab[:, j % NJ, t + 1, :].rearrange("p (a d) -> p a d", a=2).unsqueeze(1).broadcast_to([P, 8, 2, DH // 2])
                dve.wait_ge(squared, n8[4] + 4 * j + c + 1)
                dve.tensor_tensor(qk[:, c * 512:(c + 1) * 512].rearrange("p (h d) -> p h d", d=DH), src, ctab, ALU.mult)
                if c > 1:
                    dve.wait_ge(summed, n8[4] + 4 * j + c - 1)
                dve.tensor_tensor(m2[:, c % 2, :].rearrange("p (h a d) -> p h a d", a=2, d=DH // 2), swapped, stab, ALU.mult)\
                    .then_inc(chunk_read, 1)
                dve.tensor_reduce(ss[:, 8 * c:8 * c + 8], sq[:, c % 2, :].rearrange("p (h d) -> p h d", d=DH), AX.X, ALU.add)\
                   .then_inc(sq_summed, 1)

            def norms(n8, j, own):
                dve.wait_ge(sq_summed, n8[4] + 4 * j + 4)
                k = [0]
                link = linker(own)
                rsqrt_on_dve(dve, link, ss[:, :], rn[:, j % 2, :], bits[:, :], half[:, :], guard=1e-24)
                dve.sem_inc(rn_ready, 1)

            def masks(n8, j):
                var = 1 if j == 0 else 0
                for s, (h0, nh) in enumerate(SB):
                    dve.wait_ge(scored, n8[6] + 6 * j + s + 1)
                    dve.tensor_tensor(Sm[:, j % 2, h0:h0 + nh, :], PS[s % 2][:, 0:nh * KW].rearrange("p (h k) -> p h k", k=KW),
                                      mask[:, var, :].unsqueeze(1).broadcast_to([P, nh, KW]), ALU.add).then_inc(masked, 1)
                    if s % 3 == 2:
                        a = s // 3
                        dve.wait_ge(masked, n8[6] + 6 * j + 3 * a + 3)
                        x = nmx[:, 8 * a:8 * a + 8]
                        dve.tensor_reduce(x, Sm[:, j % 2, 8 * a:8 * a + 8, :], AX.X, ALU.max, negate=True).then_inc(max_found, 1)
                        dve.wait_ge(max_found, n8[2] + 2 * j + a + 1)
                        dve.tensor_tensor(x, x, rn[:, j % 2, a:H:2], ALU.mult).then_inc(max_ready, 1)

            def inverses(n8, j):
                for a in range(2):
                    dve.wait_ge(exped, n8[16] + 16 * j + 8 * a + 8)
                    dve.reciprocal(rinv[:, 8 * a:8 * a + 8], rs[:, j % 2, 8 * a:8 * a + 8]).then_inc(rinv_ready, 1)

            def spread_prev(n8, j):
                dve.wait_ge(pp_turned, n8[1] + j + 1)
                src = PS[0][:, 0:4 * WIN].rearrange("p (s t) -> p s t", t=WIN).unsqueeze(2).broadcast_to([P, 4, 4, WIN])
                dve.tensor_tensor(PPs[:, :, :, :], src, quad[:, :].unsqueeze(1).unsqueeze(3).broadcast_to([P, 4, 4, WIN]),
                                  ALU.mult).then_inc(pp_copied, 1)

            def residual(n8, colb, j):
                dve.wait_ge(wo_mm, n8[1] + j + 1)
                for a in range(2):
                    cols = bass.ds(colb + j * P + a, P)
                    r = slice(HALF * a, HALF * a + HALF)
                    ins = dve.tensor_tensor(XBf[r, cols], PS[1][r, 0:P], XAf[r, cols], ALU.add)
                ins.then_inc(attn_added, 1)

            def row(l):
                def body(b, last):
                    n8 = counts(dve, l * NBLK + b * NJ, 1, 2, 4, 6, 16)
                    own = dve.snap(l * ((NBLK + NG) * OWN) + b * (NJ * OWN))
                    colb = dve.snap(b * T1) if not isinstance(b, int) else b * T1
                    for j in range(NJ):
                        masks(n8, j)
                        if j >= 1:
                            spread_prev(n8, j - 1)
                        if j + 1 < NJ:
                            for c in range(4):
                                chunk(n8, j + 1, c)
                            norms(n8, j + 1, own + OWN * (j + 1))
                        inverses(n8, j)
                        if j >= 1:
                            residual(n8, colb, j - 1)
                    spread_prev(n8, NJ - 1)
                    if not last:
                        for c in range(4):
                            chunk(n8, NJ, c)
                        norms(n8, NJ, own + OWN * NJ)
                    residual(n8, colb, NJ - 1)
                return body

            dve.sem_inc(attn_added, 1)
            dve.sem_inc(pp_copied, 1)
            dve.sem_inc(ff_added, NG)
            dve.wait_ge(mask_in, 32)
            dve.wait_ge(zeroed, 3)
            with dve.Fori(0, DEPTH) as l:
                n0 = counts(dve, l * NBLK, 1, 2, 4, 6, 16)
                dve.wait_ge(tab_ready, l + 1)
                for c in range(4):
                    chunk(n0, 0, c)
                norms(n0, 0, dve.snap(l * ((NBLK + NG) * OWN)))
                rows(dve, l, row(l), lambda b: row(l)(b, True))
                g8 = counts(dve, l * NG, 1, 3, 6)
                own = dve.snap(l * ((NBLK + NG) * OWN) + NBLK * OWN)

                def layer_norm(n):
                    x = PT[0][:, :].rearrange("p (q c) -> p q c", q=4)
                    dve.wait_ge(f_turned, g8[1] + n + 1)
                    for q in range(4):
                        ins = dve.bn_stats(st[:, q, :], x[:, q, :])
                    ins.then_inc(f_own, 1)
                    dve.wait_ge(f_own, g8[3] + 3 * n + 1)
                    apart(dve)
                    for q in range(4):
                        ins = dve.bn_aggr(mv[:, q, :], st[:, q, :])
                    ins.then_inc(f_own, 1)
                    dve.wait_ge(f_own, g8[3] + 3 * n + 2)
                    dve.tensor_copy(var4[:, :], mv[:, :, 1]).then_inc(f_own, 1)
                    dve.wait_ge(f_own, g8[3] + 3 * n + 3)
                    rsqrt_on_dve(dve, linker(own + OWN * n), var4[:, :], rstd[:, :], bits4[:, :], half4[:, :], bias=1e-5)
                    if n > 0:
                        dve.wait_ge(f_back, g8[1] + n)
                    for q in range(4):
                        ins = dve.tensor_scalar(xn[:, q, :], x[:, q, :], mv[:, q, 0:1], rstd[:, q:q + 1], ALU.subtract, ALU.mult)
                    ins.then_inc(f_normed, 1)

                layer_norm(0)
                for n in range(NG):
                    if n + 1 < NG:
                        layer_norm(n + 1)
                    for c, k in enumerate(FK):
                        dve.wait_ge(w1_mm, g8[6] + 6 * n + 2 * c + 2)
                        dve.wait_ge(gelued, g8[3] + 3 * n + c + 1)
                        if n > 0 and c == 0:
                            dve.wait_ge(w2_mm, g8[1] + n)
                        dve.scalar_tensor_tensor(hg[0:k, c, :], (PQ, PS)[c % 2][1][0:k, :], b1c[0:k, 2 * c:2 * c + 1],
                                                 gg[0:k, c, :], ALU.add, ALU.mult).then_inc(gated, 1)
                    b, t0 = n // (T // FG), (n % (T // FG)) * FG
                    dve.wait_ge(w2_mm, g8[1] + n + 1)
                    for a in range(2):
                        r = slice(HALF * a, HALF * a + HALF)
                        ins = dve.scalar_tensor_tensor(XA[r, b, t0 + a:t0 + a + FG], PO[n % 2][r, :], b2c[r, 0:1],
                                                       XB[r, b, t0 + a:t0 + a + FG], ALU.add, ALU.add)
                    ins.then_inc(ff_added, 1)


def stage_c(nc, sem, XA, X2, Y, identf, x1_dram, Wq, Wk, Wv, tri_dram):
    B, T, D = x1_dram.shape
    NJ = T // P
    NBLK = B * NJ
    GAMMA = float(D) ** -0.5
    HALF = 64
    FG = 512
    NG = B * T // FG
    cum = lambda i: i if i <= 4 else 4 + 2 * (i - 4)
    CUM = cum(NJ)
    assert NJ == 8

    with ExitStack() as ctx:
        sb = lambda n, s, d=F32: ctx.enter_context(nc.sbuf_tensor("c_" + n, s, d))
        pb = lambda n, w=512: ctx.enter_context(nc.psum_tensor("c_" + n, [P, w], F32))
        xu = sb("xu", [P, 2, FG])
        xnT = sb("xnT", [P, B * T])
        xb = sb("xb", [P, T])
        qT = sb("qT", [P, T])
        kT = sb("kT", [P, T])
        V = sb("V", [P, NJ, D])
        wq = sb("wq", [P, D])
        wk = sb("wk", [P, D])
        wv = sb("wv", [P, D])
        tri = sb("tri", [P, P])
        E = sb("E", [P, 2, T])
        ET = sb("ET", [P, 2, NJ, P])
        nmx = sb("nmx", [P, 2])
        rs = sb("rs", [P, 2])
        rinv = sb("rinv", [P, 2])
        nb = NormBuffers(lambda n, s, d=F32: sb(n, s, d), NBLK)
        PS = [pb("PS0", 1024), pb("PS1", 1024)]
        PT = [pb("PT0"), pb("PT1")]
        PA, PY = pb("PA"), pb("PY")

        x1_in, w_in, dve_own = sem("c_x1_in"), sem("c_w_in"), sem("c_dve_own")
        unshifted, turned, y_copied, xn_ready, xnT_ready = (
            sem("c_unshifted"), sem("c_turned"), sem("c_y_copied"), sem("c_xn_ready"), sem("c_xnT_ready"))
        xb_ready, projected, copied, scored, masked, max_found, max_ready, exped = (
            sem("c_xb_ready"), sem("c_projected"), sem("c_copied"), sem("c_scored"), sem("c_masked"),
            sem("c_max_found"), sem("c_max_ready"), sem("c_exped"))
        rinv_ready, p_turned, pt_copied, pv_mm, y_ready, pool_apart = (
            sem("c_rinv_ready"), sem("c_p_turned"), sem("c_pt_copied"), sem("c_pv_mm"), sem("c_y_ready"), sem("c_pool_apart"))
        block = ctx.enter_context(nc.Block())

        @block.sync
        def _(sp):
            sp.dma_start(X2[:, :, :], x1_dram.rearrange("b (j p) d -> p (b j) d", p=P)).then_inc(x1_in, 16)
            for dst, src in ((wq, Wq), (wk, Wk), (wv, Wv), (tri, tri_dram)):
                sp.dma_start(dst[:, :], src).then_inc(w_in, 16)

        @block.gpsimd
        def _(pool):
            pool.wait_ge(xnT_ready, NG)
            with pool.Fori(0, B) as b:
                col = pool.snap(b * T)
                pool.wait_ge(projected, pool.snap(6 * b))
                pool.sem_inc(pool_apart, 1)
                pool.tensor_copy(xb[:, :], xnT[:, bass.ds(col, T)]).then_inc(xb_ready, 1)

        @block.tensor
        def _(pe):
            for g in range(NG):
                pe.wait_ge(unshifted, g + 1)
                if g >= 2:
                    pe.wait_ge(y_copied, g - 1)
                for u in range(4):
                    ins = pe.transpose(PT[g % 2][:, u * P:(u + 1) * P], xu[:, g % 2, u * P:(u + 1) * P], identf[:, :])
                ins.then_inc(turned, 1)
            pe.wait_ge(xn_ready, 1)
            for g in range(NG):
                if g >= 2:
                    pe.wait_ge(xnT_ready, g - 1)
                for u in range(4):
                    ins = pe.transpose(PT[g % 2][:, u * P:(u + 1) * P], Y[:, 4 * g + u, :], identf[:, :])
                ins.then_inc(turned, 1)
            pe.wait_ge(w_in, 64)
            pe.wait_ge(xnT_ready, NG)

            def scores(b8, b6, i):
                if i < 2:
                    pe.wait_ge(copied, b6 + 4)
                else:
                    pe.wait_ge(exped, b8 + i - 1)
                n = (i + 1) * P
                for lo in range(0, n, 512):
                    hi = min(n, lo + 512)
                    ins = pe.matmul(PS[i % 2][:, lo:hi], qT[:, i * P:(i + 1) * P], kT[:, lo:hi], start=True, stop=True)
                ins.then_inc(scored, 1)

            with pe.Fori(0, B) as b:
                b6, b8, b12 = pe.snap(b * 6), pe.snap(b * NJ), pe.snap(b * CUM)
                pe.wait_ge(xb_ready, pe.snap(b + 1))
                pe.wait_ge(exped, b8)
                for k, w in enumerate((wq, wk)):
                    for h in range(2):
                        pe.matmul(PS[k][:, h * 512:(h + 1) * 512], w[:, :], xb[:, h * 512:(h + 1) * 512], start=True, stop=True)\
                          .then_inc(projected, 1)
                for h in range(2):
                    if h == 1:
                        pe.wait_ge(copied, b6 + 5)
                    for u in range(4):
                        ins = pe.matmul(PA[:, u * P:(u + 1) * P], xb[:, (4 * h + u) * P:(4 * h + u + 1) * P], wv[:, :],
                                        start=True, stop=True)
                    ins.then_inc(projected, 1)
                scores(b8, b6, 0)
                for i in range(NJ):
                    if i + 1 < NJ:
                        scores(b8, b6, i + 1)
                    pe.wait_ge(exped, b8 + i + 1)
                    pe.wait_ge(pt_copied, b12 + cum(i))
                    for g in range(i // 4 + 1):
                        for u in range(4 * g, min(4 * g + 4, i + 1)):
                            ins = pe.transpose(PT[g][:, (u % 4) * P:(u % 4 + 1) * P], E[:, i % 2, u * P:(u + 1) * P], identf[:, :])
                        ins.then_inc(p_turned, 1)
                    pe.wait_ge(copied, b6 + 6)
                    pe.wait_ge(y_ready, b8 + i)
                    for u in range(i + 1):
                        if u % 4 == 0:
                            pe.wait_ge(pt_copied, b12 + cum(i) + u // 4 + 1)
                        ins = pe.matmul(PY[:, 0:D], ET[:, i % 2, u, :], V[:, u, :], start=(u == 0), stop=(u == i))
                    ins.then_inc(pv_mm, 1)

        @block.scalar
        def _(act):
            for g in range(NG + 1):
                if g < NG:
                    if g >= 2:
                        act.wait_ge(turned, g - 1)
                    b, t0 = g // 2, (g % 2) * FG
                    act.copy(xu[0:HALF, g % 2, :], XA[0:HALF, b, t0:t0 + FG])
                    act.copy(xu[HALF:P, g % 2, :], XA[HALF:P, b, t0 + 1:t0 + 1 + FG]).then_inc(unshifted, 1)
                if g >= 1:
                    act.wait_ge(turned, g)
                    act.copy(Y[:, 4 * g - 4:4 * g, :].rearrange("p n d -> p (n d)"), PT[(g - 1) % 2][:, :]).then_inc(y_copied, 1)
            for g in range(NG):
                act.wait_ge(turned, NG + g + 1)
                act.copy(xnT[:, g * FG:(g + 1) * FG], PT[g % 2][:, :]).then_inc(xnT_ready, 1)
            with act.Fori(0, B) as b:
                b6, b8 = act.snap(b * 6), act.snap(b * NJ)
                act.wait_ge(pv_mm, b8)
                for k, dst in enumerate((qT, kT)):
                    for h in range(2):
                        act.wait_ge(projected, b6 + 2 * k + h + 1)
                        act.copy(dst[:, h * 512:(h + 1) * 512], PS[k][:, h * 512:(h + 1) * 512]).then_inc(copied, 1)
                for h in range(2):
                    act.wait_ge(projected, b6 + 5 + h)
                    act.copy(V[:, 4 * h:4 * h + 4, :].rearrange("p n d -> p (n d)"), PA[:, :]).then_inc(copied, 1)
                for i in range(NJ):
                    n = (i + 1) * P
                    act.wait_ge(max_ready, b8 + i + 1)
                    if i >= 2:
                        act.wait_ge(p_turned, act.snap(b * CUM + cum(i - 1)))
                        act.wait_ge(rinv_ready, b8 + i - 1)
                    act.activation(E[:, i % 2, 0:n], PS[i % 2][:, 0:n], ACT.Exp, bias=nmx[:, i % 2:i % 2 + 1], scale=GAMMA,
                                   accum_out=rs[:, i % 2:i % 2 + 1]).then_inc(exped, 1)

        @block.vector
        def _(dve):
            step = Steps(dve, dve_own)
            ys, xs = (lambda q: Y[:, q, :]), (lambda q: X2[:, q, :])
            for g in range(NG):
                dve.wait_ge(y_copied, g + 1)
                norm_stats(dve, step, nb, ys, range(4 * g, 4 * g + 4))
            norm_apply(dve, step, nb, ys, ys)
            dve.wait_ge(x1_in, 16)
            step(dve.tensor_tensor(X2[:, :, :], X2[:, :, :], Y[:, :, :], ALU.add))
            norm_stats(dve, step, nb, xs, range(NBLK))
            norm_apply(dve, step, nb, xs, ys)
            dve.sem_inc(xn_ready, 1)
            dve.wait_ge(w_in, 64)
            dve.wait_ge(turned, 2 * NG)
            Yf = Y[:, :, :].rearrange("p n d -> p (n d)")

            def maxima(b8, i):
                dve.wait_ge(scored, b8 + i + 1)
                diag = PS[i % 2][:, i * P:(i + 1) * P]
                dve.tensor_tensor(diag, diag, tri[:, :], ALU.add).then_inc(masked, 1)
                dve.wait_ge(masked, b8 + i + 1)
                m = nmx[:, i % 2:i % 2 + 1]
                dve.tensor_reduce(m, PS[i % 2][:, 0:(i + 1) * P], AX.X, ALU.max, negate=True).then_inc(max_found, 1)
                dve.wait_ge(max_found, b8 + i + 1)
                dve.tensor_scalar(m, m, GAMMA, None, ALU.mult).then_inc(max_ready, 1)

            with dve.Fori(0, B) as b:
                b8, b12, col = dve.snap(b * NJ), dve.snap(b * CUM), dve.snap(b * (NJ * D))
                maxima(b8, 0)
                for i in range(NJ):
                    if i + 1 < NJ:
                        maxima(b8, i + 1)
                    dve.wait_ge(exped, b8 + i + 1)
                    dve.reciprocal(rinv[:, i % 2:i % 2 + 1], rs[:, i % 2:i % 2 + 1]).then_inc(rinv_ready, 1)
                    for g in range(i // 4 + 1):
                        n = min(4, i + 1 - 4 * g)
                        dve.wait_ge(p_turned, b12 + cum(i) + g + 1)
                        if i >= 2:
                            dve.wait_ge(pv_mm, b8 + i - 1)
                        dve.tensor_copy(ET[:, i % 2, 4 * g:4 * g + n, :].rearrange("p n k -> p (n k)"), PT[g][:, 0:n * P])\
                           .then_inc(pt_copied, 1)
                    dve.wait_ge(pv_mm, b8 + i + 1)
                    dve.wait_ge(rinv_ready, b8 + i + 1)
                    dve.tensor_scalar(Yf[:, bass.ds(col + i * D, D)], PY[:, 0:D], rinv[:, i % 2:i % 2 + 1], None, ALU.mult)\
                       .then_inc(y_ready, 1)
            dve.wait_ge(y_ready, NBLK)
            norm_stats(dve, step, nb, ys, range(NBLK))
            norm_apply(dve, step, nb, ys, ys)
            step(dve.tensor_tensor(X2[:, :, :], X2[:, :, :], Y[:, :, :], ALU.add))


def stage_d(nc, sem, X3, Y, identf, gate, W1, b1, W2, b2, lower_dram, out_dram):
    B, T, D = out_dram.shape
    NE, _, FH = W1.shape
    TOPK = int(NE * 0.2)
    NBLK = B * T // P
    FG = 512
    NG = NBLK // 4
    NC = FH // P
    assert NE * NBLK == 512 and NC == 2 and NE % 2 == 0

    with ExitStack() as ctx:
        sb = lambda n, s, d=F32: ctx.enter_context(nc.sbuf_tensor("d_" + n, s, d))
        pb = lambda n: ctx.enter_context(nc.psum_tensor("d_" + n, [P, 512], F32))
        xT = sb("xT", [P, B * T])
        acc = sb("acc", [P, NBLK, D])
        wg = sb("wg", [P, NE])
        b1r = sb("b1r", [NE, FH])
        b1c = sb("b1c", [P, NC, NE])
        b2r = sb("b2r", [NE, D])
        lower = sb("lower", [P, NE, NE])
        w1 = sb("w1", [P, 2, FH])
        w2 = sb("w2", [P, 2, NC, D])
        G = sb("G", [P, NBLK, NE])
        GE = sb("GE", [P, NE, NBLK])
        mx = sb("mx", [P, NBLK])
        gs = sb("gs", [P, NBLK])
        ahead = sb("ahead", [P, 8, NE, NE])
        tie = sb("tie", [P, 8, NE, NE])
        rank = sb("rank", [P, NBLK, NE])
        gT = sb("gT", [NE, NBLK * P])
        HT = sb("HT", [P, 2, NC, FG])
        nb = NormBuffers(lambda n, s, d=F32: sb(n, s, d), NBLK)
        PT = [pb("PT0"), pb("PT1")]
        PH = [pb("PH%d" % k) for k in range(4)]
        PY = [pb("PY0"), pb("PY1")]

        c_in, w_in, out_done, dve_own = sem("d_c_in"), [sem("d_w_in0"), sem("d_w_in1")], sem("d_out_done"), sem("d_dve_own")
        xn_ready, turned, xT_ready, logits, shifted, gate_exped, g_ready, g_turned, gT_ready, bias_mm, acc_ready = (
            sem("d_xn_ready"), sem("d_turned"), sem("d_xT_ready"), sem("d_logits"), sem("d_shifted"), sem("d_gate_exped"),
            sem("d_g_ready"), sem("d_g_turned"), sem("d_gT_ready"), sem("d_bias_mm"), sem("d_acc_ready"))
        b1_turned, b1_ready = sem("d_b1_turned"), sem("d_b1_ready")
        up_mm, h_ready, down_mm, added, y_ready, sp_apart, act_apart = (
            sem("d_up_mm"), sem("d_h_ready"), sem("d_down_mm"), sem("d_added"), sem("d_y_ready"), sem("d_sp_apart"), sem("d_act_apart"))
        block = ctx.enter_context(nc.Block())
        EG = 2 * NG

        @block.sync
        def _(sp):
            sp.dma_start(wg[:, :], gate).then_inc(c_in, 16)
            sp.dma_start(b1r[:, :], b1).then_inc(c_in, 16)
            sp.dma_start(b2r[:, :], b2).then_inc(c_in, 16)
            sp.dma_start(lower[:, :, :], lower_dram.partition_broadcast(P)).then_inc(c_in, 16)
            with sp.Fori(0, NE // 2) as i:
                for a in range(2):
                    sp.wait_ge(down_mm, sp.snap(i * EG + a * NG))
                    sp.sem_inc(sp_apart, 1)
                    sp.dma_start(w1[:, a, :], W1[bass.ds(2 * i + a, 1)].rearrange("e p n -> p (e n)")).then_inc(w_in[a], 16)
                    sp.dma_start(w2[:, a, :, :], W2[bass.ds(2 * i + a, 1)].rearrange("e (c p) d -> p (e c) d", p=P)).then_inc(w_in[a], 16)
            sp.wait_ge(y_ready, 1)
            sp.dma_start(out_dram.rearrange("b (j p) d -> p (b j) d", p=P), X3[:, :, :]).then_inc(out_done, 16)
            sp.wait_ge(out_done, 16)

        @block.tensor
        def _(pe):
            pe.sem_inc(down_mm, NG)
            pe.wait_ge(xn_ready, 1)
            for g in range(NG):
                if g >= 2:
                    pe.wait_ge(xT_ready, g - 1)
                for u in range(4):
                    ins = pe.transpose(PT[g % 2][:, u * P:(u + 1) * P], Y[:, 4 * g + u, :], identf[:, :])
                ins.then_inc(turned, 1)
            pe.wait_ge(c_in, 64)
            for c in range(NC):
                ins = pe.transpose(PH[0][:, c * NE:(c + 1) * NE], b1r[:, c * P:(c + 1) * P], identf[0:NE, 0:NE])
            ins.then_inc(b1_turned, 1)
            pe.wait_ge(xT_ready, NG)
            for n in range(NBLK):
                ins = pe.matmul(PY[0][:, n * NE:(n + 1) * NE], xT[:, n * P:(n + 1) * P], wg[:, :], start=True, stop=True)
            ins.then_inc(logits, 1)
            pe.wait_ge(g_ready, 1)
            for g in range(NG):
                if g >= 2:
                    pe.wait_ge(gT_ready, g - 1)
                for u in range(4):
                    ins = pe.transpose(PT[g % 2][0:NE, u * P:(u + 1) * P], G[:, 4 * g + u, :], identf[:, :])
                ins.then_inc(g_turned, 1)
            for g in range(NG):
                pe.wait_ge(gT_ready, g + 1)
                if g >= 2:
                    pe.wait_ge(acc_ready, g - 1)
                for u in range(4):
                    ins = pe.matmul(PY[g % 2][:, u * P:(u + 1) * P], gT[:, (4 * g + u) * P:(4 * g + u + 1) * P], b2r[:, :],
                                    start=True, stop=True)
                ins.then_inc(bias_mm, 1)
            pe.wait_ge(acc_ready, NG)

            def up(t2, w32, k):
                a, g = k // NG, k % NG
                if g == 0:
                    pe.wait_ge(w_in[a], w32)
                for c in range(NC):
                    pe.wait_ge(h_ready, t2 + 2 * k + c + 1)
                    pe.matmul(PH[2 * (k % 2) + c][:, :], w1[:, a, c * P:(c + 1) * P], xT[:, g * FG:(g + 1) * FG],
                              start=True, stop=True).then_inc(up_mm, 1)

            def down(t, t2, k):
                a = k // NG
                pe.wait_ge(h_ready, t2 + 2 * k + 6)
                pe.wait_ge(added, t + k + NG - 1)
                for u in range(4):
                    for c in range(NC):
                        ins = pe.matmul(PY[k % 2][:, u * P:(u + 1) * P], HT[:, k % 2, c, u * P:(u + 1) * P], w2[:, a, c, :],
                                        start=(c == 0), stop=(c == NC - 1))
                ins.then_inc(down_mm, 1)

            with pe.Fori(0, NE // 2) as i:
                t, t2, w32 = pe.snap(i * EG), pe.snap(i * (2 * EG)), pe.snap(i * 32 + 32)
                up(t2, w32, 0)
                for k in range(EG):
                    if k + 1 < EG:
                        up(t2, w32, k + 1)
                    down(t, t2, k)

        @block.scalar
        def _(act):
            for g in range(NG):
                act.wait_ge(turned, g + 1)
                act.copy(xT[:, g * FG:(g + 1) * FG], PT[g % 2][:, :]).then_inc(xT_ready, 1)
            act.wait_ge(b1_turned, 1)
            act.copy(b1c[:, :, :].rearrange("p c e -> p (c e)"), PH[0][:, 0:NC * NE]).then_inc(b1_ready, 1)
            act.wait_ge(shifted, 1)
            act.activation(G[:, :, :], G[:, :, :], ACT.Exp).then_inc(gate_exped, 1)
            for g in range(NG):
                act.wait_ge(g_turned, g + 1)
                act.copy(gT[:, g * FG:(g + 1) * FG], PT[g % 2][0:NE, :]).then_inc(gT_ready, 1)
            for g in range(NG):
                act.wait_ge(bias_mm, g + 1)
                act.copy(acc[:, 4 * g:4 * g + 4, :].rearrange("p n d -> p (n d)"), PY[g % 2][:, :]).then_inc(acc_ready, 1)
            act.sem_inc(h_ready, 4)
            b1f = b1c[:, :, :].rearrange("p c e -> p (c e)")
            act.wait_ge(b1_ready, 1)
            with act.Fori(0, NE // 2) as i:
                t, t2, e0 = act.snap(i * EG), act.snap(i * (2 * EG)), act.snap(i * 2)
                for k in range(EG):
                    act.wait_ge(down_mm, t + k + NG - 1)
                    for c in range(NC):
                        act.wait_ge(up_mm, t2 + 2 * k + c + 1)
                        act.sem_inc(act_apart, 1)
                        act.activation(HT[:, k % 2, c, :], PH[2 * (k % 2) + c][:, :], ACT.Relu,
                                       bias=b1f[:, bass.ds(e0 + c * NE + k // NG, 1)]).then_inc(h_ready, 1)

        @block.vector
        def _(dve):
            step = Steps(dve, dve_own)
            xs, ys, accs = (lambda q: X3[:, q, :]), (lambda q: Y[:, q, :]), (lambda q: acc[:, q, :])
            norm_stats(dve, step, nb, xs, range(NBLK))
            norm_apply(dve, step, nb, xs, ys)
            dve.sem_inc(xn_ready, 1)
            dve.wait_ge(logits, 1)
            lg = PY[0][:, :].rearrange("p (n e) -> p n e", e=NE)
            over_e = lambda x: x.unsqueeze(2).broadcast_to([P, NBLK, NE])
            step(dve.tensor_reduce(mx[:, :], lg, AX.X, ALU.max))
            dve.tensor_tensor(G[:, :, :], lg, over_e(mx[:, :]), ALU.subtract).then_inc(shifted, 1)
            dve.wait_ge(gate_exped, 1)
            step(dve.tensor_reduce(gs[:, :], G[:, :, :], AX.X, ALU.add))
            step(dve.reciprocal(gs[:, :], gs[:, :]))
            step(dve.tensor_tensor(G[:, :, :], G[:, :, :], over_e(gs[:, :]), ALU.mult))
            dve.wait_ge(c_in, 64)
            for n in range(0, NBLK, 8):
                g = G[:, n:n + 8, :]
                other, this = g.unsqueeze(2).broadcast_to([P, 8, NE, NE]), g.unsqueeze(3).broadcast_to([P, 8, NE, NE])
                step(dve.tensor_tensor(ahead[:, :, :, :], other, this, ALU.is_gt))
                step(dve.tensor_tensor(tie[:, :, :, :], other, this, ALU.is_equal))
                step(dve.tensor_tensor(tie[:, :, :, :], tie[:, :, :, :], lower[:, :, :].unsqueeze(1).broadcast_to([P, 8, NE, NE]), ALU.mult))
                step(dve.tensor_tensor(ahead[:, :, :, :], ahead[:, :, :, :], tie[:, :, :, :], ALU.add))
                step(dve.tensor_reduce(rank[:, n:n + 8, :], ahead[:, :, :, :], AX.X, ALU.add))
            step(dve.tensor_scalar(rank[:, :, :], rank[:, :, :], TOPK - 0.5, None, ALU.is_lt))
            step(dve.tensor_tensor(G[:, :, :], G[:, :, :], rank[:, :, :], ALU.mult))
            step(dve.tensor_reduce(gs[:, :], G[:, :, :], AX.X, ALU.add))
            step(dve.tensor_scalar(gs[:, :], gs[:, :], 1e-12, None, ALU.max))
            step(dve.reciprocal(gs[:, :], gs[:, :]))
            step(dve.tensor_tensor(G[:, :, :], G[:, :, :], over_e(gs[:, :]), ALU.mult))
            step(dve.tensor_copy(GE[:, :, :], G[:, :, :].rearrange("p n e -> p e n")))
            dve.sem_inc(g_ready, 1)
            dve.wait_ge(acc_ready, NG)
            dve.sem_inc(added, NG)
            GEf = GE[:, :, :].rearrange("p e n -> p (e n)")
            with dve.Fori(0, NE // 2) as i:
                t, e0 = dve.snap(i * EG), dve.snap(i * (2 * NBLK))
                for k in range(EG):
                    a, g = k // NG, k % NG
                    dve.wait_ge(added, t + k + 1)
                    dve.wait_ge(down_mm, t + k + NG + 1)
                    for u in range(4):
                        n = 4 * g + u
                        ins = dve.scalar_tensor_tensor(acc[:, n, :], PY[k % 2][:, u * P:(u + 1) * P],
                                                       GEf[:, bass.ds(e0 + a * NBLK + n, 1)], acc[:, n, :], ALU.mult, ALU.add)
                    ins.then_inc(added, 1)
            dve.wait_ge(added, NG + NE * NG)
            norm_stats(dve, step, nb, accs, range(NBLK))
            norm_apply(dve, step, nb, accs, ys)
            step(dve.tensor_tensor(X3[:, :, :], X3[:, :, :], Y[:, :, :], ALU.add))
            dve.sem_inc(y_ready, 1)


def sandwich(nc, x, Wv, Wo, Wg, Wb, Wqkv, q_scale, k_scale, Wo2, ln_g, ln_b, W1, b1, W2, b2,
             w_q, w_k, w_v, gate, EW1, Eb1, EW2, Eb2, ident, rot, mask, quad, tri, lower, out):
    B, T, D = x.shape
    NBLK = B * T // P
    H = Wg.shape[0]
    NC = P // B
    x1_dram = nc.dram_tensor("x1", [B, T, D], F32, kind="Internal").ap()
    z_dram = nc.dram_tensor("chunk_maps", [B, NC, H, 2 * (D // H) ** 2], F32, kind="Internal").ap()
    s_dram = nc.dram_tensor("chunk_states", [B, NC, H, (D // H) ** 2], F32, kind="Internal").ap()
    with ExitStack() as ctx:
        sem = lambda n: ctx.enter_context(nc.semaphore(n))
        XA = ctx.enter_context(nc.sbuf_tensor("XA", [P, B, T + 1], F32))
        identf = ctx.enter_context(nc.sbuf_tensor("identf", [P, P], F32))
        ident_in = sem("ident_in")
        with nc.Block() as block:
            @block.sync
            def _(sp):
                sp.dma_start(identf[:, :], ident).then_inc(ident_in, 16)
                sp.wait_ge(ident_in, 16)
        stage_a(nc, sem, XA, identf, x, Wv, Wg, Wb, Wo, x1_dram, z_dram, s_dram)
        stage_b(nc, sem, XA, identf, Wqkv, q_scale, k_scale, Wo2, ln_g, ln_b, W1, b1, W2, b2, rot, mask, quad)
        X2 = ctx.enter_context(nc.sbuf_tensor("X2", [P, NBLK, D], F32))
        Y = ctx.enter_context(nc.sbuf_tensor("Y", [P, NBLK, D], F32))
        stage_c(nc, sem, XA, X2, Y, identf, x1_dram, w_q, w_k, w_v, tri)
        stage_d(nc, sem, X2, Y, identf, gate, EW1, Eb1, EW2, Eb2, lower, out)


def constants(T, dh, window, experts):
    import numpy as np
    f = np.float32
    half = np.arange(0, dh, 2, dtype=f)
    inv_freq = (1.0 / 10000.0 ** (half / dh)).astype(f)
    t = np.arange(T, dtype=f)
    freqs = t[:, None] * inv_freq[None]
    freqs = np.concatenate([freqs, freqs], -1).astype(f)
    base = ((half + 0.4 * dh) / (1.4 * dh)).astype(f)
    power = ((t - T // 2) / (window // 2)).astype(f)
    scale = base[None] ** power[:, None]
    scale = np.concatenate([scale, scale], -1).astype(f)
    sign = np.where(np.arange(dh) < dh // 2, -1, 1).astype(f)
    cos, sin = np.cos(freqs), np.sin(freqs) * sign
    qk_scale = 8.0
    tab = np.stack([qk_scale * cos * scale, qk_scale * sin * scale, cos / scale, sin / scale], 1).astype(f)
    rot = np.ascontiguousarray(tab.reshape(T // P, P, 4, dh).transpose(1, 0, 2, 3))
    q, k = np.arange(P)[:, None], np.arange(P + window)[None] - window
    w0 = (q // window) * window
    ok = (k >= w0 - window) & (k < w0 + window) & (k <= q) & (k >= q - window)
    hidden = -1e25
    mask = np.stack([np.where(ok, 0, hidden), np.where(ok & (k >= 0), 0, hidden)], 1).astype(f)
    return {
        "ident": np.eye(P, dtype=f),
        "rot": rot,
        "mask": np.ascontiguousarray(mask),
        "quad": np.kron(np.eye(4), np.ones((window, 1))).astype(f),
        "tri": np.where(np.arange(P)[:, None] >= np.arange(P)[None], 0, -1e38).astype(f),
        "lower": (np.arange(experts)[:, None] > np.arange(experts)[None]).astype(f),
    }


_INS = ["L0_attn_x", "L0_attn_Wv", "L0_attn_Wo", "L0_attn_Wg", "L0_attn_Wb", "L0_ffn_Wqkv", "L0_ffn_q_scale",
        "L0_ffn_k_scale", "L0_ffn_Wo", "L0_ffn_ln_g", "L0_ffn_ln_b", "L0_ffn_W1", "L0_ffn_b1", "L0_ffn_W2", "L0_ffn_b2",
        "L1_attn_w_q", "L1_attn_w_k", "L1_attn_w_v", "L1_ffn_gate", "L1_ffn_W1", "L1_ffn_b1", "L1_ffn_W2", "L1_ffn_b2"]


def kernel(**inputs):
    import numpy as _np
    import concourse.bacc as _bacc
    from concourse.bass_utils import run_bass_kernel_spmd as _run

    nc = _bacc.Bacc("TRN2", target_bir_lowering=False, num_devices=1)
    arrays, args = {}, []
    data = [(name, _np.ascontiguousarray(inputs[name])) for name in _INS]
    shape = inputs["L0_attn_x"].shape
    data += constants(shape[1], inputs["L0_ffn_q_scale"].shape[1], 32, inputs["L1_ffn_gate"].shape[1]).items()
    for name, a in data:
        arrays[f"in_{name}_dram"] = a
        args.append(nc.dram_tensor(f"in_{name}_dram", a.shape, F32, kind="ExternalInput").ap())
    args.append(nc.dram_tensor("out_0_dram", shape, F32, kind="ExternalOutput").ap())
    sandwich(nc, *args)
    r = _run(nc, [arrays], core_ids=[0])
    return r.results[0]["out_0_dram"]
```

```python
import concourse.bass as bass
from concourse import mybir
from contextlib import ExitStack
F32 = mybir.dt.float32
I32 = mybir.dt.int32
ALU = mybir.AluOpType
ACT = mybir.ActivationFunctionType
AX = mybir.AxisListType
P = 128
RSQRT_MAGIC = float(0x5F3759DF)
NEWTON = 3
LOWEST = -3.4028235e38
LN_EPS = 1e-5


def rsqrt_on_dve(v, link, x, y, bits, half, guard=None, bias=None):
    if guard is not None:
        link(v.tensor_scalar(x, x, guard, None, ALU.max))
    else:
        link(v.tensor_scalar(x, x, bias, None, ALU.add))
    link(v.tensor_scalar(bits, x.bitcast(I32), 1, None, ALU.arith_shift_right))
    link(v.tensor_scalar(y.bitcast(I32), bits, -1.0, RSQRT_MAGIC, ALU.mult, ALU.add))
    for _ in range(NEWTON):
        link(v.scalar_tensor_tensor(half, y, -0.5, x, ALU.mult, ALU.mult))
        link(v.tensor_tensor(half, half, y, ALU.mult))
        link(v.scalar_tensor_tensor(y, half, 1.5, y, ALU.add, ALU.mult))


class Steps:

    def __init__(self, eng, own, base=0):
        self.eng, self.own, self.base, self.n = eng, own, base, 0

    def __call__(self, ins):
        ins.then_inc(self.own, 1)
        self.n += 1
        self.eng.wait_ge(self.own, self.base + self.n)


class NormBuffers:

    def __init__(self, sb, n):
        self.n = n
        self.st = sb("ln_st", [P, n, 6])
        self.mv = sb("ln_mv", [P, n, 2])
        self.var = sb("ln_var", [P, n])
        self.rstd = sb("ln_rstd", [P, n])
        self.bits = sb("ln_bits", [P, n], I32)
        self.half = sb("ln_half", [P, n])


def norm_stats(dve, step, nb, src, rows):
    for q in rows:
        ins = dve.bn_stats(nb.st[:, q, :], src(q))
    step(ins)


def norm_apply(dve, step, nb, src, dst, lo=0, n=None):
    n = nb.n if n is None else n
    for q in range(lo, lo + n):
        ins = dve.bn_aggr(nb.mv[:, q, :], nb.st[:, q, :])
    step(ins)
    r = slice(lo, lo + n)
    step(dve.tensor_copy(nb.var[:, r], nb.mv[:, r, 1]))
    rsqrt_on_dve(dve, step, nb.var[:, r], nb.rstd[:, r], nb.bits[:, r], nb.half[:, r], bias=LN_EPS)
    for q in range(lo, lo + n):
        ins = dve.tensor_scalar(dst(q), src(q), nb.mv[:, q, 0:1], nb.rstd[:, q:q + 1], ALU.subtract, ALU.mult)
    step(ins)


def stage_a(nc, sem, XA, identf, x_dram, Wv, Wg, Wb, Wo, x1_dram, z_dram, s_dram):
    B, T, D = x_dram.shape
    H = Wg.shape[0]
    DK = D // H
    NC = P // B
    L = T // NC
    HZ = 2 * DK
    NW = D + 2 * H
    HALF = 64
    DVE_HEADS, POOL_HEADS = (0, 11), (11, 16)
    UN = 4
    assert H == 16 and L % UN == 0

    with ExitStack() as ctx:
        sb = lambda n, s, d=F32: ctx.enter_context(nc.sbuf_tensor("a_" + n, s, d))
        pb = lambda n: ctx.enter_context(nc.psum_tensor("a_" + n, [P, 512], F32))
        X = sb("X", [P, L, D])
        xn = sb("xn", [P, L, D])
        R = sb("R", [P, L + 1, D])
        V = sb("V", [P, L, D])
        O = sb("O", [P, L, D])
        GB = sb("GB", [P, L, 2 * H])
        nbeta = sb("nbeta", [P, L, H])
        PH = sb("PH", [P, L + 1, H, HZ])
        Z = sb("Z", [P, H, DK, HZ])
        tmp = sb("tmp", [P, H, DK, HZ])
        tree = sb("tree", [P, H, DK // 2, HZ])
        E = sb("E", [P, H, HZ])
        ss = sb("ss", [P, L * H])
        rn = sb("rn", [P, L * H])
        bits = sb("bits", [P, L * H], I32)
        half = sb("half", [P, L * H])
        ZS = sb("ZS", [B * H, NC, DK, HZ])
        SI = sb("SI", [B * H, NC, DK, DK])
        stmp = sb("stmp", [B * H, DK, DK, DK])
        S0 = sb("S0", [P, H, DK, DK])
        xT = sb("xT", [P, 2, 4, P])
        wv = sb("wv", [P, D])
        wgb = sb("wgb", [2 * H, D])
        wo = sb("wo", [P, D])
        wT = sb("wT", [P, NW + D])
        nb = NormBuffers(sb, L)
        PT = [pb("PT0"), pb("PT1")]
        PV = [pb("PV%d" % k) for k in range(4)]

        x_in, w_in, prev_in, z_out, zs_in, s_out, s0_in, x1_out = (
            sem("a_x_in"), sem("a_w_in"), sem("a_prev_in"), sem("a_z_out"), sem("a_zs_in"), sem("a_s_out"),
            sem("a_s0_in"), sem("a_x1_out"))
        dve_own, pool_own, dve_run, pool_run = sem("a_dve_own"), sem("a_pool_own"), sem("a_dve_run"), sem("a_pool_run")
        pool_apart = sem("a_pool_apart")
        normed, r_ready, w_turned, wT_ready, turned, xT_ready, projected, v_ready, gb_ready = (
            sem("a_normed"), sem("a_r_ready"), sem("a_w_turned"), sem("a_wT_ready"), sem("a_turned"),
            sem("a_xT_ready"), sem("a_projected"), sem("a_v_ready"), sem("a_gb_ready"))
        bv_ready, z_ready, scanned, o_dve, o_pool, x1_ready, xn1_ready, xa_ready = (
            sem("a_bv_ready"), sem("a_z_ready"), sem("a_scanned"), sem("a_o_dve"), sem("a_o_pool"), sem("a_x1_ready"),
            sem("a_xn1_ready"), sem("a_xa_ready"))
        block = ctx.enter_context(nc.Block())
        NG = L // 4

        Rf = R[:, :, :].rearrange("p l d -> p (l d)")
        PHf = PH[:, :, :, :].rearrange("p l h c -> p (l h c)")
        Vf = V[:, :, :].rearrange("p l d -> p (l d)")
        nbf = nbeta[:, :, :].rearrange("p l h -> p (l h)")

        def apart(eng, on_pool):
            if on_pool:
                eng.sem_inc(pool_apart, 1)

        def state_read(eng, step, heads, i, on_pool):
            a, b = heads
            n = b - a
            w = Rf[:, bass.ds(i * D + a * DK, n * DK)].rearrange("p (h k) -> p h k", k=DK)
            apart(eng, on_pool)
            step(eng.tensor_tensor(tmp[:, a:b], Z[:, a:b], w.unsqueeze(3).broadcast_to([P, n, DK, HZ]), ALU.mult))
            out = PHf[:, bass.ds(i * (H * HZ) + a * HZ, n * HZ)].rearrange("p (h c) -> p h c", c=HZ)
            if on_pool:
                step(eng.tensor_tensor(tree[:, a:b], tmp[:, a:b, 0:4], tmp[:, a:b, 4:8], ALU.add))
                step(eng.tensor_tensor(tree[:, a:b, 0:2], tree[:, a:b, 0:2], tree[:, a:b, 2:4], ALU.add))
                apart(eng, on_pool)
                step(eng.tensor_tensor(out, tree[:, a:b, 0], tree[:, a:b, 1], ALU.add))
            else:
                step(eng.tensor_reduce(out, tmp[:, a:b].rearrange("p h k c -> p h c k"), AX.X, ALU.add))

        def state_step(eng, step, heads, i, on_pool):
            a, b = heads
            n = b - a
            state_read(eng, step, heads, i, on_pool)
            w = Rf[:, bass.ds(i * D + a * DK, n * DK)].rearrange("p (h k) -> p h k", k=DK)
            rd = PHf[:, bass.ds(i * (H * HZ) + a * HZ, n * HZ)].rearrange("p (h c) -> p h c", c=HZ)
            nbi = nbf[:, bass.ds(i * H + a, n)]
            bv = Vf[:, bass.ds(i * D + a * DK, n * DK)].rearrange("p (h k) -> p h k", k=DK)
            apart(eng, on_pool)
            step(eng.tensor_tensor(E[:, a:b], rd, nbi.unsqueeze(2).broadcast_to([P, n, HZ]), ALU.mult))
            apart(eng, on_pool)
            step(eng.tensor_tensor(E[:, a:b, DK:HZ], E[:, a:b, DK:HZ], bv, ALU.add))
            apart(eng, on_pool)
            step(eng.tensor_tensor(tmp[:, a:b], w.unsqueeze(3).broadcast_to([P, n, DK, HZ]),
                                   E[:, a:b].unsqueeze(2).broadcast_to([P, n, DK, HZ]), ALU.mult))
            step(eng.tensor_tensor(Z[:, a:b], Z[:, a:b], tmp[:, a:b], ALU.add))

        def recurrence(eng, own, heads, on_pool):
            per = 8 if on_pool else 6
            with eng.Fori(0, L // UN) as t:
                base = eng.snap(t * (UN * per))
                i0 = eng.snap(t * UN)
                step = Steps(eng, own, base)
                for u in range(UN):
                    state_step(eng, step, heads, i0 + u, on_pool)
                assert step.n == UN * per
            step = Steps(eng, own, L * per)
            state_read(eng, step, heads, L, on_pool)
            eng.sem_inc(z_ready, 1)
            return step

        def outputs(eng, step, heads, on_pool):
            a, b = heads
            n = b - a
            flat = tmp[:, :, :, :].rearrange("p h k c -> p (h k c)")
            for u in range(L):
                m = 64 * n
                x = flat[:, a * P + (u % 2) * m:a * P + (u % 2 + 1) * m].rearrange("p (h j k) -> p h j k", j=DK, k=DK)
                step(eng.tensor_tensor(x, PH[:, u + 1, a:b, 0:DK].unsqueeze(2).broadcast_to([P, n, DK, DK]),
                                       S0[:, a:b].rearrange("p h k j -> p h j k"), ALU.mult))
                out = O[:, u, a * DK:b * DK].rearrange("p (h j) -> p h j", j=DK)
                if on_pool:
                    step(eng.tensor_tensor(x[:, :, :, 0:4], x[:, :, :, 0:4], x[:, :, :, 4:8], ALU.add))
                    step(eng.tensor_tensor(x[:, :, :, 0:2], x[:, :, :, 0:2], x[:, :, :, 2:4], ALU.add))
                    step(eng.tensor_tensor(out, x[:, :, :, 0], x[:, :, :, 1], ALU.add))
                else:
                    step(eng.tensor_reduce(out, x, AX.X, ALU.add))
                if u % 4 == 3:
                    o = O[:, u - 3:u + 1, a * DK:b * DK].rearrange("p l (h j) -> p l h j", j=DK)
                    step(eng.tensor_tensor(o, o, PH[:, u - 2:u + 2, a:b, DK:HZ], ALU.add))
                    step(eng.tensor_tensor(o, o, GB[:, u - 3:u + 1, a:b].unsqueeze(3).broadcast_to([P, 4, n, DK]), ALU.mult))
                    eng.sem_inc(o_pool if on_pool else o_dve, 1)

        @block.sync
        def _(sp):
            sp.dma_start(X[:, :, :], x_dram.rearrange("b (c i) d -> (b c) i d", i=L)).then_inc(x_in, 16)
            sp.dma_start(wv[:, :], Wv).then_inc(w_in, 16)
            sp.dma_start(wgb[0:H, :], Wg).then_inc(w_in, 16)
            sp.dma_start(wgb[H:2 * H, :], Wb).then_inc(w_in, 16)
            sp.dma_start(wo[:, :], Wo).then_inc(w_in, 16)
            sp.wait_ge(r_ready, 2)
            for b in range(B):
                sp.dma_start(R[b * NC + 1:(b + 1) * NC, 0, :], R[b * NC:(b + 1) * NC - 1, L, :]).then_inc(prev_in, 16)
            sp.wait_ge(z_ready, 2)
            sp.dma_start(z_dram.rearrange("b c h x -> (b c) (h x)"), Z[:, :, :, :].rearrange("p h k c -> p (h k c)"))\
              .then_inc(z_out, 16)
            sp.wait_ge(z_out, 16)
            for b in range(B):
                sp.dma_start(ZS[b * H:(b + 1) * H].rearrange("p c k z -> p c (k z)"),
                             z_dram[b].rearrange("c h x -> h c x")).then_inc(zs_in, 16)
            sp.wait_ge(scanned, 1)
            for b in range(B):
                sp.dma_start(s_dram[b].rearrange("c h x -> h c x"),
                             SI[b * H:(b + 1) * H].rearrange("p c k j -> p c (k j)")).then_inc(s_out, 16)
            sp.wait_ge(s_out, 16 * B)
            sp.dma_start(S0[:, :, :, :].rearrange("p h k j -> p (h k j)"), s_dram.rearrange("b c h x -> (b c) (h x)"))\
              .then_inc(s0_in, 16)
            sp.wait_ge(x1_ready, 1)
            sp.dma_start(x1_dram.rearrange("b (c i) d -> (b c) i d", i=L), X[:, :, :]).then_inc(x1_out, 16)
            sp.wait_ge(x1_out, 16)

        @block.gpsimd
        def _(pool):
            pool.memset(R[:, 0, :], 0.0).then_inc(r_ready, 1)
            step = Steps(pool, pool_own)
            pool.memset(XA[:, :, 0:1], 0.0)
            step(pool.memset(Z[:, :, :, :], 0.0))
            Zf = Z[:, :, :, :].rearrange("p h k c -> p h (k c)")
            pool.memset(Zf[:, :, 0:(DK - 1) * (HZ + 1) + 1:HZ + 1], 1.0).then_inc(bv_ready, 1)
            for g in range(NG):
                pool.wait_ge(gb_ready, 2 * g + 2)
                r = slice(4 * g, 4 * g + 4)
                v = V[:, r, :].rearrange("p l (h k) -> p l h k", k=DK)
                pool.tensor_tensor(v, v, GB[:, r, H:2 * H].unsqueeze(3).broadcast_to([P, 4, H, DK]), ALU.mult).then_inc(bv_ready, 1)
            pool.wait_ge(prev_in, 16 * B)
            pool.wait_ge(bv_ready, NG + 2)
            step = recurrence(pool, pool_run, POOL_HEADS, True)
            pool.wait_ge(s0_in, 16)
            outputs(pool, step, POOL_HEADS, True)

        @block.tensor
        def _(pe):
            pe.wait_ge(w_in, 64)
            pe.transpose(PT[0][:, 0:D], wv[:, :], identf[:, :])
            pe.transpose(PT[0][:, D:NW], wgb[:, :], identf[0:2 * H, 0:2 * H])
            pe.transpose(PT[0][:, NW:NW + D], wo[:, :], identf[:, :]).then_inc(w_turned, 1)
            pe.wait_ge(wT_ready, 1)

            def turn(src, g, k):
                for u in range(4):
                    ins = pe.transpose(PT[k % 2][:, u * P:(u + 1) * P], src[:, 4 * g + u, :], identf[:, :])
                ins.then_inc(turned, 1)

            def project(g):
                pe.wait_ge(xT_ready, g + 1)
                for u in range(4):
                    if g >= 2 and u % 2 == 0:
                        pe.wait_ge(gb_ready, 2 * (g - 2) + u // 2 + 1)
                    bank = PV[2 * (g % 2) + u // 2]
                    ins = pe.matmul(bank[:, (u % 2) * NW:(u % 2 + 1) * NW], xT[:, g % 2, u, :], wT[:, 0:NW], start=True, stop=True)
                    if u % 2 == 1:
                        ins.then_inc(projected, 1)

            pe.wait_ge(normed, 1)
            for g in range(NG):
                if g >= 2:
                    pe.wait_ge(xT_ready, g - 1)
                turn(xn, g, g)
                if g >= 1:
                    project(g - 1)
            project(NG - 1)
            for g in range(NG):
                pe.wait_ge(o_dve, g + 1)
                pe.wait_ge(o_pool, g + 1)
                if g >= 2:
                    pe.wait_ge(xT_ready, NG + g - 1)
                turn(O, g, g)
                pe.wait_ge(xT_ready, NG + g + 1)
                if g >= 2:
                    pe.wait_ge(v_ready, NG * 2 + g - 1)
                for u in range(4):
                    ins = pe.matmul(PV[g % 2][:, u * P:(u + 1) * P], xT[:, g % 2, u, :], wT[:, NW:NW + D], start=True, stop=True)
                ins.then_inc(projected, 1)
            pe.wait_ge(xn1_ready, 1)
            for g in range(NG):
                if g >= 2:
                    pe.wait_ge(xa_ready, g - 1)
                turn(xn, g, g)

        @block.scalar
        def _(act):
            act.wait_ge(w_turned, 1)
            act.copy(wT[:, :], PT[0][:, 0:NW + D]).then_inc(wT_ready, 1)

            def copy_turned(k, g):
                act.wait_ge(turned, k * NG + g + 1)
                if k * NG + g >= 2:
                    act.wait_ge(projected, 2 * min(g - 1, NG) if k == 0 else 2 * NG + max(0, g - 1))
                act.copy(xT[:, g % 2, :, :].rearrange("p u t -> p (u t)"), PT[g % 2][:, :]).then_inc(xT_ready, 1)

            def copy_projected(g):
                for a in range(2):
                    act.wait_ge(projected, 2 * g + a + 1)
                    x = PV[2 * (g % 2) + a][:, 0:2 * NW].rearrange("p (u n) -> p u n", n=NW)
                    r = slice(4 * g + 2 * a, 4 * g + 2 * a + 2)
                    act.copy(V[:, r, :], x[:, :, 0:D]).then_inc(v_ready, 1)
                    act.activation(GB[:, r, :], x[:, :, D:NW], ACT.Sigmoid).then_inc(gb_ready, 1)

            for g in range(NG):
                copy_turned(0, g)
                if g >= 1:
                    copy_projected(g - 1)
            copy_projected(NG - 1)
            for g in range(NG):
                copy_turned(1, g)
                act.wait_ge(projected, 2 * NG + g + 1)
                act.copy(V[:, 4 * g:4 * g + 4, :].rearrange("p l d -> p (l d)"), PV[g % 2][:, :]).then_inc(v_ready, 1)
            for g in range(NG):
                act.wait_ge(turned, 2 * NG + g + 1)
                x = PT[g % 2][:, :].rearrange("p (u b c) -> p u b c", u=4, b=B)
                for a in range(2):
                    r = slice(HALF * a, HALF * a + HALF)
                    for u in range(4):
                        s = 4 * g + u + a
                        ins = act.copy(XA[r, :, s:s + (NC - 1) * L + 1:L], x[r, u])
                ins.then_inc(xa_ready, 1)

        @block.vector
        def _(dve):
            step = Steps(dve, dve_own)
            dve.wait_ge(x_in, 16)
            xs, xns = (lambda q: X[:, q, :]), (lambda q: xn[:, q, :])
            norm_stats(dve, step, nb, xs, range(L))
            norm_apply(dve, step, nb, xs, xns)
            dve.sem_inc(normed, 1)
            flat = lambda t: t[:, :, :].rearrange("p l d -> p (l d)")
            step(dve.tensor_tensor(flat(O), flat(xn), flat(xn), ALU.mult))
            step(dve.tensor_reduce(ss[:, :], flat(O).rearrange("p (n k) -> p n k", k=DK), AX.X, ALU.add))
            rsqrt_on_dve(dve, step, ss[:, :], rn[:, :], bits[:, :], half[:, :], guard=1e-24)
            dve.tensor_tensor(Rf[:, D:(L + 1) * D].rearrange("p (n k) -> p n k", k=DK), flat(xn).rearrange("p (n k) -> p n k", k=DK),
                              rn[:, :].unsqueeze(2).broadcast_to([P, L * H, DK]), ALU.mult).then_inc(r_ready, 1)
            dve.wait_ge(gb_ready, 2 * NG)
            dve.tensor_scalar(nbeta[:, :, :], GB[:, :, H:2 * H], -1.0, None, ALU.mult).then_inc(bv_ready, 1)
            dve.wait_ge(prev_in, 16 * B)
            dve.wait_ge(bv_ready, NG + 2)
            recurrence(dve, dve_run, DVE_HEADS, False)
            dve.wait_ge(zs_in, 16 * B)
            step(dve.memset(SI[:, 0], 0.0))
            step(dve.tensor_copy(SI[:, 1], ZS[:, 0, :, DK:HZ]))
            BH = B * H
            for c in range(1, NC - 1):
                step(dve.tensor_tensor(stmp[:, :, :, :], ZS[:, c, :, 0:DK].unsqueeze(2).broadcast_to([BH, DK, DK, DK]),
                                       SI[:, c].rearrange("p m j -> p j m").unsqueeze(1).broadcast_to([BH, DK, DK, DK]), ALU.mult))
                step(dve.tensor_reduce(SI[:, c + 1], stmp[:, :, :, :], AX.X, ALU.add))
                step(dve.tensor_tensor(SI[:, c + 1], SI[:, c + 1], ZS[:, c, :, DK:HZ], ALU.add))
            dve.sem_inc(scanned, 1)
            dve.wait_ge(s0_in, 16)
            outputs(dve, step, DVE_HEADS, False)
            vs = lambda q: V[:, q, :]
            for g in range(NG):
                dve.wait_ge(v_ready, 2 * NG + g + 1)
                norm_stats(dve, step, nb, vs, range(4 * g, 4 * g + 4))
            norm_apply(dve, step, nb, vs, vs)
            step(dve.tensor_tensor(flat(X), flat(X), flat(V), ALU.add))
            dve.sem_inc(x1_ready, 1)
            norm_stats(dve, step, nb, xs, range(L))
            norm_apply(dve, step, nb, xs, xns)
            dve.sem_inc(xn1_ready, 1)


def stage_b(nc, sem_of, XA, identf, Wqkv, q_scale, k_scale, Wo, ln_g, ln_b, W1, b1, W2, b2, rot_dram, mask_dram, quad_dram):
    DEPTH, D, QKV = Wqkv.shape
    INNER = QKV // 3
    DH = q_scale.shape[1]
    H = INNER // DH
    FI = W2.shape[1]
    NB, T1 = XA.shape[1], XA.shape[2]
    T = T1 - 1
    NJ = T // P
    NBLK = NB * NJ
    WIN = 32
    KW = P + WIN
    NP = H // 2
    FG = 512
    NG = NB * T // FG
    FK = [min(P, FI - c * P) for c in range(-(-FI // P))]
    HALF = 64
    head = lambda slot: 2 * (slot % NP) + slot // NP
    SB = [(hh * NP + p, min(3, NP - p)) for hh in range(2) for p in range(0, NP, 3)]
    PG = [0, NP, NP // 2, NP + NP // 2]
    NS = len(SB)
    LATE = 13
    assert NS == 6 and len(FK) == 3 and H == 16 and NJ % 2 == 0

    with ExitStack() as ctx:
        sb = lambda n, s, d=F32: ctx.enter_context(nc.sbuf_tensor("b_" + n, s, d))
        pb = lambda n: ctx.enter_context(nc.psum_tensor("b_" + n, [P, 512], F32))
        sem = lambda n: sem_of("b_" + n)

        XB = sb("XB", [P, NB, T1])
        wqkv = sb("wqkv", [P, QKV])
        wo = sb("wo", [P, NP, D])
        w1 = sb("w1", [P, 2 * FI])
        w2 = sb("w2", [P, len(FK), D])
        b1c = sb("b1c", [P, 2 * len(FK)])
        gcol = sb("gcol", [P, 1])
        bcol = sb("bcol", [P, 1])
        b2c = sb("b2c", [P, 1])
        tab = sb("tab", [P, NJ, 4, DH])
        svec = sb("svec", [P, 4, DH])
        mask = sb("mask", [P, 2, KW])
        xst = sb("xst", [P, 2, P])
        qk = sb("qk", [P, 2, 2 * INNER])
        m2 = sb("m2", [P, 2, 512])
        sq = sb("sq", [P, 2, 512])
        ss = sb("ss", [P, 2 * H])
        rn = sb("rn", [P, 4, 2 * H])
        bits = sb("bits", [P, 2 * H], I32)
        half = sb("half", [P, 2 * H])
        qT = sb("qT", [P, NP, P])
        kT = sb("kT", [P, 2, NP, KW])
        V = sb("V", [P, 4, H, DH])
        VP = sb("VP", [P, 2, H // 4, DH])
        Sm = sb("Sm", [P, 2, H, KW])
        mx = sb("mx", [P, H])
        nmx = sb("nmx", [P, H])
        rs = sb("rs", [P, 2, H])
        rinv = sb("rinv", [P, H])
        PTs = sb("PTs", [P, H, P])
        PPs = sb("PPs", [P, H // 4, 4, WIN])
        quad = sb("quad", [P, 4])
        PC = sb("PC", [WIN, H, WIN])
        OT = sb("OT", [P, NP, P])
        st = sb("st", [P, 4, 6])
        mv = sb("mv", [P, 4, 2])
        var4 = sb("var4", [P, 4])
        rstd = sb("rstd", [P, 4])
        bits4 = sb("bits4", [P, 4], I32)
        half4 = sb("half4", [P, 4])
        xn = sb("xn", [P, 4, P])
        xnT = sb("xnT", [P, 2, FG])
        gg = sb("gg", [P, len(FK), FG])
        hg = sb("hg", [P, len(FK), FG])

        PQ = [pb("PQ0"), pb("PQ1")]
        PT = [pb("PT0"), pb("PT1")]
        PS = [pb("PS0"), pb("PS1")]
        PO = [pb("PO0"), pb("PO1")]

        wqkv_in, wo_in, ff_in, tab_in = sem("wqkv_in"), sem("wo_in"), sem("ff_in"), sem("tab_in")
        mask_in, zeroed = sem("mask_in"), sem("zeroed")
        vprev_in = [sem("vprev_in0"), sem("vprev_in1")]
        tab_ready, xst_ready, qkv_mm = sem("tab_ready"), sem("xst_ready"), sem("qkv_mm")
        v_copied, squared, chunk_read, rn_ready = sem("v_copied"), sem("squared"), sem("chunk_read"), sem("rn_ready")
        summed, k_normed, qk_turned, pt_copied, kprev_ready = (
            sem("summed"), sem("k_normed"), sem("qk_turned"), sem("pt_copied"), sem("kprev_ready"))
        scored, masked, max_ready, exped, rinv_ready, p_normed = (
            sem("scored"), sem("masked"), sem("max_ready"), sem("exped"), sem("rinv_ready"), sem("p_normed"))
        p_turned, pp_turned, pp_copied, pv_mm, ot_copied, wo_mm, attn_added = (
            sem("p_turned"), sem("pp_turned"), sem("pp_copied"), sem("pv_mm"), sem("ot_copied"), sem("wo_mm"),
            sem("attn_added"))
        sq_summed = sem("sq_summed")
        dve_own, f_own = sem("dve_own"), sem("f_own")
        f_turned, f_normed, f_back, xnT_ready, w1_mm, gelued, gated, w2_mm, ff_added = (
            sem("f_turned"), sem("f_normed"), sem("f_back"), sem("xnT_ready"), sem("w1_mm"), sem("gelued"),
            sem("gated"), sem("w2_mm"), sem("ff_added"))
        block = ctx.enter_context(nc.Block())

        aparts = {nc.gpsimd: sem("pool_apart"), nc.tensor: sem("pe_apart"), nc.vector: sem("dve_apart"), nc.sync: sem("sp_apart")}

        def apart(eng):
            eng.sem_inc(aparts[eng], 1)

        def counts(eng, n, *multiples):
            return {m: (eng.snap(n * m) if not isinstance(n, int) else n * m) for m in multiples}

        def q_use(j, g, first):
            return g if first else 8 * j - 4 + g

        def k_use(j, g, first):
            return (2 if first else 8 * j - 2) + g - 2

        def p_use(j, g, last):
            return 8 * (j + 1) + g - (4 if last else 0)

        def rows(eng, body):
            body(0, True, NB == 1)
            if NB > 2:
                with eng.Fori(1, NB - 1) as b:
                    body(b, False, False)
            if NB > 1:
                body(NB - 1, False, True)

        @block.sync
        def _(sp):
            def load_layer(l):
                at = lambda w: w[bass.ds(l, 1)]
                sp.dma_start(wqkv[:, :], at(Wqkv).rearrange("l p n -> p (l n)"))\
                  .then_inc(wqkv_in, 16)
                sp.dma_start(tab[:, :, :, :], rot_dram).then_inc(tab_in, 16)
                for t, (src, lo) in enumerate([(q_scale, 0), (q_scale, 1), (k_scale, 0), (k_scale, 1)]):
                    for a in range(2):
                        f = (a + lo) % 2
                        sp.dma_start(svec[:, t, a * DH // 2:(a + 1) * DH // 2],
                                     at(src)[0, f * DH // 2:(f + 1) * DH // 2].partition_broadcast(P)).then_inc(tab_in, 16)

            def load_wo(l):
                sp.dma_start(wo[:, :, :], Wo[bass.ds(l, 1)].rearrange("l (c p) n -> p (l c) n", p=P)).then_inc(wo_in, 16)

            def load_ff(l):
                at = lambda w: w[bass.ds(l, 1)]
                sp.dma_start(w1[:, :], at(W1).rearrange("l p n -> p (l n)")).then_inc(ff_in, 16)
                for c, k in enumerate(FK):
                    sp.dma_start(w2[0:k, c, :], at(W2)[:, c * P:c * P + k, :].rearrange("l p n -> p (l n)")).then_inc(ff_in, 16)
                    for a in range(2):
                        sp.dma_start(b1c[0:k, 2 * c + a:2 * c + a + 1],
                                     at(b1)[:, a * FI + c * P:a * FI + c * P + k].rearrange("l p -> p l")).then_inc(ff_in, 16)
                for dst, src in ((gcol, ln_g), (bcol, ln_b), (b2c, b2)):
                    sp.dma_start(dst[:, :], at(src).rearrange("l p -> p l")).then_inc(ff_in, 16)

            sp.dma_start(mask[:, :, :], mask_dram).then_inc(mask_in, 16)
            sp.dma_start(quad[:, :], quad_dram).then_inc(mask_in, 16)
            load_layer(0)
            load_wo(0)
            load_ff(0)

            def vprev(n8, j):
                sp.wait_ge(v_copied, n8[2] + 2 * j + 1)
                apart(sp)
                sp.wait_ge(qk_turned, n8[4] + 4 * j + 3)
                src = V[P - WIN:P, (j - 1) % 4, :, :].rearrange("p (s g) d -> p g s d", g=4)
                for g in range(4):
                    sp.dma_start(VP[WIN * g:WIN * (g + 1), j % 2, :, :], src[:, g]).then_inc(vprev_in[j % 2], 16)

            def row(l):
                def body(b, first, last):
                    n8 = counts(sp, l * NBLK + b * NJ, 2, 4)
                    for j in range(NJ):
                        vprev(n8, j)
                return body

            def layer(l, more):
                rows(sp, row(l))
                if more:
                    end = counts(sp, l + 1, 6 * NBLK, 4 * NBLK, NBLK, NG)
                    end_ff = sp.snap(end[NG] + NG)
                    sp.wait_ge(qkv_mm, end[6 * NBLK])
                    apart(sp)
                    sp.wait_ge(chunk_read, end[4 * NBLK])
                    apart(sp)
                    load_layer(l + 1)
                    sp.wait_ge(wo_mm, end[NBLK])
                    apart(sp)
                    load_wo(l + 1)
                    sp.wait_ge(ff_added, end_ff)
                    apart(sp)
                    load_ff(l + 1)

            if DEPTH > 1:
                with sp.Fori(0, DEPTH - 1) as l:
                    layer(l, True)
            layer(DEPTH - 1, False)

        @block.gpsimd
        def _(pool):
            pool.memset(kT[:, 1, :, :], 0.0).then_inc(zeroed, 1)
            pool.memset(V[:, 3, :, :], 0.0).then_inc(zeroed, 1)
            pool.memset(XB[:, :, 0:1], 0.0).then_inc(zeroed, 1)

            def stage(colb, b8, j, done):
                if done:
                    pool.wait_ge(qkv_mm, b8[6] + 6 * (j - 1))
                apart(pool)
                pool.tensor_copy(xst[:, j % 2, :], XAf[:, bass.ds(colb + (j // NJ) * T1 + (j % NJ) * P, P)]).then_inc(xst_ready, 1)

            XAf = XA[:, :, :].rearrange("p b t -> p (b t)")

            def sums(n8, j):
                for c in range(4):
                    x = qk[:, j % 2, c * 512:(c + 1) * 512]
                    pool.wait_ge(chunk_read, n8[4] + 4 * j + c + 1)
                    pool.tensor_tensor(x, x, m2[:, c % 2, :], ALU.add).then_inc(summed, 1)

            def k_norm(n8, j):
                pool.wait_ge(rn_ready, n8[1] + j + 1)
                pool.wait_ge(summed, n8[4] + 4 * j + 4)
                for c in (2, 3):
                    x = qk[:, j % 2, c * 512:(c + 1) * 512].rearrange("p (h d) -> p h d", d=DH)
                    pool.tensor_tensor(x, x, rn[:, j % 4, 8 * c:8 * c + 8].unsqueeze(2).broadcast_to([P, 8, DH]), ALU.mult)\
                        .then_inc(k_normed, 1)

            def kprev(n8, u8, j, first):
                pool.wait_ge(pt_copied, u8 + 3 + k_use(j - 1, 3, first))
                apart(pool)
                if j % NJ == 0:
                    pool.memset(kT[:, j % 2, :, 0:WIN], 0.0).then_inc(kprev_ready, 1)
                else:
                    pool.tensor_copy(kT[:, j % 2, :, 0:WIN], kT[:, (j + 1) % 2, :, P:KW]).then_inc(kprev_ready, 1)

            def p_norm(n8, j, a):
                heads = slice(8 * a, 8 * a + 8)
                pool.wait_ge(rinv_ready, n8[2] + 2 * j + a + 1)
                pool.tensor_tensor(PC[:, heads, :], Sm[0:WIN, j % 2, heads, 0:WIN],
                                   rinv[0:WIN, heads].unsqueeze(2).broadcast_to([WIN, 8, WIN]), ALU.mult)
                x = Sm[:, j % 2, heads, WIN:KW]
                pool.tensor_tensor(x, x, rinv[:, heads].unsqueeze(2).broadcast_to([P, 8, P]), ALU.mult).then_inc(p_normed, 1)

            def row(l):
                def body(b, first, last):
                    n8 = counts(pool, l * NBLK + b * NJ, 1, 2, 4, 6)
                    u8 = pool.snap(l * (8 * NBLK) + b * (8 * NJ))
                    colb = pool.snap(b * T1) if not isinstance(b, int) else b * T1
                    for j in range(NJ):
                        if not (first and j == 0):
                            p_norm(n8, j - 1, 1)
                        if j + 1 < NJ or not last:
                            kprev(n8, u8, j + 1, first and j == 0)
                        if j + 3 < NJ or not last:
                            stage(colb, n8, j + 3, True)
                        if j + 2 < NJ or not last:
                            sums(n8, j + 2)
                        p_norm(n8, j, 0)
                        if j + 2 < NJ or not last:
                            k_norm(n8, j + 2)
                    if last:
                        p_norm(n8, NJ - 1, 1)
                return body

            def layer(l):
                pool.wait_ge(tab_in, pool.snap((l + 1) * (16 * 9)))
                pool.tensor_tensor(tab[:, :, :, :], tab[:, :, :, :],
                                   svec[:, :, :].unsqueeze(1).broadcast_to([P, NJ, 4, DH]), ALU.mult).then_inc(tab_ready, 1)
                all_in = pool.snap((l + 1) * NG)
                pool.wait_ge(ff_added, pool.snap(l * NG + 1))
                n0 = counts(pool, l * NBLK, 1, 2, 4, 6)
                stage(0, n0, 0, False)
                stage(0, n0, 1, False)
                pool.wait_ge(ff_added, all_in)
                apart(pool)
                pool.memset(kT[:, 0, :, 0:WIN], 0.0).then_inc(kprev_ready, 1)
                sums(n0, 0)
                k_norm(n0, 0)
                stage(0, n0, 2, True)
                sums(n0, 1)
                k_norm(n0, 1)
                rows(pool, row(l))

            pool.wait_ge(zeroed, 3)
            with pool.Fori(0, DEPTH) as l:
                layer(l)

        @block.tensor
        def _(pe):
            def qkv(n8, j, chunks, first=False):
                x = xst[:, j % 2, :]
                if 0 in chunks:
                    pe.wait_ge(xst_ready, n8[1] + j + 1)
                for c in chunks:
                    if c < 2 and not first:
                        pe.wait_ge(v_copied, n8[2] + 2 * j - 1 + c)
                    if c > 1:
                        pe.wait_ge(chunk_read, n8[4] + 4 * j + c - 1)
                    pe.matmul(PQ[c % 2][:, :], x, wqkv[:, c * 512:(c + 1) * 512], start=True, stop=True).then_inc(qkv_mm, 1)

            def turn_q(n8, u8, j, first):
                for g in range(2):
                    pe.wait_ge(summed, n8[4] + 4 * j + g + 1)
                    if not first:
                        pe.wait_ge(pt_copied, u8 + 1 + q_use(j, g, first))
                    turn_group(j, g)

            def turn_k(n8, u8, j, first):
                for g in (2, 3):
                    pe.wait_ge(k_normed, n8[2] + 2 * j + g - 1)
                    pe.wait_ge(pt_copied, u8 + 1 + k_use(j, g, first))
                    turn_group(j, g)

            def turn_group(j, g):
                for p in range(4):
                    mm = pe.transpose(PT[g % 2][:, p * P:(p + 1) * P], qk[:, j % 2, (4 * g + p) * P:(4 * g + p + 1) * P], identf[:, :])
                mm.then_inc(qk_turned, 1)

            def scores(n8, u8, j, first, banks):
                for s in banks:
                    h0, nh = SB[s]
                    if s == 0:
                        pe.wait_ge(pt_copied, u8 + 3 + k_use(j, 3, first))
                        pe.wait_ge(kprev_ready, n8[1] + j + 1)
                        if not first:
                            pe.wait_ge(pp_copied, n8[1] + j)
                    elif s == 1:
                        if not first:
                            pe.wait_ge(attn_added, n8[1] + j)
                    else:
                        pe.wait_ge(masked, n8[6] + 6 * j + s - 1)
                    for i in range(nh):
                        p, hh = (h0 + i) % NP, (h0 + i) // NP
                        mm = pe.matmul(PS[s % 2][:, i * KW:(i + 1) * KW], qT[HALF * hh:HALF * hh + HALF, p, :],
                                       kT[HALF * hh:HALF * hh + HALF, j % 2, p, :], start=True, stop=True)
                    mm.then_inc(scored, 1)

            def turn_p(n8, u8, j, g, last):
                pe.wait_ge(p_normed, n8[2] + 2 * j + g % 2 + 1)
                pe.wait_ge(pt_copied, u8 + 1 + p_use(j, g, last))
                for i in range(4):
                    mm = pe.transpose(PT[g % 2][:, i * P:(i + 1) * P], Sm[:, j % 2, PG[g] + i, WIN:KW], identf[:, :])
                mm.then_inc(p_turned, 1)

            def turn_prev(n8, last, j):
                pe.wait_ge(p_normed, n8[2] + 2 * j + 2)
                pe.wait_ge(masked, n8[6] + 6 * j + (5 if last else 11))
                apart(pe)
                for g in range(4):
                    mm = pe.transpose(PS[0][:, g * WIN:(g + 1) * WIN], PC[:, 4 * g:4 * g + 4, :],
                                      identf[0:WIN, 0:WIN])
                mm.then_inc(pp_turned, 1)

            def pv(n8, u8, j, a, last, b2):
                pe.wait_ge(pt_copied, u8 + 3 + p_use(j, 2 * a + 1, last))
                if a == 0:
                    pe.wait_ge(pp_copied, n8[1] + j + 2)
                    pe.wait_ge(v_copied, n8[2] + 2 * j + 2)
                    pe.wait_ge(vprev_in[j % 2], b2 + ((j + NJ) // 2 + 1 - NJ // 2) * 64)
                pe.wait_ge(ot_copied, n8[2] + 2 * j + 1 + a)
                for hh in range(2):
                    r = slice(HALF * hh, HALF * hh + HALF)
                    G = 2 * hh + a
                    for g in range(4):
                        pe.matmul(PO[a][r, g * P:(g + 1) * P], V[:, j % 4, 4 * G + g, :], PTs[:, 4 * G + g, :],
                                  start=(g == 0), stop=False, skip_group_check=True)
                    mm = pe.matmul(PO[a][r, :].rearrange("p (g t) -> p g t", g=4)[:, :, 0:WIN], VP[:, j % 2, G, :],
                                   PPs[:, G, :, :], start=False, stop=True, skip_group_check=True)
                mm.then_inc(pv_mm, 1)

            def out_proj(n8, last, j):
                pe.wait_ge(masked, n8[6] + 6 * j + (6 if last else 12))
                for p in range(NP):
                    if p % 4 == 0:
                        pe.wait_ge(ot_copied, n8[2] + 2 * j + p // 4 + 3)
                    mm = pe.matmul(PS[1][:, 0:P], wo[:, p, :], OT[:, p, :], start=(p == 0), stop=(p == NP - 1))
                mm.then_inc(wo_mm, 1)

            def slot(n8, u8, b2, j, first, this, end, nxt, turn, last=False):
                if this:
                    scores(n8, u8, j, first, (0, 1))
                if nxt:
                    qkv(n8, j + 2, (0,))
                if this:
                    scores(n8, u8, j, first, (2,))
                if nxt:
                    qkv(n8, j + 2, (1,))
                if this:
                    scores(n8, u8, j, first, (3, 4))
                if nxt:
                    qkv(n8, j + 2, (2,))
                if end:
                    turn_p(n8, u8, j - 1, 0, last)
                    turn_p(n8, u8, j - 1, 1, last)
                    turn_prev(n8, last, j - 1)
                if this:
                    scores(n8, u8, j, first, (5,))
                if end:
                    turn_p(n8, u8, j - 1, 2, last)
                    turn_p(n8, u8, j - 1, 3, last)
                    pv(n8, u8, j - 1, 0, last, b2)
                if nxt:
                    qkv(n8, j + 2, (3,))
                if end:
                    pv(n8, u8, j - 1, 1, last, b2)
                if nxt:
                    qkv(n8, j + 2, (4,))
                if turn:
                    turn_q(n8, u8, j + 1, False)
                if nxt:
                    qkv(n8, j + 2, (5,))
                if turn:
                    turn_k(n8, u8, j + 1, False)
                if end:
                    out_proj(n8, last, j - 1)

            def row(l):
                def body(b, first, last):
                    n8 = counts(pe, l * NBLK + b * NJ, 1, 2, 4, 6)
                    u8 = pe.snap(l * (8 * NBLK) + b * (8 * NJ))
                    b2 = pe.snap((l * NBLK + b * NJ) * 32)
                    for j in range(NJ):
                        head_of = first and j == 0
                        if last and j == NJ - 1:
                            pe.wait_ge(v_copied, n8[2] + 2 * NJ)
                            pe.wait_ge(attn_added, n8[1] + NJ - 2)
                            ff_turn({1: 0}, 0)
                        slot(n8, u8, b2, j, head_of, True, not head_of, j + 2 < NJ or not last, j + 1 < NJ or not last)
                    if last:
                        ff_back({1: pe.snap(l * NG)}, 0)
                        slot(n8, u8, b2, NJ, False, False, True, False, False, True)
                return body

            def ff_turn(g8, n):
                b, t0 = n // (T // FG), (n % (T // FG)) * FG
                bank = PQ[0] if n == 0 else PT[0]
                if n > 1:
                    pe.wait_ge(f_normed, g8[1] + n)
                for q in range(4):
                    mm = pe.transpose(bank[:, q * P:(q + 1) * P], XB[:, b, t0 + q * P:t0 + (q + 1) * P], identf[:, :])
                mm.then_inc(f_turned, 1)

            def ff_back(g8, n):
                pe.wait_ge(f_normed, g8[1] + n + 1)
                bank = PQ[1] if n == 0 else PT[1]
                if n > 1:
                    pe.wait_ge(xnT_ready, g8[1] + n)
                for q in range(4):
                    mm = pe.transpose(bank[:, q * P:(q + 1) * P], xn[:, q, :], identf[:, :])
                mm.then_inc(f_back, 1)

            def ff_up(g8, n):
                pe.wait_ge(xnT_ready, g8[1] + n + 1)
                for c, k in enumerate(FK):
                    for a in range(2):
                        if c == 0 and n > 0:
                            pe.wait_ge(gated, g8[3] + 3 * n)
                        if c == 2:
                            pe.wait_ge((gelued, gated)[a], g8[3] + 3 * n + 1)
                        bank = (PQ, PS)[c % 2][a]
                        lo = (1 - a) * FI + c * P
                        pe.matmul(bank[0:k, :], w1[:, lo:lo + k], xnT[:, n % 2, :], start=True, stop=True).then_inc(w1_mm, 1)

            def ff_down(g8, n):
                if n > 1:
                    pe.wait_ge(ff_added, g8[1] + NG + n - 1)
                for c, k in enumerate(FK):
                    pe.wait_ge(gated, g8[3] + 3 * n + c + 1)
                    mm = pe.matmul(PO[n % 2][:, :], w2[0:k, c, :], hg[0:k, c, :], start=(c == 0), stop=(c == 2))
                mm.then_inc(w2_mm, 1)

            with pe.Fori(0, DEPTH) as l:
                pe.wait_ge(wqkv_in, pe.snap((l + 1) * 16))
                pe.wait_ge(wo_in, pe.snap((l + 1) * 16))
                n0 = counts(pe, l * NBLK, 1, 2, 4, 6)
                qkv(n0, 0, range(6), True)
                turn_q(n0, 0, 0, True)
                turn_k(n0, pe.snap(l * (8 * NBLK)), 0, True)
                qkv(n0, 1, range(6))
                rows(pe, row(l))
                g8 = counts(pe, l * NG, 1, 3)
                pe.wait_ge(attn_added, pe.snap((l + 1) * NBLK + 1))
                pe.wait_ge(ff_in, pe.snap((l + 1) * (16 * 13)))
                ff_turn(g8, 1)
                for n in range(NG):
                    ff_up(g8, n)
                    if n + 1 < NG:
                        ff_back(g8, n + 1)
                    if n + 2 < NG:
                        ff_turn(g8, n + 2)
                    ff_down(g8, n)

        @block.scalar
        def _(act):
            def copy_v(n8, j, c):
                act.wait_ge(qkv_mm, n8[6] + 6 * j + c + 5)
                act.copy(V[:, j % 4, :, :].rearrange("p (h a) d -> p h a d", h=2)[:, :, 4 * c:4 * c + 4, :],
                         PQ[c][:, :].rearrange("p (a h d) -> p h a d", h=2, d=DH)).then_inc(v_copied, 1)

            def square(n8, j, c, fresh=False):
                act.wait_ge(qkv_mm, n8[6] + 6 * j + c + 1)
                if c > 1 or not fresh:
                    act.wait_ge(sq_summed, n8[4] + 4 * j + c - 1)
                act.activation(sq[:, c % 2, :], PQ[c % 2][:, :], ACT.Square).then_inc(squared, 1)

            def copy_qk(n8, j, groups):
                for g in groups:
                    act.wait_ge(qk_turned, n8[4] + 4 * j + g + 1)
                    src = PT[g % 2][:, :].rearrange("p (c t) -> p c t", t=P)
                    dst = qT[:, 4 * g:4 * g + 4, :] if g < 2 else kT[:, j % 2, 4 * g - 8:4 * g - 4, WIN:KW]
                    act.copy(dst, src).then_inc(pt_copied, 1)

            def exps(n8, j, s0, s1):
                for s in range(s0, s1):
                    if s % 8 == 0:
                        act.wait_ge(max_ready, n8[2] + 2 * j + s // 8 + 1)
                    x = Sm[:, j % 2, s, :]
                    act.activation(x, x, ACT.Exp, bias=nmx[:, s:s + 1], scale=rn[:, j % 4, head(s):head(s) + 1],
                                   accum_out=rs[:, j % 2, s:s + 1]).then_inc(exped, 1)

            def copy_p(n8, j, g):
                act.wait_ge(p_turned, n8[4] + 4 * j + g + 1)
                act.copy(PTs[:, PG[g]:PG[g] + 4, :], PT[g % 2][:, :].rearrange("p (c t) -> p c t", t=P)).then_inc(pt_copied, 1)

            def copy_ot(n8, j, a):
                act.wait_ge(pv_mm, n8[2] + 2 * j + a + 1)
                act.copy(OT[:, 4 * a:4 * a + 4, :], PO[a][:, :].rearrange("p (c t) -> p c t", t=P)).then_inc(ot_copied, 1)

            def slot(n8, j, this, end, nxt, turn):
                if end:
                    exps(n8, j - 1, LATE, H)
                if nxt:
                    square(n8, j + 2, 0)
                    square(n8, j + 2, 1)
                if this:
                    exps(n8, j, 0, 4)
                if nxt:
                    square(n8, j + 2, 2)
                if end:
                    copy_p(n8, j - 1, 0)
                    copy_p(n8, j - 1, 1)
                if this:
                    exps(n8, j, 4, 6)
                if end:
                    copy_p(n8, j - 1, 2)
                    copy_p(n8, j - 1, 3)
                if this:
                    exps(n8, j, 6, 9)
                if end:
                    copy_ot(n8, j - 1, 0)
                if nxt:
                    square(n8, j + 2, 3)
                if this:
                    exps(n8, j, 9, 11)
                if end:
                    copy_ot(n8, j - 1, 1)
                if nxt:
                    copy_v(n8, j + 2, 0)
                if turn:
                    copy_qk(n8, j + 1, (0, 1))
                if nxt:
                    copy_v(n8, j + 2, 1)
                if this:
                    exps(n8, j, 11, 12)
                if turn:
                    copy_qk(n8, j + 1, (2, 3))
                if this:
                    exps(n8, j, 12, LATE)

            def row(l):
                def body(b, first, last):
                    n8 = counts(act, l * NBLK + b * NJ, 1, 2, 4, 6)
                    for j in range(NJ):
                        slot(n8, j, True, not (first and j == 0), j + 2 < NJ or not last, j + 1 < NJ or not last)
                    if last:
                        slot(n8, NJ, False, True, False, False)
                return body

            act.sem_inc(pt_copied, 2)
            act.sem_inc(ot_copied, 2)
            act.wait_ge(zeroed, 3)
            with act.Fori(0, DEPTH) as l:
                n0 = counts(act, l * NBLK, 2, 4, 6)
                for j in range(2):
                    for c in range(4):
                        square(n0, j, c, j == 0)
                    copy_v(n0, j, 0)
                    copy_v(n0, j, 1)
                    if j == 0:
                        copy_qk(n0, 0, (0, 1, 2, 3))
                rows(act, row(l))
                g8 = counts(act, l * NG, 1, 3, 6)

                def norm_out(n):
                    act.wait_ge(f_back, g8[1] + n + 1)
                    if n > 1:
                        act.wait_ge(w1_mm, g8[6] + 6 * (n - 1))
                    act.activation(xnT[:, n % 2, :], (PQ if n == 0 else PT)[1][:, :], ACT.Identity, bias=bcol[:, 0:1], scale=gcol[:, 0:1])\
                       .then_inc(xnT_ready, 1)

                act.wait_ge(ff_in, act.snap((l + 1) * (16 * 13)))
                norm_out(0)
                for n in range(NG):
                    for c, k in enumerate(FK):
                        act.wait_ge(w1_mm, g8[6] + 6 * n + 2 * c + 1)
                        if n > 0 and c == 0:
                            act.wait_ge(gated, g8[3] + 3 * n)
                        act.activation(gg[0:k, c, :], (PQ, PS)[c % 2][0][0:k, :], ACT.Gelu, bias=b1c[0:k, 2 * c + 1:2 * c + 2])\
                           .then_inc(gelued, 1)
                    if n + 1 < NG:
                        norm_out(n + 1)

        @block.vector
        def _(dve):
            XAf = XA[:, :, :].rearrange("p b t -> p (b t)")
            XBf = XB[:, :, :].rearrange("p b t -> p (b t)")
            OWN = 12

            def linker(base):
                k = [0]

                def link(ins):
                    k[0] += 1
                    ins.then_inc(dve_own, 1)
                    dve.wait_ge(dve_own, base + k[0])
                return link

            def chunk(n8, j, c, fresh=False):
                src = PQ[c % 2][:, :].rearrange("p (h d) -> p h d", d=DH)
                swapped = PQ[c % 2][:, :].rearrange("p (h a d) -> p h a d", a=2, d=DH // 2)[:, :, ::-1, :]
                t = 2 * (c // 2)
                ctab = tab[:, j % NJ, t, :].unsqueeze(1).broadcast_to([P, 8, DH])
                stab = tab[:, j % NJ, t + 1, :].rearrange("p (a d) -> p a d", a=2).unsqueeze(1).broadcast_to([P, 8, 2, DH // 2])
                dve.wait_ge(squared, n8[4] + 4 * j + c + 1)
                dve.tensor_tensor(qk[:, j % 2, c * 512:(c + 1) * 512].rearrange("p (h d) -> p h d", d=DH), src, ctab, ALU.mult)
                if c > 1 or not fresh:
                    dve.wait_ge(summed, n8[4] + 4 * j + c - 1)
                dve.tensor_tensor(m2[:, c % 2, :].rearrange("p (h a d) -> p h a d", a=2, d=DH // 2), swapped, stab, ALU.mult)\
                    .then_inc(chunk_read, 1)
                dve.tensor_reduce(ss[:, 8 * c:8 * c + 8], sq[:, c % 2, :].rearrange("p (h d) -> p h d", d=DH), AX.X, ALU.add)\
                   .then_inc(sq_summed, 1)

            def norms(n8, j, own):
                dve.wait_ge(sq_summed, n8[4] + 4 * j + 4)
                rsqrt_on_dve(dve, linker(own), ss[:, :], rn[:, j % 4, :], bits[:, :], half[:, :], guard=1e-24)
                dve.sem_inc(rn_ready, 1)

            def masks(n8, j, banks):
                var = 1 if j == 0 else 0
                for s in banks:
                    h0, nh = SB[s]
                    dve.wait_ge(scored, n8[6] + 6 * j + s + 1)
                    apart(dve)
                    for i in range(nh):
                        ins = dve.tensor_tensor_reduce(Sm[:, j % 2, h0 + i, :], PS[s % 2][:, i * KW:(i + 1) * KW], mask[:, var, :],
                                                       1.0, LOWEST, ALU.add, ALU.max, mx[:, h0 + i:h0 + i + 1])
                    ins.then_inc(masked, 1)
                    if s % 3 == 2:
                        a = s // 3
                        dve.wait_ge(masked, n8[6] + 6 * j + 3 * a + 3)
                        dve.scalar_tensor_tensor(nmx[:, 8 * a:8 * a + 8], mx[:, 8 * a:8 * a + 8], -1.0, rn[:, j % 4, a:H:2],
                                                 ALU.mult, ALU.mult).then_inc(max_ready, 1)

            def inverses(n8, j, a):
                dve.wait_ge(exped, n8[16] + 16 * j + 8 * a + 8)
                dve.reciprocal(rinv[:, 8 * a:8 * a + 8], rs[:, j % 2, 8 * a:8 * a + 8]).then_inc(rinv_ready, 1)

            def spread_prev(n8, j):
                dve.wait_ge(pp_turned, n8[1] + j + 1)
                src = PS[0][:, 0:4 * WIN].rearrange("p (s t) -> p s t", t=WIN).unsqueeze(2).broadcast_to([P, 4, 4, WIN])
                dve.tensor_tensor(PPs[:, :, :, :], src, quad[:, :].unsqueeze(1).unsqueeze(3).broadcast_to([P, 4, 4, WIN]),
                                  ALU.mult).then_inc(pp_copied, 1)

            def residual(n8, colb, j):
                dve.wait_ge(wo_mm, n8[1] + j + 1)
                for a in range(2):
                    cols = bass.ds(colb + (j * P + a if j >= 0 else a - P - 1), P)
                    r = slice(HALF * a, HALF * a + HALF)
                    ins = dve.tensor_tensor(XBf[r, cols], PS[1][r, 0:P], XAf[r, cols], ALU.add)
                ins.then_inc(attn_added, 1)

            def layer_norm(g8, own, n):
                x = (PQ if n == 0 else PT)[0][:, :].rearrange("p (q c) -> p q c", q=4)
                dve.wait_ge(f_turned, g8[1] + n + 1)
                for q in range(4):
                    ins = dve.bn_stats(st[:, q, :], x[:, q, :])
                ins.then_inc(f_own, 1)
                dve.wait_ge(f_own, g8[3] + 3 * n + 1)
                apart(dve)
                for q in range(4):
                    ins = dve.bn_aggr(mv[:, q, :], st[:, q, :])
                ins.then_inc(f_own, 1)
                dve.wait_ge(f_own, g8[3] + 3 * n + 2)
                dve.tensor_copy(var4[:, :], mv[:, :, 1]).then_inc(f_own, 1)
                dve.wait_ge(f_own, g8[3] + 3 * n + 3)
                rsqrt_on_dve(dve, linker(own + OWN * n), var4[:, :], rstd[:, :], bits4[:, :], half4[:, :], bias=1e-5)
                if n > 0:
                    dve.wait_ge(f_back, g8[1] + n)
                for q in range(4):
                    ins = dve.tensor_scalar(xn[:, q, :], x[:, q, :], mv[:, q, 0:1], rstd[:, q:q + 1], ALU.subtract, ALU.mult)
                ins.then_inc(f_normed, 1)

            def row(l):
                def body(b, first, last):
                    n8 = counts(dve, l * NBLK + b * NJ, 1, 2, 4, 6, 16)
                    own = dve.snap(l * ((NBLK + NG) * OWN) + b * (NJ * OWN))
                    colb = dve.snap(b * T1) if not isinstance(b, int) else b * T1
                    for j in range(NJ):
                        end, nxt = not (first and j == 0), j + 2 < NJ or not last
                        masks(n8, j, (0, 1))
                        if end:
                            inverses(n8, j - 1, 1)
                        masks(n8, j, (2,))
                        if nxt:
                            chunk(n8, j + 2, 0)
                        masks(n8, j, (3, 4))
                        if end:
                            spread_prev(n8, j - 1)
                        masks(n8, j, (5,))
                        if last and j == NJ - 1:
                            layer_norm(counts(dve, l * NG, 1, 3), dve.snap(l * ((NBLK + NG) * OWN) + NBLK * OWN), 0)
                        if nxt:
                            chunk(n8, j + 2, 1)
                            chunk(n8, j + 2, 2)
                            chunk(n8, j + 2, 3)
                            norms(n8, j + 2, own + OWN * (j + 2))
                        inverses(n8, j, 0)
                        if end:
                            residual(n8, colb, j - 1)
                    if last:
                        inverses(n8, NJ - 1, 1)
                        spread_prev(n8, NJ - 1)
                        residual(n8, colb, NJ - 1)
                return body

            dve.sem_inc(attn_added, 1)
            dve.sem_inc(pp_copied, 1)
            dve.sem_inc(ff_added, NG)
            dve.wait_ge(mask_in, 32)
            dve.wait_ge(zeroed, 3)
            with dve.Fori(0, DEPTH) as l:
                n0 = counts(dve, l * NBLK, 1, 2, 4, 6, 16)
                dve.wait_ge(tab_ready, l + 1)
                for j in range(2):
                    for c in range(4):
                        chunk(n0, j, c, j == 0)
                    norms(n0, j, dve.snap(l * ((NBLK + NG) * OWN) + j * OWN))
                rows(dve, row(l))
                g8 = counts(dve, l * NG, 1, 3, 6)
                own = dve.snap(l * ((NBLK + NG) * OWN) + NBLK * OWN)

                def gate(n, c):
                    k = FK[c]
                    dve.wait_ge(w1_mm, g8[6] + 6 * n + 2 * c + 2)
                    dve.wait_ge(gelued, g8[3] + 3 * n + c + 1)
                    if n > 0 and c == 0:
                        dve.wait_ge(w2_mm, g8[1] + n)
                    dve.scalar_tensor_tensor(hg[0:k, c, :], (PQ, PS)[c % 2][1][0:k, :], b1c[0:k, 2 * c:2 * c + 1],
                                             gg[0:k, c, :], ALU.add, ALU.mult).then_inc(gated, 1)

                def ff_residual(n):
                    b, t0 = n // (T // FG), (n % (T // FG)) * FG
                    dve.wait_ge(w2_mm, g8[1] + n + 1)
                    for a in range(2):
                        r = slice(HALF * a, HALF * a + HALF)
                        ins = dve.scalar_tensor_tensor(XA[r, b, t0 + a:t0 + a + FG], PO[n % 2][r, :], b2c[r, 0:1],
                                                       XB[r, b, t0 + a:t0 + a + FG], ALU.add, ALU.add)
                    ins.then_inc(ff_added, 1)

                layer_norm(g8, own, 1)
                for n in range(NG):
                    gate(n, 0)
                    if n > 0:
                        ff_residual(n - 1)
                    gate(n, 1)
                    gate(n, 2)
                    if n + 2 < NG:
                        layer_norm(g8, own, n + 2)
                ff_residual(NG - 1)


def stage_c(nc, sem, XA, X2, Y, identf, x1_dram, Wq, Wk, Wv, tri_dram):
    B, T, D = x1_dram.shape
    NJ = T // P
    NBLK = B * NJ
    GAMMA = float(D) ** -0.5
    HALF = 64
    FG = 512
    NG = B * T // FG
    cum = lambda i: i if i <= 4 else 4 + 2 * (i - 4)
    CUM = cum(NJ)
    assert NJ == 8

    with ExitStack() as ctx:
        sb = lambda n, s, d=F32: ctx.enter_context(nc.sbuf_tensor("c_" + n, s, d))
        pb = lambda n, w=512: ctx.enter_context(nc.psum_tensor("c_" + n, [P, w], F32))
        xu = sb("xu", [P, 2, FG])
        xnT = sb("xnT", [P, B * T])
        xb = sb("xb", [P, T])
        qT = sb("qT", [P, T])
        kT = sb("kT", [P, T])
        V = sb("V", [P, NJ, D])
        wq = sb("wq", [P, D])
        wk = sb("wk", [P, D])
        wv = sb("wv", [P, D])
        tri = sb("tri", [P, P])
        E = sb("E", [P, 2, T])
        ET = sb("ET", [P, 2, NJ, P])
        nmx = sb("nmx", [P, 2])
        rs = sb("rs", [P, 2])
        rinv = sb("rinv", [P, 2])
        nb = NormBuffers(lambda n, s, d=F32: sb(n, s, d), NBLK)
        PS = [pb("PS0", 1024), pb("PS1", 1024)]
        PT = [pb("PT0"), pb("PT1")]
        PA, PY = pb("PA"), pb("PY")

        x1_in, w_in, dve_own = sem("c_x1_in"), sem("c_w_in"), sem("c_dve_own")
        unshifted, turned, y_copied, xn_ready, xnT_ready = (
            sem("c_unshifted"), sem("c_turned"), sem("c_y_copied"), sem("c_xn_ready"), sem("c_xnT_ready"))
        xb_ready, projected, copied, scored, masked, max_found, max_ready, exped = (
            sem("c_xb_ready"), sem("c_projected"), sem("c_copied"), sem("c_scored"), sem("c_masked"),
            sem("c_max_found"), sem("c_max_ready"), sem("c_exped"))
        rinv_ready, p_turned, pt_copied, pv_mm, y_ready, pool_apart = (
            sem("c_rinv_ready"), sem("c_p_turned"), sem("c_pt_copied"), sem("c_pv_mm"), sem("c_y_ready"), sem("c_pool_apart"))
        block = ctx.enter_context(nc.Block())

        @block.sync
        def _(sp):
            sp.dma_start(X2[:, :, :], x1_dram.rearrange("b (j p) d -> p (b j) d", p=P)).then_inc(x1_in, 16)
            for dst, src in ((wq, Wq), (wk, Wk), (wv, Wv), (tri, tri_dram)):
                sp.dma_start(dst[:, :], src).then_inc(w_in, 16)

        @block.gpsimd
        def _(pool):
            pool.wait_ge(xnT_ready, NG)
            with pool.Fori(0, B) as b:
                col = pool.snap(b * T)
                pool.wait_ge(projected, pool.snap(6 * b + 1))
                pool.sem_inc(pool_apart, 1)
                pool.tensor_copy(xb[:, :], xnT[:, bass.ds(col, T)]).then_inc(xb_ready, 1)

        @block.tensor
        def _(pe):
            pe.sem_inc(projected, 1)
            pe.sem_inc(pv_mm, 1)
            for g in range(NG):
                pe.wait_ge(unshifted, g + 1)
                if g >= 2:
                    pe.wait_ge(y_copied, g - 1)
                for u in range(4):
                    ins = pe.transpose(PT[g % 2][:, u * P:(u + 1) * P], xu[:, g % 2, u * P:(u + 1) * P], identf[:, :])
                ins.then_inc(turned, 1)
            pe.wait_ge(xn_ready, 1)
            for g in range(NG):
                if g >= 2:
                    pe.wait_ge(xnT_ready, g - 1)
                for u in range(4):
                    ins = pe.transpose(PT[g % 2][:, u * P:(u + 1) * P], Y[:, 4 * g + u, :], identf[:, :])
                ins.then_inc(turned, 1)
            pe.wait_ge(w_in, 64)
            pe.wait_ge(xnT_ready, NG)

            def scores(b8, b6, i):
                if i < 2:
                    pe.wait_ge(copied, b6 + 4)
                else:
                    pe.wait_ge(exped, b8 + i)
                n = (i + 1) * P
                for lo in range(0, n, 512):
                    hi = min(n, lo + 512)
                    ins = pe.matmul(PS[i % 2][:, lo:hi], qT[:, i * P:(i + 1) * P], kT[:, lo:hi], start=True, stop=True)
                ins.then_inc(scored, 1)

            with pe.Fori(0, B) as b:
                b6, b8, b12 = pe.snap(b * 6), pe.snap(b * NJ), pe.snap(b * CUM)
                pe.wait_ge(xb_ready, pe.snap(b + 1))
                pe.wait_ge(exped, b8 + 1)
                for k, w in enumerate((wq, wk)):
                    for h in range(2):
                        pe.matmul(PS[k][:, h * 512:(h + 1) * 512], w[:, :], xb[:, h * 512:(h + 1) * 512], start=True, stop=True)\
                          .then_inc(projected, 1)
                for h in range(2):
                    if h == 1:
                        pe.wait_ge(copied, b6 + 5)
                    for u in range(4):
                        ins = pe.matmul(PA[:, u * P:(u + 1) * P], xb[:, (4 * h + u) * P:(4 * h + u + 1) * P], wv[:, :],
                                        start=True, stop=True)
                    ins.then_inc(projected, 1)
                scores(b8, b6, 0)
                scores(b8, b6, 1)
                for i in range(NJ):
                    pe.wait_ge(exped, b8 + i + 2)
                    pe.wait_ge(pt_copied, b12 + cum(i) + 1)
                    for g in range(i // 4 + 1):
                        for u in range(4 * g, min(4 * g + 4, i + 1)):
                            ins = pe.transpose(PT[g][:, (u % 4) * P:(u % 4 + 1) * P], E[:, i % 2, u * P:(u + 1) * P], identf[:, :])
                        ins.then_inc(p_turned, 1)
                    if i + 2 < NJ:
                        scores(b8, b6, i + 2)
                    pe.wait_ge(copied, b6 + 6)
                    pe.wait_ge(y_ready, b8 + i + 1)
                    for u in range(i + 1):
                        if u % 4 == 0:
                            pe.wait_ge(pt_copied, b12 + cum(i) + u // 4 + 2)
                        ins = pe.matmul(PY[:, 0:D], ET[:, i % 2, u, :], V[:, u, :], start=(u == 0), stop=(u == i))
                    ins.then_inc(pv_mm, 1)

        @block.scalar
        def _(act):
            for g in range(NG + 1):
                if g < NG:
                    if g >= 2:
                        act.wait_ge(turned, g - 1)
                    b, t0 = g // 2, (g % 2) * FG
                    act.copy(xu[0:HALF, g % 2, :], XA[0:HALF, b, t0:t0 + FG])
                    act.copy(xu[HALF:P, g % 2, :], XA[HALF:P, b, t0 + 1:t0 + 1 + FG]).then_inc(unshifted, 1)
                if g >= 1:
                    act.wait_ge(turned, g)
                    act.copy(Y[:, 4 * g - 4:4 * g, :].rearrange("p n d -> p (n d)"), PT[(g - 1) % 2][:, :]).then_inc(y_copied, 1)
            for g in range(NG):
                act.wait_ge(turned, NG + g + 1)
                act.copy(xnT[:, g * FG:(g + 1) * FG], PT[g % 2][:, :]).then_inc(xnT_ready, 1)
            act.sem_inc(exped, 1)
            with act.Fori(0, B) as b:
                b6, b8 = act.snap(b * 6), act.snap(b * NJ)
                act.wait_ge(pv_mm, b8 + 1)
                for k, dst in enumerate((qT, kT)):
                    for h in range(2):
                        act.wait_ge(projected, b6 + 2 * k + h + 2)
                        act.copy(dst[:, h * 512:(h + 1) * 512], PS[k][:, h * 512:(h + 1) * 512]).then_inc(copied, 1)
                for h in range(2):
                    act.wait_ge(projected, b6 + 6 + h)
                    act.copy(V[:, 4 * h:4 * h + 4, :].rearrange("p n d -> p (n d)"), PA[:, :]).then_inc(copied, 1)
                for i in range(NJ):
                    n = (i + 1) * P
                    act.wait_ge(max_ready, b8 + i + 1)
                    if i >= 2:
                        act.wait_ge(p_turned, act.snap(b * CUM + cum(i - 1)))
                        act.wait_ge(rinv_ready, b8 + i - 1)
                    act.activation(E[:, i % 2, 0:n], PS[i % 2][:, 0:n], ACT.Exp, bias=nmx[:, i % 2:i % 2 + 1], scale=GAMMA,
                                   accum_out=rs[:, i % 2:i % 2 + 1]).then_inc(exped, 1)

        @block.vector
        def _(dve):
            step = Steps(dve, dve_own)
            ys, xs = (lambda q: Y[:, q, :]), (lambda q: X2[:, q, :])
            for g in range(NG):
                dve.wait_ge(y_copied, g + 1)
                norm_stats(dve, step, nb, ys, range(4 * g, 4 * g + 4))
            norm_apply(dve, step, nb, ys, ys)
            dve.wait_ge(x1_in, 16)
            step(dve.tensor_tensor(X2[:, :, :], X2[:, :, :], Y[:, :, :], ALU.add))
            norm_stats(dve, step, nb, xs, range(NBLK))
            norm_apply(dve, step, nb, xs, ys)
            dve.sem_inc(xn_ready, 1)
            dve.wait_ge(w_in, 64)
            dve.wait_ge(turned, 2 * NG)
            Yf = Y[:, :, :].rearrange("p n d -> p (n d)")

            def maxima(b8, i):
                dve.wait_ge(scored, b8 + i + 1)
                diag = PS[i % 2][:, i * P:(i + 1) * P]
                dve.tensor_tensor(diag, diag, tri[:, :], ALU.add).then_inc(masked, 1)
                dve.wait_ge(masked, b8 + i + 1)
                m = nmx[:, i % 2:i % 2 + 1]
                dve.tensor_reduce(m, PS[i % 2][:, 0:(i + 1) * P], AX.X, ALU.max, negate=True).then_inc(max_found, 1)
                dve.wait_ge(max_found, b8 + i + 1)
                dve.tensor_scalar(m, m, GAMMA, None, ALU.mult).then_inc(max_ready, 1)

            dve.sem_inc(pt_copied, 1)
            dve.sem_inc(y_ready, 1)
            with dve.Fori(0, B) as b:
                b8, b12, col = dve.snap(b * NJ), dve.snap(b * CUM), dve.snap(b * (NJ * D))
                maxima(b8, 0)
                maxima(b8, 1)
                for i in range(NJ):
                    dve.wait_ge(exped, b8 + i + 2)
                    dve.reciprocal(rinv[:, i % 2:i % 2 + 1], rs[:, i % 2:i % 2 + 1]).then_inc(rinv_ready, 1)
                    for g in range(i // 4 + 1):
                        n = min(4, i + 1 - 4 * g)
                        dve.wait_ge(p_turned, b12 + cum(i) + g + 1)
                        if i >= 2:
                            dve.wait_ge(pv_mm, b8 + i)
                        dve.tensor_copy(ET[:, i % 2, 4 * g:4 * g + n, :].rearrange("p n k -> p (n k)"), PT[g][:, 0:n * P])\
                           .then_inc(pt_copied, 1)
                    if i + 2 < NJ:
                        maxima(b8, i + 2)
                    dve.wait_ge(pv_mm, b8 + i + 2)
                    dve.wait_ge(rinv_ready, b8 + i + 1)
                    dve.tensor_scalar(Yf[:, bass.ds(col + i * D, D)], PY[:, 0:D], rinv[:, i % 2:i % 2 + 1], None, ALU.mult)\
                       .then_inc(y_ready, 1)
            dve.wait_ge(y_ready, NBLK + 1)
            norm_stats(dve, step, nb, ys, range(NBLK))
            norm_apply(dve, step, nb, ys, ys)
            step(dve.tensor_tensor(X2[:, :, :], X2[:, :, :], Y[:, :, :], ALU.add))


def stage_d(nc, sem, X3, Y, identf, gate, W1, b1, W2, b2, order_dram, out_dram):
    B, T, D = out_dram.shape
    NE, _, FH = W1.shape
    TOPK = int(NE * 0.2)
    NBLK = B * T // P
    FG = 512
    NG = NBLK // 4
    NC = FH // P
    assert NE * NBLK == 512 and NC == 2 and NE % 2 == 0

    with ExitStack() as ctx:
        sb = lambda n, s, d=F32: ctx.enter_context(nc.sbuf_tensor("d_" + n, s, d))
        pb = lambda n: ctx.enter_context(nc.psum_tensor("d_" + n, [P, 512], F32))
        xT = sb("xT", [P, B * T])
        acc = sb("acc", [P, NBLK, D])
        wg = sb("wg", [P, NE])
        b1r = sb("b1r", [NE, FH])
        b1c = sb("b1c", [P, NC, NE])
        b2r = sb("b2r", [NE, D])
        order = sb("order", [P, NE])
        w1 = sb("w1", [P, 2, FH])
        w2 = sb("w2", [P, 2, NC, D])
        G = sb("G", [P, NBLK, NE])
        GE = sb("GE", [P, NE, NBLK])
        mx = sb("mx", [P, NBLK])
        gs = sb("gs", [P, NBLK])
        rest = sb("rest", [P, NBLK, NE])
        hot = sb("hot", [P, NBLK, NE])
        best = sb("best", [P, NBLK])
        chosen = sb("chosen", [P, NBLK, NE])
        gT = sb("gT", [NE, NBLK * P])
        HT = sb("HT", [P, 2, NC, FG])
        nb = NormBuffers(lambda n, s, d=F32: sb(n, s, d), NBLK)
        PT = [pb("PT0"), pb("PT1")]
        PH = [pb("PH%d" % k) for k in range(4)]
        PY = [pb("PY0"), pb("PY1")]

        c_in, w_in, out_done, dve_own = sem("d_c_in"), [sem("d_w_in0"), sem("d_w_in1")], sem("d_out_done"), sem("d_dve_own")
        xn_ready, turned, xT_ready, logits, shifted, gate_exped, g_ready, g_turned, gT_ready, bias_mm, acc_ready = (
            sem("d_xn_ready"), sem("d_turned"), sem("d_xT_ready"), sem("d_logits"), sem("d_shifted"), sem("d_gate_exped"),
            sem("d_g_ready"), sem("d_g_turned"), sem("d_gT_ready"), sem("d_bias_mm"), sem("d_acc_ready"))
        b1_turned, b1_ready = sem("d_b1_turned"), sem("d_b1_ready")
        up_mm, h_ready, down_mm, added, y_ready, sp_apart, act_apart = (
            sem("d_up_mm"), sem("d_h_ready"), sem("d_down_mm"), sem("d_added"), sem("d_y_ready"), sem("d_sp_apart"), sem("d_act_apart"))
        block = ctx.enter_context(nc.Block())
        EG = 2 * NG

        @block.sync
        def _(sp):
            sp.dma_start(wg[:, :], gate).then_inc(c_in, 16)
            sp.dma_start(b1r[:, :], b1).then_inc(c_in, 16)
            sp.dma_start(b2r[:, :], b2).then_inc(c_in, 16)
            sp.dma_start(order[:, :], order_dram.partition_broadcast(P)).then_inc(c_in, 16)
            with sp.Fori(0, NE // 2) as i:
                for a in range(2):
                    sp.wait_ge(down_mm, sp.snap(i * EG + a * NG + 1))
                    sp.sem_inc(sp_apart, 1)
                    sp.dma_start(w1[:, a, :], W1[bass.ds(2 * i + a, 1)].rearrange("e p n -> p (e n)")).then_inc(w_in[a], 16)
                    sp.dma_start(w2[:, a, :, :], W2[bass.ds(2 * i + a, 1)].rearrange("e (c p) d -> p (e c) d", p=P)).then_inc(w_in[a], 16)
            sp.wait_ge(y_ready, 1)
            sp.dma_start(out_dram.rearrange("b (j p) d -> p (b j) d", p=P), X3[:, :, :]).then_inc(out_done, 16)
            sp.wait_ge(out_done, 16)

        @block.tensor
        def _(pe):
            pe.sem_inc(down_mm, NG + 1)
            pe.wait_ge(xn_ready, 1)
            for g in range(NG):
                if g >= 2:
                    pe.wait_ge(xT_ready, g - 1)
                for u in range(4):
                    ins = pe.transpose(PT[g % 2][:, u * P:(u + 1) * P], Y[:, 4 * g + u, :], identf[:, :])
                ins.then_inc(turned, 1)
            pe.wait_ge(c_in, 64)
            for c in range(NC):
                ins = pe.transpose(PH[0][:, c * NE:(c + 1) * NE], b1r[:, c * P:(c + 1) * P], identf[0:NE, 0:NE])
            ins.then_inc(b1_turned, 1)
            pe.wait_ge(xT_ready, NG)
            for n in range(NBLK):
                ins = pe.matmul(PY[0][:, n * NE:(n + 1) * NE], xT[:, n * P:(n + 1) * P], wg[:, :], start=True, stop=True)
            ins.then_inc(logits, 1)
            pe.wait_ge(g_ready, 1)
            for g in range(NG):
                if g >= 2:
                    pe.wait_ge(gT_ready, g - 1)
                for u in range(4):
                    ins = pe.transpose(PT[g % 2][0:NE, u * P:(u + 1) * P], G[:, 4 * g + u, :], identf[:, :])
                ins.then_inc(g_turned, 1)
            for g in range(NG):
                pe.wait_ge(gT_ready, g + 1)
                if g >= 2:
                    pe.wait_ge(acc_ready, g - 1)
                for u in range(4):
                    ins = pe.matmul(PY[g % 2][:, u * P:(u + 1) * P], gT[:, (4 * g + u) * P:(4 * g + u + 1) * P], b2r[:, :],
                                    start=True, stop=True)
                ins.then_inc(bias_mm, 1)
            pe.wait_ge(acc_ready, NG)

            def up(t2, w32, k):
                a, g = k // NG, k % NG
                if g == 0:
                    pe.wait_ge(w_in[a], w32)
                for c in range(NC):
                    pe.wait_ge(h_ready, t2 + 2 * k + c + 1)
                    pe.matmul(PH[2 * (k % 2) + c][:, :], w1[:, a, c * P:(c + 1) * P], xT[:, g * FG:(g + 1) * FG],
                              start=True, stop=True).then_inc(up_mm, 1)

            def down(t, t2, k):
                a = k // NG
                pe.wait_ge(h_ready, t2 + 2 * k + 6)
                pe.wait_ge(added, t + k + NG - 1)
                for u in range(4):
                    for c in range(NC):
                        ins = pe.matmul(PY[k % 2][:, u * P:(u + 1) * P], HT[:, k % 2, c, u * P:(u + 1) * P], w2[:, a, c, :],
                                        start=(c == 0), stop=(c == NC - 1))
                ins.then_inc(down_mm, 1)

            with pe.Fori(0, NE // 2) as i:
                t, t2, w32 = pe.snap(i * EG), pe.snap(i * (2 * EG)), pe.snap(i * 32 + 32)
                up(t2, w32, 0)
                for k in range(EG):
                    if k + 1 < EG:
                        up(t2, w32, k + 1)
                    down(t, t2, k)

        @block.scalar
        def _(act):
            for g in range(NG):
                act.wait_ge(turned, g + 1)
                act.copy(xT[:, g * FG:(g + 1) * FG], PT[g % 2][:, :]).then_inc(xT_ready, 1)
            act.wait_ge(b1_turned, 1)
            act.copy(b1c[:, :, :].rearrange("p c e -> p (c e)"), PH[0][:, 0:NC * NE]).then_inc(b1_ready, 1)
            act.wait_ge(shifted, 1)
            act.activation(G[:, :, :], G[:, :, :], ACT.Exp).then_inc(gate_exped, 1)
            for g in range(NG):
                act.wait_ge(g_turned, g + 1)
                act.copy(gT[:, g * FG:(g + 1) * FG], PT[g % 2][0:NE, :]).then_inc(gT_ready, 1)
            for g in range(NG):
                act.wait_ge(bias_mm, g + 1)
                act.copy(acc[:, 4 * g:4 * g + 4, :].rearrange("p n d -> p (n d)"), PY[g % 2][:, :]).then_inc(acc_ready, 1)
            act.sem_inc(h_ready, 4)
            b1f = b1c[:, :, :].rearrange("p c e -> p (c e)")
            act.wait_ge(b1_ready, 1)
            with act.Fori(0, NE // 2) as i:
                t, t2, e0 = act.snap(i * EG), act.snap(i * (2 * EG)), act.snap(i * 2)
                for k in range(EG):
                    act.wait_ge(down_mm, t + k + NG)
                    for c in range(NC):
                        act.wait_ge(up_mm, t2 + 2 * k + c + 1)
                        act.sem_inc(act_apart, 1)
                        act.activation(HT[:, k % 2, c, :], PH[2 * (k % 2) + c][:, :], ACT.Relu,
                                       bias=b1f[:, bass.ds(e0 + c * NE + k // NG, 1)]).then_inc(h_ready, 1)

        @block.vector
        def _(dve):
            step = Steps(dve, dve_own)
            xs, ys, accs = (lambda q: X3[:, q, :]), (lambda q: Y[:, q, :]), (lambda q: acc[:, q, :])
            norm_stats(dve, step, nb, xs, range(NBLK))
            norm_apply(dve, step, nb, xs, ys)
            dve.sem_inc(xn_ready, 1)
            dve.wait_ge(logits, 1)
            lg = PY[0][:, :].rearrange("p (n e) -> p n e", e=NE)
            over_e = lambda x: x.unsqueeze(2).broadcast_to([P, NBLK, NE])
            step(dve.tensor_reduce(mx[:, :], lg, AX.X, ALU.max))
            dve.tensor_tensor(G[:, :, :], lg, over_e(mx[:, :]), ALU.subtract).then_inc(shifted, 1)
            dve.wait_ge(gate_exped, 1)
            step(dve.tensor_reduce(gs[:, :], G[:, :, :], AX.X, ALU.add))
            step(dve.reciprocal(gs[:, :], gs[:, :]))
            step(dve.tensor_tensor(G[:, :, :], G[:, :, :], over_e(gs[:, :]), ALU.mult))
            dve.wait_ge(c_in, 64)
            step(dve.tensor_copy(rest[:, :, :], G[:, :, :]))
            for k in range(TOPK):
                step(dve.tensor_reduce(best[:, :], rest[:, :, :], AX.X, ALU.max))
                step(dve.tensor_tensor(hot[:, :, :], rest[:, :, :], over_e(best[:, :]), ALU.is_equal))
                step(dve.tensor_tensor(hot[:, :, :], hot[:, :, :], order[:, :].unsqueeze(1).broadcast_to([P, NBLK, NE]), ALU.mult))
                step(dve.tensor_reduce(best[:, :], hot[:, :, :], AX.X, ALU.max))
                step(dve.tensor_tensor(hot[:, :, :], hot[:, :, :], over_e(best[:, :]), ALU.is_equal))
                if k == 0:
                    dve.tensor_copy(chosen[:, :, :], hot[:, :, :])
                else:
                    dve.tensor_tensor(chosen[:, :, :], chosen[:, :, :], hot[:, :, :], ALU.add)
                step(dve.scalar_tensor_tensor(rest[:, :, :], hot[:, :, :], -2.0, rest[:, :, :], ALU.mult, ALU.add))
            step(dve.tensor_tensor(G[:, :, :], G[:, :, :], chosen[:, :, :], ALU.mult))
            step(dve.tensor_reduce(gs[:, :], G[:, :, :], AX.X, ALU.add))
            step(dve.tensor_scalar(gs[:, :], gs[:, :], 1e-12, None, ALU.max))
            step(dve.reciprocal(gs[:, :], gs[:, :]))
            step(dve.tensor_tensor(G[:, :, :], G[:, :, :], over_e(gs[:, :]), ALU.mult))
            step(dve.tensor_copy(GE[:, :, :], G[:, :, :].rearrange("p n e -> p e n")))
            dve.sem_inc(g_ready, 1)
            dve.wait_ge(acc_ready, NG)
            dve.sem_inc(added, NG)
            GEf = GE[:, :, :].rearrange("p e n -> p (e n)")
            with dve.Fori(0, NE // 2) as i:
                t, e0 = dve.snap(i * EG), dve.snap(i * (2 * NBLK))
                for k in range(EG):
                    a, g = k // NG, k % NG
                    dve.wait_ge(added, t + k + 1)
                    dve.wait_ge(down_mm, t + k + NG + 2)
                    for u in range(4):
                        n = 4 * g + u
                        ins = dve.scalar_tensor_tensor(acc[:, n, :], PY[k % 2][:, u * P:(u + 1) * P],
                                                       GEf[:, bass.ds(e0 + a * NBLK + n, 1)], acc[:, n, :], ALU.mult, ALU.add)
                    ins.then_inc(added, 1)
            dve.wait_ge(added, NG + NE * NG)
            norm_stats(dve, step, nb, accs, range(NBLK))
            norm_apply(dve, step, nb, accs, ys)
            step(dve.tensor_tensor(X3[:, :, :], X3[:, :, :], Y[:, :, :], ALU.add))
            dve.sem_inc(y_ready, 1)


def sandwich(nc, x, Wv, Wo, Wg, Wb, Wqkv, q_scale, k_scale, Wo2, ln_g, ln_b, W1, b1, W2, b2,
             w_q, w_k, w_v, gate, EW1, Eb1, EW2, Eb2, ident, rot, mask, quad, tri, order, out):
    B, T, D = x.shape
    NBLK = B * T // P
    H = Wg.shape[0]
    NC = P // B
    x1_dram = nc.dram_tensor("x1", [B, T, D], F32, kind="Internal").ap()
    z_dram = nc.dram_tensor("chunk_maps", [B, NC, H, 2 * (D // H) ** 2], F32, kind="Internal").ap()
    s_dram = nc.dram_tensor("chunk_states", [B, NC, H, (D // H) ** 2], F32, kind="Internal").ap()
    with ExitStack() as ctx:
        sem = lambda n: ctx.enter_context(nc.semaphore(n))
        XA = ctx.enter_context(nc.sbuf_tensor("XA", [P, B, T + 1], F32))
        identf = ctx.enter_context(nc.sbuf_tensor("identf", [P, P], F32))
        ident_in = sem("ident_in")
        with nc.Block() as block:
            @block.sync
            def _(sp):
                sp.dma_start(identf[:, :], ident).then_inc(ident_in, 16)
                sp.wait_ge(ident_in, 16)
        stage_a(nc, sem, XA, identf, x, Wv, Wg, Wb, Wo, x1_dram, z_dram, s_dram)
        stage_b(nc, sem, XA, identf, Wqkv, q_scale, k_scale, Wo2, ln_g, ln_b, W1, b1, W2, b2, rot, mask, quad)
        X2 = ctx.enter_context(nc.sbuf_tensor("X2", [P, NBLK, D], F32))
        Y = ctx.enter_context(nc.sbuf_tensor("Y", [P, NBLK, D], F32))
        stage_c(nc, sem, XA, X2, Y, identf, x1_dram, w_q, w_k, w_v, tri)
        stage_d(nc, sem, X2, Y, identf, gate, EW1, Eb1, EW2, Eb2, order, out)


def constants(T, dh, window, experts):
    import numpy as np
    f = np.float32
    half = np.arange(0, dh, 2, dtype=f)
    inv_freq = (1.0 / 10000.0 ** (half / dh)).astype(f)
    t = np.arange(T, dtype=f)
    freqs = t[:, None] * inv_freq[None]
    freqs = np.concatenate([freqs, freqs], -1).astype(f)
    base = ((half + 0.4 * dh) / (1.4 * dh)).astype(f)
    power = ((t - T // 2) / (window // 2)).astype(f)
    scale = base[None] ** power[:, None]
    scale = np.concatenate([scale, scale], -1).astype(f)
    sign = np.where(np.arange(dh) < dh // 2, -1, 1).astype(f)
    cos, sin = np.cos(freqs), np.sin(freqs) * sign
    qk_scale = 8.0
    tab = np.stack([qk_scale * cos * scale, qk_scale * sin * scale, cos / scale, sin / scale], 1).astype(f)
    rot = np.ascontiguousarray(tab.reshape(T // P, P, 4, dh).transpose(1, 0, 2, 3))
    q, k = np.arange(P)[:, None], np.arange(P + window)[None] - window
    w0 = (q // window) * window
    ok = (k >= w0 - window) & (k < w0 + window) & (k <= q) & (k >= q - window)
    hidden = -1e25
    mask = np.stack([np.where(ok, 0, hidden), np.where(ok & (k >= 0), 0, hidden)], 1).astype(f)
    return {
        "ident": np.eye(P, dtype=f),
        "rot": rot,
        "mask": np.ascontiguousarray(mask),
        "quad": np.kron(np.eye(4), np.ones((window, 1))).astype(f),
        "tri": np.where(np.arange(P)[:, None] >= np.arange(P)[None], 0, -1e38).astype(f),
        "order": (experts - np.arange(experts)).astype(f),
    }


_INS = ["L0_attn_x", "L0_attn_Wv", "L0_attn_Wo", "L0_attn_Wg", "L0_attn_Wb", "L0_ffn_Wqkv", "L0_ffn_q_scale",
        "L0_ffn_k_scale", "L0_ffn_Wo", "L0_ffn_ln_g", "L0_ffn_ln_b", "L0_ffn_W1", "L0_ffn_b1", "L0_ffn_W2", "L0_ffn_b2",
        "L1_attn_w_q", "L1_attn_w_k", "L1_attn_w_v", "L1_ffn_gate", "L1_ffn_W1", "L1_ffn_b1", "L1_ffn_W2", "L1_ffn_b2"]


def kernel(**inputs):
    import numpy as _np
    import concourse.bacc as _bacc
    from concourse.bass_utils import run_bass_kernel_spmd as _run

    nc = _bacc.Bacc("TRN2", target_bir_lowering=False, num_devices=1)
    arrays, args = {}, []
    data = [(name, _np.ascontiguousarray(inputs[name])) for name in _INS]
    shape = inputs["L0_attn_x"].shape
    data += constants(shape[1], inputs["L0_ffn_q_scale"].shape[1], 32, inputs["L1_ffn_gate"].shape[1]).items()
    for name, a in data:
        arrays[f"in_{name}_dram"] = a
        args.append(nc.dram_tensor(f"in_{name}_dram", a.shape, F32, kind="ExternalInput").ap())
    args.append(nc.dram_tensor("out_0_dram", shape, F32, kind="ExternalOutput").ap())
    sandwich(nc, *args)
    r = _run(nc, [arrays], core_ids=[0])
    return r.results[0]["out_0_dram"]
```
